# Optimizing a Trainium2 kernel written in Bass

```python
import numpy as np
import jax
import jax.numpy as jnp

def _softmax(x, axis=-1):
    return jax.nn.softmax(x, axis=axis)

def _gelu(x):
    return jax.nn.gelu(x, approximate=True)

def _silu(x):
    return jax.nn.silu(x)

def _sigmoid(x):
    return jax.nn.sigmoid(x)

def _layernorm(x, axis=-1, eps=1e-05):
    m = jnp.mean(x, axis=axis, keepdims=True)
    v = jnp.var(x, axis=axis, keepdims=True)
    return (x - m) / jnp.sqrt(v + eps)

def _scatter_add(tgt, idx, src, axis=0):
    return tgt.at[idx].add(src)

def _segment_sum(src, seg, n):
    return jax.ops.segment_sum(src, seg, n)
kernel_name = 'mk_flamingo_gated_d2_seqx_r8_8a3694'

def setup_inputs(seed: int=0):
    np.random.seed(seed)
    _w = jnp.asarray

    def _rec_inputs():
        import jax
        import jax.numpy as jnp
        _rk = jax.random.key(seed)
        x = 0.0003765 + 1 * jax.random.normal(jax.random.fold_in(_rk, 1), (8, 128, 256), jnp.float32)
        _lenS = 128 - jax.random.randint(jax.random.fold_in(_rk, 7), (8,), 0, max(1, 128 // 4) + 1, jnp.int32)
        _lenS2 = 128 - jax.random.randint(jax.random.fold_in(_rk, 8), (8,), 0, max(1, 128 // 4) + 1, jnp.int32)
        _ctx_2048P = jax.random.normal(jax.random.fold_in(_rk, 11), (8, 16, 256), jnp.float32)
        _ctx_2048c = jax.random.dirichlet(jax.random.fold_in(_rk, 511), 0.3 * jnp.ones((16,), jnp.float32), (8, 128))
        _ctx_2048t = jnp.einsum('bsk,bkd->bsd', _ctx_2048c, _ctx_2048P)
        _ctx_2048t = _ctx_2048t * jax.lax.rsqrt(jnp.mean(jnp.square(_ctx_2048t)) + 1e-12) * 0.953939
        ctx_2048 = -0.000292821 + 1.00034 * (_ctx_2048t + 0.3 * jax.random.normal(jax.random.fold_in(_rk, 611), (8, 128, 256), jnp.float32))
        _validS = jnp.arange(128)[None, :] < _lenS[:, None]
        _validS2 = jnp.arange(128)[None, :] < _lenS2[:, None]
        _causal = jnp.tril(jnp.ones((128, 128), dtype=bool))
        mask_BxS2_bk0 = jnp.logical_not(jnp.broadcast_to(_validS2[:, :], (8, 128)))
        _g = jax.random.normal(jax.random.fold_in(_rk, 9001), (2, 2), jnp.float32)
        _g = jnp.sign(_g) * jnp.maximum(jnp.abs(_g), 1.0) + (_g == 0) * 1.0
        g_xattn = _g[0]
        g_ffn = _g[1]
        return (x, ctx_2048, mask_BxS2_bk0, g_xattn, g_ffn)
    x, ctx_2048, mask_BxS2_bk0, g_xattn, g_ffn = _rec_inputs()

    def _L0_xattn_setup():
        import jax, jax.numpy as jnp
        import numpy as np
        key = jax.random.key(seed)
        k1, k2, k3, k4, k5 = jax.random.split(key, 5)
        B, D_MODEL, L = (2, 128, 256)
        HEAD_DIM = 8
        H = D_MODEL // HEAD_DIM
        return {'k': jax.random.normal(k1, (B, D_MODEL, L), dtype=jnp.float32), 'v': jax.random.normal(k2, (B, D_MODEL, L), dtype=jnp.float32), 'q': jax.random.normal(k3, (B, D_MODEL, L), dtype=jnp.float32), 'ssm_kernel': jax.random.normal(k4, (H, L), dtype=jnp.float32), 'D': jax.random.normal(k5, (H,), dtype=jnp.float32), 'head_dim': HEAD_DIM}
    _L0_xattn_all = _L0_xattn_setup()
    _L0_xattn_in = {k: v for k, v in _L0_xattn_all.items() if k in ('ssm_kernel', 'D')}
    del _L0_xattn_all

    def _L0_ffn_setup():
        import jax, jax.numpy as jnp
        import numpy as np
        TOP_K = 8
        NEG_INF = -1000000000.0
        key = jax.random.key(seed)
        ks = jax.random.split(key, 6)
        B, S, H, I, E, G, GS = (1, 256, 256, 176, 64, 8, 8)
        sc = 0.02
        return {'hidden_states': jax.random.normal(ks[0], (B, S, H), jnp.float32), 'gate_w': jax.random.normal(ks[1], (E, H), jnp.float32) * sc, 'mask_up_w': jax.random.normal(ks[2], (G, H, GS), jnp.float32) * sc, 'gate_proj_w': jax.random.normal(ks[3], (G, I, H), jnp.float32) * sc, 'up_proj_w': jax.random.normal(ks[4], (G, I, H), jnp.float32) * sc, 'down_proj_w': jax.random.normal(ks[5], (G, H, I), jnp.float32) * sc, 'inv_map': jnp.arange(G * GS, dtype=jnp.int64).reshape(G, GS)}
    _L0_ffn_all = _L0_ffn_setup()
    _L0_ffn_in = {k: v for k, v in _L0_ffn_all.items() if k in ('gate_w', 'mask_up_w', 'gate_proj_w', 'up_proj_w', 'down_proj_w', 'inv_map')}
    del _L0_ffn_all

    def _L1_xattn_setup():
        import jax, jax.numpy as jnp
        import numpy as np
        key = jax.random.key(seed)
        k1, k2, k3 = jax.random.split(key, 3)
        B, S, D, M = (8, 256, 256, 128)
        hidden_states = jax.random.normal(k1, (B, S, D), dtype=jnp.float32)
        memory_tokens = jax.random.normal(k2, (B, M, D), dtype=jnp.float32)
        memory_mask = jax.random.randint(k3, (B, M), 0, 2).astype(jnp.bool_)
        return {'hidden_states': hidden_states, 'memory_tokens': memory_tokens, 'memory_mask': memory_mask}
    _L1_xattn_all = _L1_xattn_setup()
    _L1_xattn_in = {k: v for k, v in _L1_xattn_all.items() if k in ()}
    del _L1_xattn_all

    def _L1_ffn_setup():
        import jax, jax.numpy as jnp
        import numpy as np
        B, S, D, H = (8, 512, 256, 640)

        def ternarize_weight(w):
            abs_mean = jnp.maximum(jnp.mean(jnp.abs(w)), 1e-05)
            thr = 0.7 * abs_mean
            one = jnp.ones((), dtype=w.dtype)
            q = jnp.where(w > thr, one, jnp.where(w < -thr, -one, jnp.zeros((), dtype=w.dtype)))
            return w + jax.lax.stop_gradient(q * abs_mean - w)
        key = jax.random.key(seed)
        k1, k2, k3 = jax.random.split(key, 3)
        x = jax.random.normal(k1, (B, S, D), dtype=jnp.float32)
        w_fc = jax.random.normal(k2, (H, D), dtype=jnp.float32) / np.sqrt(D).astype(np.float32)
        w_proj = jax.random.normal(k3, (D, H), dtype=jnp.float32) / np.sqrt(H).astype(np.float32)
        return {'x': x, 'w_fc': w_fc, 'w_proj': w_proj}
    _L1_ffn_all = _L1_ffn_setup()
    _L1_ffn_in = {k: v for k, v in _L1_ffn_all.items() if k in ('w_fc', 'w_proj')}
    del _L1_ffn_all
    return {'x': x, 'ctx_2048': ctx_2048, 'mask_BxS2_bk0': mask_BxS2_bk0, 'g_xattn': g_xattn, 'g_ffn': g_ffn, 'L0_xattn_ssm_kernel': _L0_xattn_in['ssm_kernel'], 'L0_xattn_D': _L0_xattn_in['D'], 'L0_ffn_gate_w': _L0_ffn_in['gate_w'], 'L0_ffn_mask_up_w': _L0_ffn_in['mask_up_w'], 'L0_ffn_gate_proj_w': _L0_ffn_in['gate_proj_w'], 'L0_ffn_up_proj_w': _L0_ffn_in['up_proj_w'], 'L0_ffn_down_proj_w': _L0_ffn_in['down_proj_w'], 'L0_ffn_inv_map': _L0_ffn_in['inv_map'], 'L1_ffn_w_fc': _L1_ffn_in['w_fc'], 'L1_ffn_w_proj': _L1_ffn_in['w_proj']}

def reference(x, ctx_2048, mask_BxS2_bk0, g_xattn, g_ffn, L0_xattn_ssm_kernel, L0_xattn_D, L0_ffn_gate_w, L0_ffn_mask_up_w, L0_ffn_gate_proj_w, L0_ffn_up_proj_w, L0_ffn_down_proj_w, L0_ffn_inv_map, L1_ffn_w_fc, L1_ffn_w_proj):
    import jax
    import jax.numpy as jnp

    def _L0_xattn_ref(k, v, q, ssm_kernel, D, head_dim):
        import jax, jax.numpy as jnp
        import numpy as np
        B, HD, L = k.shape
        H = HD // head_dim
        fft_size = 2 * L
        k_ = k.reshape(B, H, head_dim, L)
        v_ = v.reshape(B, H, head_dim, L)
        q_ = q.reshape(B, H, head_dim, L)
        kv = jnp.einsum('bhil,bhjl->bijhl', k_, v_)
        kv_f = jnp.fft.rfft(kv, n=fft_size)
        kernel_f = jnp.fft.rfft(ssm_kernel, n=fft_size)
        y = jnp.fft.irfft(kv_f * kernel_f, n=fft_size)[..., :L]
        out = y + kv * D[None, None, None, :, None]
        out = jnp.einsum('bijhl,bhil->bjhl', out, q_)
        out = jnp.transpose(out, (0, 2, 1, 3)).reshape(B, H * head_dim, L)
        return out.astype(k.dtype)

    def _L0_ffn_ref(hidden_states, gate_w, mask_up_w, gate_proj_w, up_proj_w, down_proj_w, inv_map):
        import jax, jax.numpy as jnp
        import numpy as np
        TOP_K = 8
        NEG_INF = -1000000000.0
        B, S, H = hidden_states.shape
        x = hidden_states.reshape(-1, H)
        N = x.shape[0]
        E = gate_w.shape[0]
        scores = jax.nn.softmax(x @ gate_w.T, axis=-1)
        topk_w, topk_idx = jax.lax.top_k(scores, TOP_K)
        w_e = jnp.zeros((N, E), x.dtype).at[jnp.arange(N)[:, None], topk_idx].add(topk_w)
        flat = w_e[:, inv_map]
        scalar = flat.sum(-1)
        soft = jax.nn.softmax(jnp.where(flat == 0, NEG_INF, flat), axis=-1)
        xg = x[:, None, :] + jnp.einsum('ngi,ghi->ngh', soft, mask_up_w)
        g = jnp.einsum('ngh,gih->ngi', xg, gate_proj_w)
        u = jnp.einsum('ngh,gih->ngi', xg, up_proj_w)
        a = jax.nn.silu(g) * u
        d = jnp.einsum('ngi,ghi->ngh', a, down_proj_w)
        y = jnp.einsum('ng,ngh->nh', scalar, d)
        return y.reshape(B, S, H)

    def _L1_xattn_ref(hidden_states, memory_tokens, memory_mask):
        import jax, jax.numpy as jnp
        import numpy as np
        B, S, D = hidden_states.shape
        scale = 1.0 / jnp.sqrt(jnp.asarray(D, hidden_states.dtype))
        scores = jnp.einsum('bsd,bmd->bsm', hidden_states, memory_tokens) * scale
        neg_inf = jnp.asarray(-1e+30, scores.dtype)
        scores = jnp.where(memory_mask[:, None, :], scores, neg_inf)
        attn = jax.nn.softmax(scores, axis=-1)
        readout = jnp.einsum('bsm,bmd->bsd', attn, memory_tokens)
        valid_b = jnp.any(memory_mask, axis=-1)
        out = jnp.where(valid_b[:, None, None], readout, jnp.zeros_like(readout))
        return out

    def _L1_ffn_ref(x, w_fc, w_proj):
        import jax, jax.numpy as jnp
        import numpy as np
        B, S, D, H = (8, 512, 256, 640)

        def ternarize_weight(w):
            abs_mean = jnp.maximum(jnp.mean(jnp.abs(w)), 1e-05)
            thr = 0.7 * abs_mean
            one = jnp.ones((), dtype=w.dtype)
            q = jnp.where(w > thr, one, jnp.where(w < -thr, -one, jnp.zeros((), dtype=w.dtype)))
            return w + jax.lax.stop_gradient(q * abs_mean - w)
        h = jnp.einsum('bsd,hd->bsh', x, ternarize_weight(w_fc))
        h = jnp.square(jax.nn.relu(h))
        return jnp.einsum('bsh,dh->bsd', h, ternarize_weight(w_proj))
    x = x + jnp.tanh(g_xattn[0]) * _L0_xattn_ref(ctx_2048, ctx_2048, _layernorm(x, axis=-1), L0_xattn_ssm_kernel, L0_xattn_D, 8)
    x = x + jnp.tanh(g_ffn[0]) * _L0_ffn_ref(_layernorm(x, axis=-1), L0_ffn_gate_w, L0_ffn_mask_up_w, L0_ffn_gate_proj_w, L0_ffn_up_proj_w, L0_ffn_down_proj_w, L0_ffn_inv_map)
    x = x + jnp.tanh(g_xattn[1]) * _L1_xattn_ref(_layernorm(x, axis=-1), ctx_2048, mask_BxS2_bk0)
    x = x + jnp.tanh(g_ffn[1]) * _L1_ffn_ref(_layernorm(x, axis=-1), L1_ffn_w_fc, L1_ffn_w_proj)
    return x

_drawn_inputs = setup_inputs


def setup_inputs(seed=0):
    import zlib

    import numpy as np

    out = dict(_drawn_inputs(seed))
    spreads = {'g_ffn': (-1.0, 0.6)}
    factors = {'L0_ffn_gate_w': 8.0,
     'L0_ffn_mask_up_w': 8.0,
     'L0_ffn_gate_proj_w': 8.0,
     'L0_ffn_up_proj_w': 8.0,
     'L0_ffn_down_proj_w': 8.0,
     'L1_ffn_w_fc': 7.661,
     'L1_ffn_w_proj': 6.833}
    for name, (base, spread) in spreads.items():
        noise = np.random.default_rng([zlib.crc32(name.encode()), seed]).standard_normal(out[name].shape)
        drawn = base * np.exp(spread * noise) if base else spread * noise
        out[name] = jnp.asarray(drawn.astype(out[name].dtype))
    for name, factor in factors.items():
        out[name] = (out[name] * factor).astype(out[name].dtype)
    return out
```

```python
import numpy as np
import concourse.bass as bass
from concourse import mybir

F32, F32R, I32, U8 = mybir.dt.float32, mybir.dt.float32r, mybir.dt.int32, mybir.dt.uint8
ALU, ACT, AXX = mybir.AluOpType, mybir.ActivationFunctionType, mybir.AxisListType.X

P = 128
B, L = 8, 256
HEADS, HD = 16, 8
Q = 4
NE, NG, GS = 64, 8, 8
NI = 176
GI = NG * NI
TILES = GI // P
CW = 2 * NI
NCH = GI // CW
NJ = 640
JT = NJ // P
TAPS = 5
SPAN = 11
YW = TAPS * SPAN - 3
EXT = 15
KPAD = 384
EPS = 1e-5
DONE_TILES = [range(0, 2), range(2, 5), range(5, 8), range(8, 11)]
WORDS = {"gate": 0, "up": 1}

RING_LOADS = ["gate0", "gate1", "gate2", "up0", "up1", "up2", "down0", "down1", "fc", "proj"]
RING_LAST = {"gate0": ("turn_w", "gate", 1), "gate1": ("turn_w", "gate", 3), "gate2": ("turn_w", "gate", 5),
             "up0": ("turn_w", "up", 1), "up1": ("turn_w", "up", 3), "up2": ("turn_w", "up", 5),
             "down0": ("turn_down", 5), "down1": ("turn_down", 5), "fc": ("turn_fc", 2), "proj": ("turn_proj", 2)}


def make_schedule():
    weights = [("turn_router",)]
    weights += [("turn_w", "gate", p) for p in range(6)] + [("turn_w", "up", p) for p in range(6)]
    weights += [("mask_up", w, c) for w in ("gate", "up") for c in range(NCH)]
    weights += [("turn_down", p) for p in range(6)]
    weights += [("tern_sum", "fc")] + [("turn_fc", p) for p in range(3)]
    weights += [("tern_sum", "proj")] + [("turn_proj", p) for p in range(3)]

    s = [("turn_ctx", 0, 0), ("turn_ctx", 0, 1), ("kv", 0, 0), ("norm", "mix", 0), ("turn_q", 0, 0), ("turn_q", 0, 1),
         ("kv", 0, 1)]

    def conv_head(half, h):
        out = [("conv", half, h)]
        g = h // 2
        if h % 2:
            if g + 2 < HEADS // 2:
                out.append(("kv", half, g + 2))
            out.append(("fold", half, g))
            if g >= 1:
                out.append(("gather", half, g - 1))
        return out

    w = list(weights)
    for h in range(HEADS):
        s += conv_head(0, h)
        if h == 7:
            s += [("turn_ctx", 1, 0), ("turn_ctx", 1, 1)]
        take = -(-len(w) // (HEADS - h))
        s += w[:take]
        w = w[take:]
    s += [("gather", 0, HEADS // 2 - 1), ("turn_att", 0, 0), ("turn_att", 0, 1)]
    s += [("norm", "mix", 1), ("turn_q", 1, 0), ("turn_q", 1, 1), ("kv", 1, 0), ("kv", 1, 1)]

    def router(half):
        return [("norm", "moe", half), ("turn_x", "moe", half, 0), ("turn_x", "moe", half, 1), ("logits", half),
                ("top", half), ("turn_top", half), ("flat", half), ("soft", half),
                ("turn_soft", half, 0), ("turn_soft", half, 1)]

    r = router(0)
    s += r[:4] + conv_head(1, 0) + r[4:5] + conv_head(1, 1) + r[5:8] + conv_head(1, 2) + conv_head(1, 3) + r[8:]

    def experts(half, between):
        out, late = [], []
        n = Q * NCH
        for k in range(n):
            b, c = half * Q + k // NCH, k % NCH
            out.append(("chunk", b, c))
            take = -(-len(between) // (n - k))
            out += sum(between[:take], [])
            between = between[take:]
            out += late
            late = [("turn_a", b, c)] + ([("down", b)] if c == NCH - 1 else [])
        return out + late

    s += experts(0, [conv_head(1, h) for h in range(4, HEADS)])
    s += [("gather", 1, HEADS // 2 - 1), ("turn_att", 1, 0), ("turn_att", 1, 1)]

    def cross(half):
        return [[("norm", "cross", half), ("turn_x", "cross", half, 0), ("turn_x", "cross", half, 1)],
                [("scores", half)], [("turn_p", half)], [("read", half, 0), ("read", half, 1)]]

    def mlp(half):
        return [[("norm", "mlp", half), ("turn_x", "mlp", half, 0), ("turn_x", "mlp", half, 1)]] + \
            [[("hidden", half, j)] for j in range(JT)] + [[("out", half, 0)], [("out", half, 1)]]

    r = router(1)
    x = cross(0)
    s += r[:4] + x[0] + r[4:5] + x[1] + r[5:7] + r[7:8] + x[2] + r[8:] + x[3]
    s += experts(1, mlp(0))
    s += sum(cross(1) + mlp(1), [])
    return s


SCHEDULE = make_schedule()
G0, U0, G1, U1, Y0, Y1, TR, DN = range(8)


def plan_psum():
    early = [G0, U0, G1, U1, TR, DN]
    late = [TR, DN]
    mixed = [Y0, Y1]
    n_early = n_late = n_mixed = 0
    uses, n_use, n_read = {}, [0] * 8, [0] * 8
    first_chunk = SCHEDULE.index(("chunk", 0, 0))
    conv_end = SCHEDULE.index(("gather", 1, HEADS // 2 - 1))
    tail = SCHEDULE.index(("down", B - 1))
    conv = 0

    def use(key, bank, reads):
        uses[key] = (bank, n_use[bank], n_read[bank], reads)
        n_use[bank] += 1
        n_read[bank] += reads

    reads = {"turn_ctx": 3, "turn_q": 3, "turn_router": 2, "turn_w": 2, "mask_up": 4, "turn_down": 2, "tern_sum": 1,
             "turn_fc": 1, "turn_proj": 1, "turn_att": 1, "turn_x": 2, "logits": 2, "turn_top": 1, "flat": 3,
             "turn_soft": 1, "scores": 1, "turn_p": 1, "read": 2, "hidden": 1, "out": 1}
    for i, step in enumerate(SCHEDULE):
        kind = step[0]
        if kind == "conv":
            use(step, [Y0, Y1][conv % 2], 2)
            conv += 1
        elif kind == "chunk":
            k = (step[1] * NCH + step[2]) % 2
            use(("gate",) + step[1:], [G0, G1][k], 1)
            use(("up",) + step[1:], [U0, U1][k], 2)
        elif kind == "turn_a":
            use(step, TR, 2)
        elif kind == "down":
            use(step, DN, 1)
        elif kind in reads:
            n = reads[kind]
            if kind == "turn_x" and step[1] == "cross":
                n = 1
            if i < first_chunk or i > tail:
                use(step, early[n_early % 6], n)
                n_early += 1
            elif i < conv_end:
                use(step, late[n_late % 2], n)
                n_late += 1
            else:
                use(step, mixed[n_mixed % 2], n)
                n_mixed += 1
    return uses


USES = plan_psum()
NORMS = [s for s in SCHEDULE if s[0] == "norm"]


def build(nc, x, ctx_rows, mask, g_xattn, g_ffn, kernel_rev, skip, gate_w, mask_up_w, gate_p, up_p, down_p, inv_map,
          w_fc, w_proj, out):
    at = [((nc.sbuf_base + 31) // 32) * 32]

    def region(size):
        start = at[0]
        at[0] += -(-size // 32) * 32
        assert at[0] <= nc.sbuf_usable_end, at[0] - nc.sbuf_usable_end
        return start

    def sb(name, shape, dt=F32, offset=None):
        size = int(np.prod(shape[1:])) * (1 if dt == U8 else 4)
        return nc.alloc_sbuf_tensor_at(name, shape, dt, offset=region(size) if offset is None else offset)

    x_res = sb("x_res", [P, B, L])
    ctx = sb("ctx", [P, B, L])
    ctx_ext = sb("ctx_ext", [P, 2, HEADS, 2, Q, EXT])
    w_split = sb("w_split", [P, 2, 2, 2, GI], F32R)
    toe_raw = nc.alloc_sbuf_tensor_at("toe_raw", [P, HEADS, 256], F32, offset=at[0] - 4 * 8 * GI)
    d_split = sb("d_split", [P, TILES, 2, L], F32R)
    m_stack = sb("m_stack", [P, 2, GI], F32R)
    fc_t = sb("fc_t", [P, 2, NJ], F32R)
    proj_t = sb("proj_t", [P, JT, L], F32R)
    xt_at = region(4 * 2 * 2 * 512)
    xt = sb("xt", [P, 2, 2, 512], F32R, xt_at)
    half_m = sb("half_m", [P, 2, CW], F32R, xt_at)
    tern_tmp = sb("tern_tmp", [P, 2 * NJ], F32, xt_at + 4 * 2 * CW)
    soft_at = region(4 * 2 * 512)
    soft_t = sb("soft_t", [P, 2, 512], F32R, soft_at)
    mu4 = sb("mu4", [P, 2, 4, 4 * 32], F32R, soft_at)
    ring_at = region(4 * TILES * 2 * P)
    a_t = sb("a_t", [P, TILES, 2, P], F32R, ring_at)
    a_at = region(4 * GI)
    act = sb("act", [P, GI], F32, a_at)
    silu_at = region(4 * 2 * CW)
    silu = sb("silu", [P, 2, CW], F32, silu_at)
    ring = [sb(f"ring{k}", [P, GI], F32, ring_at + 4 * GI * k) for k in range(3)]
    assert ring_at + 12 * GI <= silu_at + 4 * 2 * CW
    rt = [sb(f"rt{k}", [P, Q * NE], F32, a_at + 4 * Q * NE * k) for k in range(5)]
    top_t = sb("top_t", [NE, 512], F32, silu_at)
    xn_at = region(4 * Q * L)
    xn = sb("xn", [P, Q, L], F32, xn_at)
    soft_parts = sb("soft_parts", [P, Q * 2, 4, 32], F32, xn_at)
    conv_at = at[0]
    toe = sb("toe", [P, HEADS, 256])
    q_ext = sb("q_ext", [P, HEADS, 2 * Q, EXT])
    kv = sb("kv", [P, 2, 4 * Q, TAPS, SPAN])
    prod = sb("prod", [P, 2, 2, 2 * Q, HD, HD])
    fold = sb("fold", [P, 2, 4 * Q, 4, HD])
    att = sb("att", [P, 2 * Q, HEADS, HD])
    conv_end = at[0]
    at[0] = conv_at
    hid_t = sb("hid_t", [P, JT, 2, 512], F32R)
    xt1 = sb("xt1", [P, 2, 2, 512], F32R)
    qt1 = sb("qt1", [P, 2, 512])
    neg = sb("neg", [P, B * P])
    assert at[0] <= conv_end
    late_at = at[0]
    at[0] = conv_end
    late = [late_at]

    def after_conv(name, shape):
        t = nc.alloc_sbuf_tensor_at(name, shape, F32, offset=late[0])
        late[0] += 4 * int(np.prod(shape[1:]))
        assert late[0] <= conv_end, (name, late[0] - conv_end)
        return t

    relu = after_conv("relu", [P, 512])
    hsq = after_conv("hsq", [P, 512])
    s_att = after_conv("s_att", [P, Q, P])
    pt = after_conv("pt", [P, 512])
    mask_words = sb("mask_words", [P, B * P // 4], I32)
    mask_sb = mask_words[:, :].bitcast(U8)
    ident = sb("ident", [P, P])
    ones = sb("ones", [P, P])
    router_w = sb("router_w", [NE, L])
    router_t = sb("router_t", [P, 2, 2, NE], F32R)
    mu = sb("mu", [P, 2, NE])
    onehot = sb("onehot", [NE, NE])
    inv_i = sb("inv_i", [NE, NE], I32)
    inv_f = sb("inv_f", [NE, 2, NE])
    skip_sb = sb("skip_sb", [P, HEADS])
    gates = sb("gates", [P, 4])
    tg = sb("tg", [P, 4])
    pidx = sb("pidx", [P, 3], I32)
    pidx_f = sb("pidx_f", [P, 3])
    ind = sb("ind", [P, 2, 4])
    stats = sb("stats", [P, Q, 6])
    mv = sb("mv", [P, Q, 2])
    ve = sb("ve", [P, Q])
    rstd = sb("rstd", [P, Q])
    mhalf = sb("mhalf", [P, Q])
    nmax = sb("nmax", [P, Q])
    rsum = sb("rsum", [P, 2, Q])
    top8 = sb("top8", [P, Q, 8])
    scal = sb("scal", [P, B, NG])
    gmax = sb("gmax", [P, 3, Q * NG])
    tern = sb("tern", [P, 2, 6])
    out_scale = sb("out_scale", [P, 3])
    valid = sb("valid", [P, 2, B])
    esum = sb("esum", [P, Q])
    rv = sb("rv", [P, 2, Q])

    banks = [nc.alloc_psum_tensor(f"bank{k}", [P, 512], F32) for k in range(8)]
    filled = [nc.alloc_semaphore(f"filled{k}") for k in range(8)]
    drained = [nc.alloc_semaphore(f"drained{k}") for k in range(8)]
    sem = nc.alloc_semaphore
    x_loaded = [sem("x_loaded0"), sem("x_loaded1")]
    ctx_loaded = [sem("ctx_loaded0"), sem("ctx_loaded1")]
    toe_loaded = [sem("toe_loaded0"), sem("toe_loaded1")]
    small_loaded, mask_loaded = sem("small_loaded"), sem("mask_loaded")
    ring_loaded = [sem(f"ring_loaded{k}") for k in range(3)]
    consts_made = sem("consts_made")
    toe_diag, toe_off = sem("toe_diag"), sem("toe_off")
    tanh_done = sem("tanh_done")
    mu4_made, onehot_made, ind_made = sem("mu4_made"), sem("onehot_made"), sem("ind_made")
    kv_made = sem("kv_made")
    folded, gathered = sem("folded"), sem("gathered")
    stats_done, rstd_done, normed = sem("stats_done"), sem("rstd_done"), sem("normed")
    shifted, router_exp, chosen = sem("shifted"), sem("router_exp"), sem("chosen")
    soft_shifted, soft_exp, soft_made = sem("soft_shifted"), sem("soft_exp"), sem("soft_made")
    tern_abs, tern_made = sem("tern_abs"), sem("tern_made")
    s_shifted, s_exp = sem("s_shifted"), sem("s_exp")
    relu_done, sq_done, hid_hi, hid_lo = sem("relu_done"), sem("sq_done"), sem("hid_hi"), sem("hid_lo")
    dve_own, act_own = sem("dve_own"), sem("act_own")
    stored = sem("stored")

    def psum(key):
        return banks[USES[key][0]]

    def claim(eng, key):
        bank, _, before, _ = USES[key]
        if before:
            eng.wait_ge(drained[bank], before)

    def fill(ins, key):
        ins.then_inc(filled[USES[key][0]], 1)

    def wait_filled(eng, key):
        bank, n, _, _ = USES[key]
        eng.wait_ge(filled[bank], n + 1)

    def wait_drained(eng, key, reads=None):
        bank, _, before, n = USES[key]
        eng.wait_ge(drained[bank], before + (n if reads is None else reads))

    def drain(ins, key):
        ins.then_inc(drained[USES[key][0]], 1)

    def group_no(half, g):
        return half * (HEADS // 2) + g

    def view(t, offset, dims):
        whole = t[:]
        return bass.AP(whole.tensor, whole.offset + offset, [list(whole.ap[0])] + [list(d) for d in dims])

    def updates_of_x(eng, kind, half):
        if kind == "mix":
            eng.wait_ge(x_loaded[half], 16)
        elif kind == "moe":
            for p in range(2):
                wait_drained(eng, ("turn_att", half, p))
        elif kind == "cross":
            wait_drained(eng, ("down", half * Q + Q - 1))
        else:
            for p in range(2):
                wait_drained(eng, ("read", half, p))

    TURNS_OF = {"mix": lambda hf: [("turn_q", hf, t) for t in range(2)],
                "moe": lambda hf: [("turn_x", "moe", hf, t) for t in range(2)],
                "cross": lambda hf: [("turn_x", "cross", hf, t) for t in range(2)],
                "mlp": lambda hf: [("turn_x", "mlp", hf, t) for t in range(2)]}

    block = nc.Block()
    with block:
        @block.sync
        def _(sp):
            def rows_of(src, half):
                return src[half * Q:(half + 1) * Q].rearrange("b p l -> p b l")

            def ring_load(n):
                name = RING_LOADS[n]
                if n >= 3:
                    wait_filled(sp, RING_LAST[RING_LOADS[n - 3]])
                slot = ring[n % 3]
                if name[:-1] in ("gate", "up"):
                    src = (gate_p if name[0] == "g" else up_p).rearrange("g i h -> (g i) h")
                    r0 = 4 * int(name[-1])
                    n_t = min(4, TILES - r0)
                    src = src[r0 * P:(r0 + n_t) * P, :].rearrange("(r p) h -> p r h", p=P)
                    dst = slot[:, 0:n_t * L].rearrange("p (r h) -> p r h", h=L)
                elif name[:-1] == "down":
                    kt = int(name[-1])
                    src = down_p[:, kt * P:(kt + 1) * P, :].rearrange("g h i -> h g i")
                    dst = slot[:, :].rearrange("p (g i) -> p g i", i=NI)
                elif name == "fc":
                    src = w_fc.rearrange("(r p) h -> p r h", p=P)
                    dst = slot[:, 0:JT * L].rearrange("p (r h) -> p r h", h=L)
                else:
                    src = w_proj.rearrange("(r p) j -> p r j", p=P)
                    dst = slot[:, 0:2 * NJ].rearrange("p (r j) -> p r j", j=NJ)
                sp.dma_start(dst, src).then_inc(ring_loaded[n % 3], 16)

            sp.dma_start(x_res[:, 0:Q, :], rows_of(x, 0)).then_inc(x_loaded[0], 16)
            sp.dma_start(ctx[:, 0:Q, :], rows_of(ctx_rows, 0)).then_inc(ctx_loaded[0], 16)
            sp.dma_start(skip_sb[:, :], skip.partition_broadcast(P)).then_inc(small_loaded, 16)
            for k in range(2):
                src = bass.AP(kernel_rev.tensor, k * 8 * KPAD, [[1, P], [KPAD, 8], [1, 256]])
                sp.dma_start(toe_raw[:, 8 * k:8 * k + 8, :], src).then_inc(toe_loaded[k], 16)
            sp.dma_start(router_w[:, :], gate_w).then_inc(small_loaded, 16)
            sp.dma_start(gates[:, 0:2], g_xattn.partition_broadcast(P)).then_inc(small_loaded, 16)
            sp.dma_start(gates[:, 2:4], g_ffn.partition_broadcast(P)).then_inc(small_loaded, 16)
            sp.dma_start(inv_i[:, :], inv_map.rearrange("a b -> (a b)").partition_broadcast(NE)).then_inc(small_loaded, 16)
            for kt in range(2):
                sp.dma_start(mu[:, kt, :].rearrange("p (g s) -> p g s", g=NG),
                             mask_up_w[:, kt * P:(kt + 1) * P, :].rearrange("g h s -> h g s")).then_inc(small_loaded, 16)
            for n in range(3):
                ring_load(n)
            sp.dma_start(ctx[:, Q:B, :], rows_of(ctx_rows, 1)).then_inc(ctx_loaded[1], 16)
            sp.dma_start(x_res[:, Q:B, :], rows_of(x, 1)).then_inc(x_loaded[1], 16)
            sp.dma_start(mask_words[:, :], mask.rearrange("b m -> (b m)").partition_broadcast(P)).then_inc(mask_loaded, 16)
            for n in range(3, len(RING_LOADS)):
                ring_load(n)
            for half in range(2):
                for p in range(2):
                    b0 = half * Q + 2 * p
                    wait_drained(sp, ("out", half, p))
                    sp.dma_start(out[b0:b0 + 2].rearrange("b p l -> p b l"), x_res[:, b0:b0 + 2, :]).then_inc(stored, 16)
            sp.wait_ge(stored, 64)

        SMALL = 16 * 7

        @block.tensor
        def _(pe):
            def split_product(dst, lhs, rhs, start, stop):
                for i, (a, b) in enumerate(((0, 0), (1, 0), (0, 1))):
                    last = pe.matmul(dst, lhs(a), rhs(b), start=start and i == 0, stop=stop and i == 2)
                return last

            def turn(key, pieces, waits=()):
                claim(pe, key)
                for k, (piece, rows, cols) in enumerate(pieces):
                    last = pe.transpose(psum(key)[0:cols, k * rows:(k + 1) * rows], piece, ident[0:rows, 0:rows])
                fill(last, key)

            pe.wait_ge(consts_made, 2)
            for step in SCHEDULE:
                kind = step[0]
                if kind == "turn_ctx":
                    _, half, t = step
                    pe.wait_ge(ctx_loaded[half], 16)
                    turn(step, [(ctx[:, half * Q + q, t * P:(t + 1) * P], P, P) for q in range(Q)])
                elif kind in ("turn_q", "turn_x"):
                    t, half = step[-1], step[-2]
                    which = "mix" if kind == "turn_q" else step[1]
                    pe.wait_ge(normed, Q * (NORMS.index(("norm", which, half)) + 1))
                    turn(step, [(xn[:, q, t * P:(t + 1) * P], P, P) for q in range(Q)])
                elif kind == "conv":
                    _, half, h = step
                    g = group_no(half, h // 2)
                    if half == 0:
                        pe.wait_ge(toe_diag, h + 1)
                        pe.wait_ge(toe_off, h // 8 + 1)
                    pe.wait_ge(kv_made, g + 1)
                    claim(pe, step)

                    def pairs(t):
                        return kv[:, g % 2, (2 * (h % 2) + t) * Q:(2 * (h % 2) + t + 1) * Q].rearrange(
                            "p q d j -> p q (d j)")[:, :, 3:TAPS * SPAN]
                    y = psum(step)[:, 0:2 * Q * YW].rearrange("p (t q c) -> p t q c", t=2, q=Q)
                    pe.matmul(y[:, 0], toe[:, h, 0:P], pairs(0), start=True, stop=True)
                    pe.matmul(y[:, 1], toe[:, h, P:2 * P], pairs(0), start=True, stop=False)
                    fill(pe.matmul(y[:, 1], toe[:, h, 0:P], pairs(1), start=False, stop=True), step)
                elif kind == "turn_router":
                    pe.wait_ge(small_loaded, SMALL)
                    turn(step, [(router_w[:, t * P:(t + 1) * P], NE, P) for t in range(2)])
                elif kind == "turn_w":
                    _, which, p = step
                    n = RING_LOADS.index(f"{which}{p // 2}")
                    pe.wait_ge(ring_loaded[n % 3], 16 * (n // 3 + 1))
                    tiles = range(2 * p, min(2 * p + 2, TILES))
                    turn(step, [(ring[n % 3][:, (r % 4) * L + kt * P:(r % 4) * L + (kt + 1) * P], P, P)
                                for kt in range(2) for r in tiles])
                elif kind == "turn_down":
                    p = step[1]
                    for kt in range(2):
                        n = RING_LOADS.index(f"down{kt}")
                        pe.wait_ge(ring_loaded[n % 3], 16 * (n // 3 + 1))
                    n = RING_LOADS.index("down0")
                    turn(step, [(ring[(n + kt) % 3][:, r * P:(r + 1) * P], P, P)
                                for r in range(2 * p, min(2 * p + 2, TILES)) for kt in range(2)])
                elif kind == "mask_up":
                    _, which, c = step
                    pe.wait_ge(mu4_made, 2)
                    for p in range(6):
                        wait_drained(pe, ("turn_w", which, p))
                    claim(pe, step)
                    for kt in range(2):
                        last = split_product(psum(step)[:, 0:CW], lambda part: mu4[:, part, 2 * kt + c // 2, :],
                                             lambda part: w_split[:, WORDS[which], kt, part, c * CW:(c + 1) * CW],
                                             kt == 0, kt == 1)
                    fill(last, step)
                elif kind == "tern_sum":
                    k = 0 if step[1] == "fc" else 1
                    pe.wait_ge(tern_abs, k + 1)
                    claim(pe, step)
                    fill(pe.matmul(psum(step)[:, 0:1], ones[:, :], tern[:, k, 0:1], start=True, stop=True), step)
                elif kind == "turn_fc":
                    p = step[1]
                    pe.wait_ge(tern_made, 1)
                    slot = ring[RING_LOADS.index("fc") % 3]
                    turn(step, [(slot[:, r * L + kt * P:r * L + (kt + 1) * P], P, P)
                                for kt in range(2) for r in range(2 * p, min(2 * p + 2, JT))])
                elif kind == "turn_proj":
                    p = step[1]
                    pe.wait_ge(tern_made, 2)
                    slot = ring[RING_LOADS.index("proj") % 3]
                    turn(step, [(slot[:, kt * NJ + r * P:kt * NJ + (r + 1) * P], P, P)
                                for r in range(2 * p, min(2 * p + 2, JT)) for kt in range(2)])
                elif kind == "turn_att":
                    _, half, p = step
                    pe.wait_ge(gathered, group_no(half, HEADS // 2 - 1) + 1)
                    turn(step, [(att[:, t * Q + q].rearrange("p h j -> p (h j)"), P, P) for q in (2 * p, 2 * p + 1) for t in range(2)])
                elif kind == "logits":
                    half = step[1]
                    wait_drained(pe, ("turn_router",))
                    for t in range(2):
                        wait_drained(pe, ("turn_x", "moe", half, t))
                    claim(pe, step)
                    for q in range(Q):
                        for kt in range(2):
                            last = split_product(psum(step)[:, q * NE:(q + 1) * NE],
                                                 lambda part: xt[:, kt, part, q * P:(q + 1) * P],
                                                 lambda part: router_t[:, kt, part, :], kt == 0, kt == 1)
                    fill(last, step)
                elif kind == "turn_top":
                    half = step[1]
                    pe.wait_ge(chosen, half + 1)
                    turn(step, [(rt[3][:, q * NE:(q + 1) * NE], P, NE) for q in range(Q)])
                elif kind == "flat":
                    half = step[1]
                    pe.wait_ge(onehot_made, 1)
                    wait_drained(pe, ("turn_top", half))
                    claim(pe, step)
                    for q in range(Q):
                        last = pe.matmul(psum(step)[:, q * NE:(q + 1) * NE], top_t[:, q * P:(q + 1) * P], onehot[:, :],
                                         start=True, stop=True)
                    fill(last, step)
                elif kind == "turn_soft":
                    _, half, gh = step
                    pe.wait_ge(soft_made, half + 1)
                    turn(step, [(soft_parts[:, 2 * q + gh].rearrange("p a c -> p (a c)"), P, P) for q in range(Q)])
                elif kind == "chunk":
                    _, b, c = step
                    half, q = b // Q, b % Q
                    if b == 0 and c == 0:
                        for which in WORDS:
                            for k in range(NCH):
                                wait_drained(pe, ("mask_up", which, k))
                    for gh in range(2):
                        wait_drained(pe, ("turn_soft", half, gh))
                    claim(pe, ("gate", b, c))
                    claim(pe, ("up", b, c))
                    rows = slice(q * P, (q + 1) * P)
                    cols = slice(c * CW, (c + 1) * CW)
                    ops = [(xt[:, kt, pa, rows], kt, pb) for kt in range(2) for pa, pb in ((0, 0), (0, 1), (1, 0))]
                    for i, (lhs, kt, part) in enumerate(ops):
                        for w, name in enumerate(("gate", "up")):
                            pe.matmul(psum((name, b, c))[:, 0:CW], lhs, w_split[:, w, kt, part, cols],
                                      start=i == 0, stop=False)
                    for w, name in enumerate(("gate", "up")):
                        fill(pe.matmul(psum((name, b, c))[:, 0:CW], soft_t[:, c // 2, rows], m_stack[:, w, cols],
                                       start=False, stop=True), (name, b, c))
                elif kind == "turn_a":
                    _, b, c = step
                    wait_drained(pe, ("up", b, c))
                    turn(step, [(act[:, r * P:(r + 1) * P], P, P) for r in DONE_TILES[c]])
                elif kind == "down":
                    b = step[1]
                    if b == 0:
                        for p in range(6):
                            wait_drained(pe, ("turn_down", p))
                    wait_drained(pe, ("turn_a", b, NCH - 1))
                    claim(pe, step)
                    for r in range(TILES):
                        last = split_product(psum(step)[:, 0:L], lambda part: a_t[:, r, part, :],
                                             lambda part: d_split[:, r, part, :], r == 0, r == TILES - 1)
                    fill(last, step)
                elif kind == "scores":
                    half = step[1]
                    for t in range(2):
                        wait_drained(pe, ("turn_x", "cross", half, t))
                    claim(pe, step)
                    for q in range(Q):
                        for t in range(2):
                            last = pe.matmul(psum(step)[:, q * P:(q + 1) * P], qt1[:, t, q * P:(q + 1) * P],
                                             ctx_ext[:, half, :, t, q, 3:3 + HD], start=t == 0, stop=t == 1)
                    fill(last, step)
                elif kind == "turn_p":
                    half = step[1]
                    pe.wait_ge(s_exp, Q * (half + 1))
                    turn(step, [(s_att[:, q, :], P, P) for q in range(Q)])
                elif kind == "read":
                    _, half, p = step
                    wait_drained(pe, ("turn_p", half))
                    claim(pe, step)
                    for k in range(2):
                        q = 2 * p + k
                        last = pe.matmul(psum(step)[:, k * L:(k + 1) * L], pt[:, q * P:(q + 1) * P],
                                         ctx[:, half * Q + q, :], start=True, stop=True)
                    fill(last, step)
                elif kind == "hidden":
                    _, half, j = step
                    for t in range(2):
                        wait_drained(pe, ("turn_x", "mlp", half, t))
                    if half == 0 and j == 0:
                        for p in range(3):
                            wait_drained(pe, ("turn_fc", p))
                    claim(pe, step)
                    for kt in range(2):
                        for part in range(2):
                            last = pe.matmul(psum(step)[:, :], fc_t[:, kt, j * P:(j + 1) * P], xt1[:, kt, part, :],
                                             start=kt + part == 0, stop=kt + part == 2)
                    fill(last, step)
                elif kind == "out":
                    _, half, p = step
                    if half == 0 and p == 0:
                        for k in range(3):
                            wait_drained(pe, ("turn_proj", k))
                    pe.wait_ge(hid_lo, JT * (half + 1))
                    claim(pe, step)
                    for k in range(2):
                        rows = slice((2 * p + k) * P, (2 * p + k + 1) * P)
                        for j in range(JT):
                            for part in range(2):
                                last = pe.matmul(psum(step)[:, k * L:(k + 1) * L], hid_t[:, j, part, rows],
                                                 proj_t[:, j, :], start=j + part == 0, stop=j + part == JT)
                    fill(last, step)

        @block.scalar
        def _(act_e):
            def copy(dst, src):
                return act_e.activation(dst, src, ACT.Copy)

            for k in range(2):
                act_e.wait_ge(toe_loaded[k], 16)
                src = toe_raw[:, 8 * k:8 * k + 8, 0:P]
                copy(toe[:, 8 * k:8 * k + 8, P:2 * P], src[:, :, ::-1]).then_inc(toe_off, 1)
            act_e.wait_ge(small_loaded, SMALL)
            act_e.activation(tg[:, :], gates[:, :], ACT.Tanh).then_inc(tanh_done, 1)
            for step in SCHEDULE:
                kind = step[0]
                if kind == "turn_ctx":
                    _, half, t = step
                    wait_filled(act_e, step)
                    src = psum(step)[:, :].rearrange("p (q h i) -> p q h i", q=Q, h=HEADS)
                    dst = ctx_ext[:, half, :, t, :, :].rearrange("p h q e -> p q h e")
                    for d0, s0, n in ((3, 0, 8), (0, 5, 3), (11, 0, 4)):
                        drain(copy(dst[:, :, :, d0:d0 + n], src[:, :, :, s0:s0 + n]), step)
                elif kind == "turn_router":
                    wait_filled(act_e, step)
                    drain(copy(router_t[:, :, 0, :], psum(step)[:, 0:2 * NE].rearrange("p (t e) -> p t e", t=2)), step)
                elif kind == "turn_w":
                    _, which, p = step
                    if which == "gate" and p == 0:
                        act_e.wait_ge(toe_diag, HEADS)
                        act_e.wait_ge(toe_off, 2)
                    wait_filled(act_e, step)
                    n = P * len(range(2 * p, min(2 * p + 2, TILES)))
                    drain(copy(w_split[:, WORDS[which], :, 0, 2 * p * P:2 * p * P + n],
                               psum(step)[:, 0:2 * n].rearrange("p (t c) -> p t c", t=2)), step)
                elif kind == "turn_down":
                    p = step[1]
                    wait_filled(act_e, step)
                    n = len(range(2 * p, min(2 * p + 2, TILES)))
                    drain(copy(d_split[:, 2 * p:2 * p + n, 0, :],
                               psum(step)[:, 0:n * L].rearrange("p (r c) -> p r c", c=L)), step)
                elif kind == "mask_up":
                    _, which, c = step
                    act_e.wait_ge(ind_made, 2)
                    k = WORDS[which] * NCH + c
                    if k >= 2:
                        prev = [("mask_up", w, cc) for w in WORDS for cc in range(NCH)][k - 2]
                        wait_drained(act_e, prev)
                    wait_filled(act_e, step)
                    for i in range(2):
                        cols = slice(i * NI, (i + 1) * NI)
                        g = 2 * (c % 2) + i
                        drain(act_e.activation(half_m[:, k % 2, cols], psum(step)[:, cols], ACT.Copy,
                                               scale=ind[:, 1, g:g + 1]), step)
                elif kind == "turn_fc":
                    p = step[1]
                    wait_filled(act_e, step)
                    n = P * len(range(2 * p, min(2 * p + 2, JT)))
                    drain(copy(fc_t[:, :, 2 * p * P:2 * p * P + n],
                               psum(step)[:, 0:2 * n].rearrange("p (t c) -> p t c", t=2)), step)
                elif kind == "turn_proj":
                    p = step[1]
                    wait_filled(act_e, step)
                    n = len(range(2 * p, min(2 * p + 2, JT)))
                    drain(copy(proj_t[:, 2 * p:2 * p + n, :],
                               psum(step)[:, 0:n * L].rearrange("p (r c) -> p r c", c=L)), step)
                elif kind == "turn_x":
                    _, which, half, t = step
                    if which == "moe" and half == 0:
                        if t == 0:
                            for w in WORDS:
                                wait_drained(act_e, ("mask_up", w, NCH - 1))
                            act_e.wait_ge(tern_made, 2)
                    elif which == "moe":
                        wait_filled(act_e, ("up", Q - 1, NCH - 1))
                    elif which == "cross" and half == 0:
                        act_e.wait_ge(gathered, HEADS)
                        for h in (HEADS - 2, HEADS - 1):
                            wait_filled(act_e, ("conv", 1, h))
                        for p in range(2):
                            wait_filled(act_e, ("turn_att", 1, p))
                    elif which == "cross":
                        wait_filled(act_e, ("scores", 0))
                    elif half == 1:
                        wait_filled(act_e, ("hidden", 0, JT - 1))
                    wait_filled(act_e, step)
                    if which == "cross":
                        drain(copy(qt1[:, t, :], psum(step)[:, :]), step)
                    else:
                        drain(copy((xt if which == "moe" else xt1)[:, t, 0, :], psum(step)[:, :]), step)
                elif kind == "top":
                    half = step[1]
                    act_e.wait_ge(shifted, half + 1)
                    act_e.activation(rt[0][:, :], rt[0][:, :], ACT.Exp).then_inc(router_exp, 1)
                elif kind == "turn_top":
                    half = step[1]
                    if half == 0:
                        wait_filled(act_e, ("turn_proj", 2))
                    else:
                        wait_drained(act_e, ("up", Q - 1, NCH - 2))
                        wait_drained(act_e, ("up", Q - 1, NCH - 1))
                    wait_filled(act_e, step)
                    drain(copy(top_t[:, :], psum(step)[0:NE, :]), step)
                elif kind == "soft":
                    half = step[1]
                    act_e.wait_ge(soft_shifted, half + 1)
                    act_e.activation(rt[1][:, :], rt[1][:, :], ACT.Exp).then_inc(soft_exp, 1)
                elif kind == "turn_soft":
                    _, half, gh = step
                    if half == 1:
                        wait_filled(act_e, ("up", Q - 1, NCH - 1))
                    wait_filled(act_e, step)
                    drain(copy(soft_t[:, gh, :], psum(step)[:, :]), step)
                elif kind == "chunk":
                    _, b, c = step
                    n = b * NCH + c
                    if n in (0, Q * NCH):
                        wait_filled(act_e, ("flat", b // Q))
                    if n >= 2:
                        wait_drained(act_e, ("up", (n - 2) // NCH, (n - 2) % NCH))
                    wait_filled(act_e, ("gate", b, c))
                    drain(act_e.activation(silu[:, n % 2, :], psum(("gate", b, c))[:, 0:CW], ACT.Silu), ("gate", b, c))
                elif kind == "turn_a":
                    _, b, c = step
                    if b >= 1:
                        wait_filled(act_e, ("down", b - 1))
                    wait_filled(act_e, step)
                    r = DONE_TILES[c]
                    drain(copy(a_t[:, r.start:r.stop, 0, :],
                               psum(step)[:, 0:len(r) * P].rearrange("p (r n) -> p r n", n=P)), step)
                elif kind == "scores":
                    half = step[1]
                    act_e.wait_ge(s_shifted, half + 1)
                    for q in range(Q):
                        act_e.activation(s_att[:, q, :], s_att[:, q, :], ACT.Exp, bias=nmax[:, q:q + 1],
                                         accum_out=esum[:, q:q + 1]).then_inc(s_exp, 1)
                elif kind == "turn_p":
                    half = step[1]
                    if half == 1:
                        for p in range(2):
                            wait_filled(act_e, ("read", 0, p))
                    wait_filled(act_e, step)
                    drain(copy(pt[:, :], psum(step)[:, :]), step)
                elif kind == "hidden":
                    _, half, j = step
                    n = half * JT + j
                    if n:
                        act_e.wait_ge(sq_done, n)
                    wait_filled(act_e, step)
                    drain(act_e.activation(relu[:, :], psum(step)[:, :], ACT.Relu), step)
                    if half == 1 and j == 0:
                        for p in range(2):
                            wait_filled(act_e, ("out", 0, p))
                    act_e.wait_ge(sq_done, n + 1)
                    copy(hid_t[:, j, 0, :], hsq[:, :]).then_inc(hid_hi, 1)

        @block.vector
        def _(dve):
            own = [0]

            def mine(ins):
                own[0] += 1
                ins.then_inc(dve_own, 1)
                dve.wait_ge(dve_own, own[0])

            def residue(dst, key, src, hi, reads=1):
                wait_drained(dve, key, reads)
                drain(dve.tensor_tensor(dst, src, hi.bitcast(F32), ALU.subtract), key)

            dve.wait_ge(consts_made, 4)
            for k in range(2):
                dve.wait_ge(toe_loaded[k], 16)
                if k == 0:
                    dve.wait_ge(small_loaded, SMALL)
                for h in range(8 * k, 8 * k + 8):
                    src = toe_raw[:, h, P:2 * P]
                    dve.scalar_tensor_tensor(out=toe[:, h, 0:P], in0=ident[:, :], scalar=skip_sb[:, h:h + 1],
                                             in1=src[:, ::-1], op0=ALU.mult, op1=ALU.add).then_inc(toe_diag, 1)
            dve.tensor_scalar(pidx[:, 1:2], pidx[:, 0:1], 3, 3, ALU.logical_shift_right, ALU.bitwise_and)
            mine(dve.tensor_scalar(pidx[:, 2:3], pidx[:, 0:1], 5, 1, ALU.logical_shift_right, ALU.bitwise_and))
            mine(dve.tensor_copy(pidx_f[:, :], pidx[:, :]))
            for g in range(4):
                last = dve.tensor_scalar(ind[:, 0, g:g + 1], pidx_f[:, 1:2], float(g), None, ALU.is_equal)
            last.then_inc(ind_made, 1)
            dve.wait_ge(ind_made, 1)
            dve.tensor_scalar(ind[:, 1, :], ind[:, 0, :], pidx_f[:, 2:3], None, ALU.mult).then_inc(ind_made, 1)
            mine(dve.tensor_copy(inv_f[:, 0, :], inv_i[:, :]))
            mine(dve.tensor_scalar(inv_f[:, 1, :], inv_f[:, 0, :], 0.0, float(NE), ALU.is_lt, ALU.mult))
            mine(dve.tensor_tensor(inv_f[:, 0, :], inv_f[:, 0, :], inv_f[:, 1, :], ALU.add))
            dve.tensor_scalar(onehot[:, :], inv_f[:, 0, :], pidx_f[0:NE, 0:1], None, ALU.is_equal).then_inc(onehot_made, 1)
            mu_in = mu[:, :, :].rearrange("p t (a c) -> p (t a) c", c=32).unsqueeze(2).broadcast_to([P, 4, 4, 32])
            hi = mu4[:, 0, :, :].rearrange("p b (k c) -> p b k c", c=32)
            lo = mu4[:, 1, :, :].rearrange("p b (k c) -> p b k c", c=32)
            dve.tensor_copy(hi, mu_in).then_inc(mu4_made, 1)
            dve.wait_ge(mu4_made, 1)
            dve.tensor_tensor(lo, mu_in, hi.bitcast(F32), ALU.subtract).then_inc(mu4_made, 1)

            for step in SCHEDULE:
                kind = step[0]
                if kind == "norm":
                    _, which, half = step
                    n = NORMS.index(step)
                    updates_of_x(dve, which, half)
                    for q in range(Q):
                        last = dve.bn_stats(stats[:, q, :], x_res[:, half * Q + q, :])
                    mine(last)
                    for q in range(Q):
                        last = dve.bn_aggr(mv[:, q, :], stats[:, q, :])
                    last.then_inc(stats_done, 1)
                    dve.wait_ge(rstd_done, n + 1)
                    if n:
                        _, prev, ph = NORMS[n - 1]
                        for key in TURNS_OF[prev](ph):
                            wait_filled(dve, key)
                        for hf in range(half if which == "moe" else 0, 2):
                            if SCHEDULE.index(("turn_soft", hf, 1)) < SCHEDULE.index(step):
                                wait_filled(dve, ("turn_soft", hf, 1))
                    for q in range(Q):
                        dve.tensor_scalar(xn[:, q, :], x_res[:, half * Q + q, :], mv[:, q, 0:1], rstd[:, q:q + 1],
                                          ALU.subtract, ALU.mult).then_inc(normed, 1)
                elif kind == "turn_q":
                    _, half, t = step
                    if half == 1 and t == 0:
                        for h in (HEADS - 2, HEADS - 1):
                            wait_drained(dve, ("conv", 0, h))
                    wait_filled(dve, step)
                    src = psum(step)[:, :].rearrange("p (q h i) -> p q h i", q=Q, h=HEADS)
                    dst = q_ext[:, :, t * Q:(t + 1) * Q, :].rearrange("p h q e -> p q h e")
                    for d0, s0, n in ((3, 0, 8), (0, 5, 3), (11, 0, 4)):
                        drain(dve.tensor_copy(dst[:, :, :, d0:d0 + n], src[:, :, :, s0:s0 + n]), step)
                elif kind == "kv":
                    _, half, g = step
                    n = group_no(half, g)
                    if g == 0:
                        for t in range(2):
                            wait_drained(dve, ("turn_ctx", half, t))
                    if n >= 2:
                        hf, gg = divmod(n - 2, HEADS // 2)
                        for h in (2 * gg, 2 * gg + 1):
                            wait_filled(dve, ("conv", hf, h))
                    base = (half * HEADS + 2 * g) * 2 * Q * EXT
                    dve.tensor_tensor(kv[:, n % 2], view(ctx_ext, base, [[EXT, 4 * Q], [0, TAPS], [1, SPAN]]),
                                      view(ctx_ext, base, [[EXT, 4 * Q], [1, TAPS], [1, SPAN]]),
                                      ALU.mult).then_inc(kv_made, 1)
                elif kind == "conv":
                    _, half, h = step
                    n = group_no(half, h // 2)
                    if h == 0:
                        for t in range(2):
                            wait_drained(dve, ("turn_q", half, t))
                    if h % 2 == 0 and n >= 2:
                        dve.wait_ge(folded, n - 1)
                    wait_filled(dve, step)
                    y = psum(step)
                    qb = h * 2 * Q * EXT
                    o = prod[:, n % 2, h % 2]
                    drain(dve.tensor_tensor(o[:, :, 0:TAPS, :], view(y, 0, [[YW, 2 * Q], [SPAN, TAPS], [1, HD]]),
                                            view(q_ext, qb + 3, [[EXT, 2 * Q], [1, TAPS], [1, HD]]), ALU.mult), step)
                    drain(dve.tensor_tensor(o[:, :, TAPS:HD, :], view(y, SPAN - 1, [[YW, 2 * Q], [SPAN - 1, 3], [1, HD]]),
                                            view(q_ext, qb + 2, [[EXT, 2 * Q], [-1, 3], [1, HD]]), ALU.mult), step)
                elif kind == "gather":
                    _, half, g = step
                    n = group_no(half, g)
                    dve.wait_ge(folded, n + 1)
                    if half == 1 and g == 0:
                        for p in range(2):
                            wait_filled(dve, ("turn_att", 0, p))
                    dve.tensor_reduce(att[:, :, 2 * g:2 * g + 2].rearrange("p n h j -> p h n j"),
                                      fold[:, n % 2].rearrange("p (h n) s j -> p h n j s", h=2), AXX,
                                      ALU.add).then_inc(gathered, 1)
                elif kind == "turn_att":
                    _, half, p = step
                    b0 = half * Q + 2 * p
                    if half == 0 and p == 0:
                        dve.wait_ge(tanh_done, 1)
                    dve.wait_ge(x_loaded[half], 16)
                    wait_filled(dve, step)
                    rows = x_res[:, b0:b0 + 2, :].rearrange("p b l -> p (b l)")
                    drain(dve.scalar_tensor_tensor(out=rows, in0=psum(step)[:, :], scalar=tg[:, 0:1], in1=rows,
                                                   op0=ALU.mult, op1=ALU.add), step)
                elif kind == "turn_router":
                    residue(router_t[:, :, 1, :], step, psum(step)[:, 0:2 * NE].rearrange("p (t e) -> p t e", t=2),
                            router_t[:, :, 0, :])
                elif kind == "turn_w":
                    _, which, p = step
                    n = P * len(range(2 * p, min(2 * p + 2, TILES)))
                    cols = slice(2 * p * P, 2 * p * P + n)
                    w = WORDS[which]
                    residue(w_split[:, w, :, 1, cols], step, psum(step)[:, 0:2 * n].rearrange("p (t c) -> p t c", t=2),
                            w_split[:, w, :, 0, cols])
                elif kind == "turn_down":
                    p = step[1]
                    n = len(range(2 * p, min(2 * p + 2, TILES)))
                    residue(d_split[:, 2 * p:2 * p + n, 1, :], step,
                            psum(step)[:, 0:n * L].rearrange("p (r c) -> p r c", c=L), d_split[:, 2 * p:2 * p + n, 0, :])
                elif kind == "mask_up":
                    _, which, c = step
                    k = WORDS[which] * NCH + c
                    wait_drained(dve, step, 2)
                    for i in range(2):
                        cols = slice(i * NI, (i + 1) * NI)
                        g = 2 * (c % 2) + i
                        drain(dve.scalar_tensor_tensor(
                            out=m_stack[:, WORDS[which], c * CW + i * NI:c * CW + (i + 1) * NI], in0=psum(step)[:, cols],
                            scalar=ind[:, 0, g:g + 1], in1=half_m[:, k % 2, cols].bitcast(F32), op0=ALU.mult,
                            op1=ALU.subtract), step)
                elif kind == "tern_sum":
                    name = step[1]
                    k = 0 if name == "fc" else 1
                    n = RING_LOADS.index(name)
                    w = ring[n % 3][:, 0:2 * NJ]
                    dve.wait_ge(ring_loaded[n % 3], 16 * (n // 3 + 1))
                    dve.tensor_reduce(tern[:, k, 0:1], w, AXX, ALU.add, apply_absolute_value=True).then_inc(tern_abs, 1)
                    wait_filled(dve, step)
                    drain(dve.tensor_scalar(tern[:, k, 1:2], psum(step)[:, 0:1], 1.0 / (NJ * L), 1e-5, ALU.mult, ALU.max),
                          step)
                    wait_drained(dve, step)
                    dve.tensor_scalar(tern[:, k, 2:3], tern[:, k, 1:2], 0.7, None, ALU.mult)
                    mine(dve.tensor_scalar(tern[:, k, 3:4], tern[:, k, 1:2], -0.7, None, ALU.mult))
                    mine(dve.tensor_scalar(tern_tmp[:, :], w, tern[:, k, 3:4], None, ALU.is_lt))
                    dve.scalar_tensor_tensor(out=w, in0=w, scalar=tern[:, k, 2:3], in1=tern_tmp[:, :], op0=ALU.is_gt,
                                             op1=ALU.subtract).then_inc(tern_made, 1)
                    if k == 1:
                        dve.wait_ge(tanh_done, 1)
                        mine(dve.tensor_tensor(out_scale[:, 0:1], tern[:, 0, 1:2], tern[:, 0, 1:2], ALU.mult))
                        mine(dve.tensor_tensor(out_scale[:, 1:2], out_scale[:, 0:1], tern[:, 1, 1:2], ALU.mult))
                        mine(dve.tensor_tensor(out_scale[:, 2:3], out_scale[:, 1:2], tg[:, 3:4], ALU.mult))
                elif kind == "turn_x" and step[1] != "cross":
                    _, which, half, t = step
                    dst = xt if which == "moe" else xt1
                    residue(dst[:, t, 1, :], step, psum(step)[:, :], dst[:, t, 0, :])
                elif kind == "logits":
                    half = step[1]
                    if half == 0:
                        wait_filled(dve, ("turn_proj", 2))
                    else:
                        wait_filled(dve, ("turn_a", Q - 1, NCH - 1))
                    wait_filled(dve, step)
                    z = psum(step)[:, 0:Q * NE].rearrange("p (q e) -> p q e", q=Q)
                    drain(dve.tensor_reduce(nmax[:, :], z, AXX, ALU.max, negate=True), step)
                    wait_drained(dve, step, 1)
                    r0 = rt[0][:, :].rearrange("p (q e) -> p q e", q=Q)
                    drain(dve.tensor_tensor(r0, z, nmax[:, :].unsqueeze(2).broadcast_to([P, Q, NE]), ALU.add), step)
                    wait_drained(dve, step)
                    dve.nop().then_inc(shifted, 1)
                elif kind == "top":
                    half = step[1]
                    v = [r[:, :].rearrange("p (q e) -> p q e", q=Q) for r in rt]
                    dve.wait_ge(router_exp, half + 1)
                    mine(dve.tensor_reduce(rsum[:, 0, :], v[0], AXX, ALU.add))
                    mine(dve.reciprocal(rsum[:, 1, :], rsum[:, 0, :]))
                    mine(dve.tensor_tensor(v[1], v[0], rsum[:, 1, :].unsqueeze(2).broadcast_to([P, Q, NE]), ALU.mult))
                    for q in range(Q):
                        last = dve.max(top8[:, q, :], v[1][:, q, :])
                    mine(last)
                    for q in range(Q):
                        last = dve.match_replace(v[2][:, q, :], top8[:, q, :], v[1][:, q, :], 0.0)
                    mine(last)
                    dve.tensor_tensor(rt[3][:, :], rt[1][:, :], rt[2][:, :], ALU.subtract).then_inc(chosen, 1)
                elif kind == "flat":
                    half = step[1]
                    wait_filled(dve, step)
                    f = psum(step)[:, 0:Q * NE]
                    f3 = f.rearrange("p (n s) -> p n s", s=GS)
                    dst = scal[:, half * Q:(half + 1) * Q, :].rearrange("p q g -> p (q g)")
                    drain(dve.tensor_reduce(dst, f3, AXX, ALU.add), step)
                    drain(dve.tensor_scalar(rt[0][:, :], f, 0.0, -1e9, ALU.is_equal, ALU.mult), step)
                    wait_drained(dve, step, 2)
                    drain(dve.tensor_tensor(rt[2][:, :], f, rt[0][:, :], ALU.add), step)
                    wait_drained(dve, step)
                    v2 = rt[2][:, :].rearrange("p (n s) -> p n s", s=GS)
                    v1 = rt[1][:, :].rearrange("p (n s) -> p n s", s=GS)
                    mine(dve.tensor_reduce(gmax[:, 0, :], v2, AXX, ALU.max))
                    dve.tensor_tensor(v1, v2, gmax[:, 0, :].unsqueeze(2).broadcast_to([P, Q * NG, GS]),
                                      ALU.subtract).then_inc(soft_shifted, 1)
                elif kind == "soft":
                    half = step[1]
                    v1 = rt[1][:, :].rearrange("p (n s) -> p n s", s=GS)
                    v0 = rt[0][:, :].rearrange("p (n s) -> p n s", s=GS)
                    dve.wait_ge(soft_exp, half + 1)
                    mine(dve.tensor_reduce(gmax[:, 1, :], v1, AXX, ALU.add))
                    mine(dve.reciprocal(gmax[:, 2, :], gmax[:, 1, :]))
                    mine(dve.tensor_tensor(v0, v1, gmax[:, 2, :].unsqueeze(2).broadcast_to([P, Q * NG, GS]), ALU.mult))
                    src = rt[0][:, :].rearrange("p (n c) -> p n c", c=32).unsqueeze(2).broadcast_to([P, 2 * Q, 2, 32])
                    for t in range(2):
                        wait_filled(dve, ("turn_x", "moe", half, t))
                    mine(dve.tensor_copy(soft_parts[:, :, 0:2, :].bitcast(F32R), src))
                    dve.tensor_tensor(soft_parts[:, :, 2:4, :].bitcast(F32R), src, soft_parts[:, :, 0:2, :],
                                      ALU.subtract).then_inc(soft_made, 1)
                elif kind == "chunk":
                    _, b, c = step
                    n = b * NCH + c
                    if n in (0, Q * NCH):
                        wait_filled(dve, ("turn_top", b // Q))
                    if b % Q:
                        wait_filled(dve, ("turn_a", b - 1, min(c + 1, NCH - 1)))
                    wait_drained(dve, ("gate", b, c))
                    wait_filled(dve, ("up", b, c))
                    for i in range(2):
                        cols = slice(i * NI, (i + 1) * NI)
                        g = 2 * c + i
                        drain(dve.scalar_tensor_tensor(out=act[:, g * NI:(g + 1) * NI], in0=silu[:, n % 2, cols],
                                                       scalar=scal[:, b, g:g + 1], in1=psum(("up", b, c))[:, cols],
                                                       op0=ALU.mult, op1=ALU.mult), ("up", b, c))
                elif kind == "turn_a":
                    _, b, c = step
                    r = DONE_TILES[c]
                    residue(a_t[:, r.start:r.stop, 1, :], step,
                            psum(step)[:, 0:len(r) * P].rearrange("p (r n) -> p r n", n=P), a_t[:, r.start:r.stop, 0, :])
                elif kind == "down":
                    b = step[1]
                    wait_filled(dve, step)
                    drain(dve.scalar_tensor_tensor(out=x_res[:, b, :], in0=psum(step)[:, 0:L], scalar=tg[:, 2:3],
                                                   in1=x_res[:, b, :], op0=ALU.mult, op1=ALU.add), step)
                elif kind == "scores":
                    half = step[1]
                    if half == 0:
                        dve.wait_ge(mask_loaded, 16)
                        for p in range(2):
                            wait_filled(dve, ("turn_att", 1, p))
                        m8 = mask_sb.rearrange("p (b m) -> p b m", b=B)
                        mine(dve.tensor_reduce(valid[:, 0, :], m8, AXX, ALU.max))
                        dve.tensor_scalar(valid[:, 1, :], valid[:, 0, :], tg[:, 1:2], None, ALU.mult)
                        mine(dve.tensor_scalar(neg[:, :], mask_sb, -1.0, 1e30, ALU.add, ALU.mult))
                    else:
                        wait_filled(dve, ("turn_p", 0))
                    wait_filled(dve, step)
                    s2 = s_att[:, :, :].rearrange("p q m -> p (q m)")
                    drain(dve.scalar_tensor_tensor(out=s2, in0=psum(step)[:, :], scalar=1.0 / float(np.sqrt(L)),
                                                   in1=neg[:, half * Q * P:(half + 1) * Q * P], op0=ALU.mult, op1=ALU.add),
                          step)
                    wait_drained(dve, step)
                    dve.tensor_reduce(nmax[:, :], s_att[:, :, :], AXX, ALU.max, negate=True).then_inc(s_shifted, 1)
                elif kind == "read":
                    _, half, p = step
                    if p == 0:
                        dve.wait_ge(s_exp, Q * (half + 1))
                        mine(dve.reciprocal(rv[:, 0, :], esum[:, :]))
                        mine(dve.tensor_tensor(rv[:, 1, :], rv[:, 0, :], valid[:, 1, half * Q:(half + 1) * Q], ALU.mult))
                    wait_filled(dve, step)
                    for k in range(2):
                        q = 2 * p + k
                        b = half * Q + q
                        drain(dve.scalar_tensor_tensor(out=x_res[:, b, :], in0=psum(step)[:, k * L:(k + 1) * L],
                                                       scalar=rv[:, 1, q:q + 1], in1=x_res[:, b, :], op0=ALU.mult,
                                                       op1=ALU.add), step)
                elif kind == "hidden":
                    _, half, j = step
                    n = half * JT + j
                    wait_drained(dve, step)
                    if n:
                        dve.wait_ge(hid_lo, n)
                        dve.wait_ge(hid_hi, n)
                    dve.tensor_tensor(hsq[:, :], relu[:, :], relu[:, :], ALU.mult).then_inc(sq_done, 1)
                    dve.wait_ge(hid_hi, n + 1)
                    dve.tensor_tensor(hid_t[:, j, 1, :], hsq[:, :], hid_t[:, j, 0, :].bitcast(F32),
                                      ALU.subtract).then_inc(hid_lo, 1)
                elif kind == "out":
                    _, half, p = step
                    b0 = half * Q + 2 * p
                    rows = x_res[:, b0:b0 + 2, :].rearrange("p b l -> p (b l)")
                    wait_filled(dve, step)
                    drain(dve.scalar_tensor_tensor(out=rows, in0=psum(step)[:, :], scalar=out_scale[:, 2:3], in1=rows,
                                                   op0=ALU.mult, op1=ALU.add), step)

        @block.gpsimd
        def _(pool):
            pool.memset(ones[:, :], 1.0).then_inc(consts_made, 1)
            pool.iota(pidx[:, 0:1], pattern=[[0, 1]], base=0, channel_multiplier=1)
            pool.memset(mhalf[:, :], -0.5)
            pool.wait_ge(consts_made, 1)
            pool.affine_select(out=ident[:, :], in_=ones[:, :], compare_op=ALU.is_equal, fill=0.0, base=0,
                               pattern=[[1, P]], channel_multiplier=-1).then_inc(consts_made, 1)
            pool.wait_ge(consts_made, 2)
            pool.nop().then_inc(consts_made, 2)
            for step in SCHEDULE:
                kind = step[0]
                if kind == "norm":
                    n = NORMS.index(step)
                    pool.wait_ge(stats_done, n + 1)
                    pool.tensor_scalar(ve[:, :], mv[:, :, 1], EPS, None, ALU.add).then_inc(act_own, 1)
                    pool.wait_ge(act_own, n + 1)
                    pool.tensor_tensor(rstd[:, :], ve[:, :], mhalf[:, :], ALU.pow).then_inc(rstd_done, 1)
                elif kind == "fold":
                    _, half, g = step
                    n = group_no(half, g)
                    for h in (2 * g, 2 * g + 1):
                        wait_drained(pool, ("conv", half, h))
                    if n >= 2:
                        pool.wait_ge(gathered, n - 1)
                    p4 = prod[:, n % 2].rearrange("p h n s j -> p (h n) (s j)")
                    pool.tensor_tensor(fold[:, n % 2].rearrange("p n s j -> p n (s j)"), p4[:, :, 0:32], p4[:, :, 32:64],
                                       ALU.add).then_inc(folded, 1)


def kernel(**inputs):
    import concourse.bacc as bacc
    from concourse.bass_utils import run_bass_kernel_spmd as run

    a = {k: np.ascontiguousarray(v) for k, v in inputs.items()}
    rev = np.zeros((HEADS, KPAD), np.float32)
    rev[:, 0:L] = a["L0_xattn_ssm_kernel"][:, ::-1]
    arrays = {
        "x": a["x"], "ctx_rows": a["ctx_2048"], "mask": a["mask_BxS2_bk0"].view(np.int32), "g_xattn": a["g_xattn"],
        "g_ffn": a["g_ffn"], "kernel_rev": rev, "skip": a["L0_xattn_D"], "gate_w": a["L0_ffn_gate_w"],
        "mask_up_w": a["L0_ffn_mask_up_w"], "gate_p": a["L0_ffn_gate_proj_w"], "up_p": a["L0_ffn_up_proj_w"],
        "down_p": a["L0_ffn_down_proj_w"], "inv_map": a["L0_ffn_inv_map"], "w_fc": a["L1_ffn_w_fc"],
        "w_proj": a["L1_ffn_w_proj"],
    }
    nc = bacc.Bacc("TRN2", target_bir_lowering=False, num_devices=1)
    args = {n: nc.dram_tensor(f"in_{n}", v.shape, mybir.dt.from_np(v.dtype), kind="ExternalInput").ap()
            for n, v in arrays.items()}
    out = nc.dram_tensor("out_x", (B, P, L), F32, kind="ExternalOutput").ap()
    build(nc, out=out, **args)
    r = run(nc, [{f"in_{n}": v for n, v in arrays.items()}], core_ids=[0])
    return r.results[0]["out_x"]
```

```python
import numpy as np
import concourse.bass as bass
from concourse import mybir

F32, F32R, I32, U8 = mybir.dt.float32, mybir.dt.float32r, mybir.dt.int32, mybir.dt.uint8
ALU, ACT, AXX = mybir.AluOpType, mybir.ActivationFunctionType, mybir.AxisListType.X

P = 128
B, L = 8, 256
HEADS, HD = 16, 8
Q = 4
NE, NG, GS = 64, 8, 8
NI = 176
GI = NG * NI
TILES = GI // P
CW = 2 * NI
NCH = GI // CW
NJ = 640
JT = NJ // P
TAPS = 5
SPAN = 11
YW = TAPS * SPAN - 3
EXT = 15
KPAD = 384
EPS = 1e-5
DONE_TILES = [range(0, 2), range(2, 5), range(5, 8), range(8, 11)]
WORDS = {"gate": 0, "up": 1}

RING_LOADS = ["gate0", "gate1", "gate2", "up0", "up1", "up2", "down0", "down1", "fc", "proj"]
RING_LAST = {"gate0": ("turn_w", "gate", 1), "gate1": ("turn_w", "gate", 3), "gate2": ("turn_w", "gate", 5),
             "up0": ("turn_w", "up", 1), "up1": ("turn_w", "up", 3), "up2": ("turn_w", "up", 5),
             "down0": ("turn_down", 5), "down1": ("turn_down", 5), "fc": ("turn_fc", 2), "proj": ("turn_proj", 2)}


def spread(chain, filler):
    out, n = [], len(chain)
    for k, steps in enumerate(chain):
        out += steps + filler[k * len(filler) // n:(k + 1) * len(filler) // n]
    return out


def make_schedule():
    w_steps = [("turn_router",)]
    w_steps += [("turn_w", "gate", p) for p in range(6)] + [("turn_w", "up", p) for p in range(6)]
    w_steps += [("mask_up", w, c) for w in ("gate", "up") for c in range(NCH)]
    w_steps += [("turn_down", p) for p in range(6)]
    w_steps += [("tern_sum", "fc")] + [("turn_fc", p) for p in range(3)]
    w_steps += [("tern_sum", "proj")] + [("turn_proj", p) for p in range(3)]

    def conv_head(half, h):
        out = [("conv", half, h), ("fold", half, h)]
        g = h // 2
        if h % 2:
            if g + 2 < HEADS // 2:
                out.append(("kv", half, g + 2))
            if g >= 1:
                out.append(("gather", half, g - 1))
        return out

    s = [("turn_ctx", 0, 0), ("turn_ctx", 0, 1), ("stat", "mix", 0), ("kv", 0, 0), ("norm", "mix", 0), ("turn_q", 0, 0), ("turn_q", 0, 1),
         ("kv", 0, 1)]
    n_early = len(w_steps) - 6
    heads = []
    for h in range(HEADS):
        step = [("toe", h)] if h < 4 else []
        step += conv_head(0, h)
        if h == 1:
            step += [("consts",)]
        if h == 9:
            step += [("turn_ctx", 1, 0), ("turn_ctx", 1, 1)]
        if h == 14:
            step += [("stat", "mix", 1)]
        heads.append(step)
    s += sum(heads[:3], [])
    s += spread(heads[3:], w_steps[:n_early])
    rest = w_steps[n_early:]
    s += [("norm", "mix", 1), ("gather", 0, HEADS // 2 - 1), ("turn_q", 1, 0), ("turn_q", 1, 1),
          ("turn_att", 0, 0), ("turn_att", 0, 1), ("kv", 1, 0), ("kv", 1, 1)]

    def router(half):
        return [[("stat", "moe", half)], [("norm", "moe", half), ("turn_x", half, 0), ("turn_x", half, 1)], [("logits", half)],
                [("top", half)], [("turn_top", half)], [("flat", half)], [("soft", half)],
                [("turn_soft", half, 0), ("turn_soft", half, 1)]]

    n_between = 10
    chain = router(0)
    s += chain[0] + rest
    for item in spread(chain[1:-1], [conv_head(1, h) for h in range(n_between)]):
        s += item if isinstance(item, list) else [item]
    s += chain[-1]

    def experts(half, between):
        out, late = [], []
        n = Q * NCH
        for k in range(n):
            b, c = half * Q + k // NCH, k % NCH
            out.append(("chunk", b, c))
            out += between.get(k, [])
            out += late
            late = [("turn_a", b, c)] + ([("down", b)] if c == NCH - 1 else [])
        return out + late

    def layer1(u):
        return [[("stat", "cross", u)], [("norm", "cross", u), ("turn_0", u)], [("scores", u)], [("turn_p", u)],
                [("read", u), ("stat", "mlp", u)], [("norm", "mlp", u), ("turn_1", u)],
                [("hidden", u, j) for j in range(3)], [("out", u)]]

    between = {}
    for k in range((HEADS - n_between) // 2):
        between[k] = sum([conv_head(1, h) for h in (n_between + 2 * k, n_between + 2 * k + 1)], [])
    between[4] = [("gather", 1, HEADS // 2 - 1), ("turn_att", 1, 0), ("turn_att", 1, 1)]
    for k, steps in enumerate(router(1)):
        between[5 + k] = steps
    for k, steps in enumerate(layer1(0)[:6]):
        between[10 + k] = between.get(10 + k, []) + steps
    s += experts(0, between)
    between = {}
    for k, steps in enumerate(layer1(0)[6:] + layer1(1) + layer1(2)[:6]):
        between[k] = steps
    s += experts(1, between)
    s += sum(layer1(2)[6:] + layer1(3), [])
    return s


SCHEDULE = make_schedule()
G0, U0, G1, U1, Y0, Y1, TR, DN = range(8)


def plan_psum():
    early = [G0, U0, G1, U1, TR, DN]
    late = [TR, DN]
    mixed = [Y0, Y1]
    n_early = n_late = n_mixed = 0
    uses, n_use, n_read = {}, [0] * 8, [0] * 8
    first_chunk = SCHEDULE.index(("chunk", 0, 0))
    conv_end = SCHEDULE.index(("gather", 1, HEADS // 2 - 1))
    tail = SCHEDULE.index(("down", B - 1))
    conv = 0

    def use(key, bank, reads):
        uses[key] = (bank, n_use[bank], n_read[bank], reads)
        n_use[bank] += 1
        n_read[bank] += reads

    reads = {"turn_ctx": 3, "turn_q": 3, "turn_router": 2, "turn_w": 2, "mask_up": 4, "turn_down": 2, "tern_sum": 1,
             "turn_fc": 1, "turn_proj": 1, "turn_att": 1, "turn_x": 2, "logits": 2, "turn_top": 1, "flat": 3,
             "turn_soft": 1, "turn_0": 1, "turn_1": 2, "scores": 1, "turn_p": 1, "read": 2, "hidden": 1, "out": 1}
    for i, step in enumerate(SCHEDULE):
        kind = step[0]
        if kind == "conv":
            use(step, [Y0, Y1][conv % 2], 2)
            conv += 1
        elif kind == "chunk":
            k = (step[1] * NCH + step[2]) % 2
            use(("gate",) + step[1:], [G0, G1][k], 1)
            use(("up",) + step[1:], [U0, U1][k], 2)
        elif kind == "turn_a":
            use(step, TR, 2)
        elif kind == "down":
            use(step, DN, 1)
        elif kind in reads:
            n = reads[kind]
            if i < first_chunk or i > tail:
                use(step, early[n_early % 6], n)
                n_early += 1
            elif i < conv_end:
                use(step, late[n_late % 2], n)
                n_late += 1
            else:
                use(step, mixed[n_mixed % 2], n)
                n_mixed += 1
    return uses


USES = plan_psum()
NORMS = [s[1:] for s in SCHEDULE if s[0] == "stat"]
assert NORMS == [s[1:] for s in SCHEDULE if s[0] == "norm"]


def batches_of(which, k):
    return range(k * Q, (k + 1) * Q) if which in ("mix", "moe") else range(2 * k, 2 * k + 2)


def rows_normed(which, k):
    return sum(len(batches_of(*m)) for m in NORMS[:NORMS.index((which, k)) + 1])


HIDDEN = [(u, j) for _, u, j in (s for s in SCHEDULE if s[0] == "hidden")]


def build(nc, x, ctx_rows, mask, g_xattn, g_ffn, kernel_rev, skip, gate_w, mask_up_w, gate_p, up_p, down_p, inv_map,
          w_fc, w_proj, out):
    at = [((nc.sbuf_base + 31) // 32) * 32]

    def region(size):
        start = at[0]
        at[0] += -(-size // 32) * 32
        assert at[0] <= nc.sbuf_usable_end, at[0] - nc.sbuf_usable_end
        return start

    def sb(name, shape, dt=F32, offset=None):
        size = int(np.prod(shape[1:])) * (1 if dt == U8 else 4)
        return nc.alloc_sbuf_tensor_at(name, shape, dt, offset=region(size) if offset is None else offset)

    x_res = sb("x_res", [P, B, L])
    ctx = sb("ctx", [P, B, L])
    ctx_ext = sb("ctx_ext", [P, 2, HEADS, 2, Q, EXT])
    w_split = sb("w_split", [P, 2, 2, 2, GI], F32R)
    toe_raw = nc.alloc_sbuf_tensor_at("toe_raw", [P, HEADS, 256], F32, offset=at[0] - 4 * 8 * GI)
    d_split = sb("d_split", [P, TILES, 2, L], F32R)
    m_stack = sb("m_stack", [P, 2, GI], F32R)
    fc_t = sb("fc_t", [P, 2, NJ], F32R)
    proj_t = sb("proj_t", [P, JT, L], F32R)
    xt_at = region(4 * 2 * 2 * 512)
    xt = [sb("xt0", [P, 2, 2, 512], F32R, xt_at)]
    half_m = sb("half_m", [P, 2, CW], F32R, xt_at)
    tern_tmp = sb("tern_tmp", [P, 2 * NJ], F32, xt_at + 4 * 2 * CW)
    soft_at = region(4 * 2 * 512)
    soft_t = [sb("soft_t0", [P, 2, 512], F32R, soft_at)]
    mu4 = sb("mu4", [P, 2, 4, 4 * 32], F32R, soft_at)
    ring_at = region(4 * TILES * 2 * P)
    a_t = sb("a_t", [P, TILES, 2, P], F32R, ring_at)
    a_at = region(4 * GI)
    act = sb("act", [P, GI], F32, a_at)
    silu_at = region(4 * 2 * CW)
    silu = sb("silu", [P, 2, CW], F32, silu_at)
    ring = [sb(f"ring{k}", [P, GI], F32, ring_at + 4 * GI * k) for k in range(3)]
    assert ring_at + 12 * GI <= silu_at + 4 * 2 * CW
    rts = [[sb(f"rt0_{k}", [P, Q * NE], F32, a_at + 4 * Q * NE * k) for k in range(4)]]
    top_t = [sb("top_t0", [NE, 512], F32, silu_at)]
    xn_at = region(4 * Q * L)
    xn = sb("xn", [P, Q, L], F32, xn_at)
    soft_parts = sb("soft_parts", [P, Q * 2, 4, 32], F32, xn_at)
    xn1 = sb("xn1", [P, 2, L])
    mixer_at = at[0]
    toe = sb("toe", [P, HEADS, 256])
    q_ext = sb("q_ext", [P, HEADS, 2 * Q, EXT])
    kv = sb("kv", [P, 2, 4 * Q, TAPS, SPAN])
    prod = sb("prod", [P, 2, 2 * Q, HD, HD])
    fold = sb("fold", [P, 2, 4 * Q, 4, HD])
    att = sb("att", [P, 2 * Q, HEADS, HD])
    mixer_end = at[0]
    at[0] = mixer_at
    xt.append(sb("xt1", [P, 2, 2, 512], F32R))
    soft_t.append(sb("soft_t1", [P, 2, 512], F32R))
    hid_t = sb("hid_t", [P, JT, 2, 2 * P], F32R)
    x1t = sb("x1t", [P, 2, 2, 2 * P], F32R)
    qt = sb("qt", [P, 2, 2 * P])
    neg = sb("neg", [P, B * P])
    s_att = sb("s_att", [P, 2, P])
    pt = sb("pt", [P, 2 * P])
    relu_at = region(4 * 4 * 512)
    relu = sb("relu", [P, 2, 512], F32, relu_at)
    hsq = sb("hsq", [P, 2, 512], F32, relu_at + 4 * 2 * 512)
    rts.append([sb(f"rt1_{k}", [P, Q * NE], F32, relu_at + 4 * Q * NE * k) for k in range(4)])
    top_t.append(sb("top_t1", [NE, 512], F32, relu_at + 16 * Q * NE))
    assert at[0] <= mixer_end, at[0] - mixer_end
    at[0] = mixer_end
    mask_words = sb("mask_words", [P, B * P // 4], I32)
    mask_sb = mask_words[:, :].bitcast(U8)
    ident = sb("ident", [P, P])
    ones = sb("ones", [P, P])
    router_w = sb("router_w", [NE, L])
    router_t = sb("router_t", [P, 2, 2, NE], F32R)
    mu = sb("mu", [P, 2, NE])
    onehot = sb("onehot", [NE, NE])
    inv_i = sb("inv_i", [NE, NE], I32)
    inv_f = sb("inv_f", [NE, 2, NE])
    skip_sb = sb("skip_sb", [P, HEADS])
    gates = sb("gates", [P, 4])
    tg = sb("tg", [P, 4])
    pidx = sb("pidx", [P, 3], I32)
    pidx_f = sb("pidx_f", [P, 3])
    ind = sb("ind", [P, 2, 4])
    stats = sb("stats", [P, Q, 6])
    mv = sb("mv", [P, Q, 2])
    ve = sb("ve", [P, Q])
    rstd = sb("rstd", [P, Q])
    mhalf = sb("mhalf", [P, Q])
    nmax = sb("nmax", [P, Q])
    nmax1 = sb("nmax1", [P, 2])
    rsum = sb("rsum", [P, 2, Q])
    top8 = sb("top8", [P, Q, 8])
    scal = sb("scal", [P, B, NG])
    gmax = sb("gmax", [P, 3, Q * NG])
    tern = sb("tern", [P, 2, 6])
    out_scale = sb("out_scale", [P, 3])
    valid = sb("valid", [P, 2, B])
    esum = sb("esum", [P, 2])
    rv = sb("rv", [P, 2, 2])

    banks = [nc.alloc_psum_tensor(f"bank{k}", [P, 512], F32) for k in range(8)]
    filled = [nc.alloc_semaphore(f"filled{k}") for k in range(8)]
    drained = [nc.alloc_semaphore(f"drained{k}") for k in range(8)]
    sem = nc.alloc_semaphore
    x_loaded = [sem("x_loaded0"), sem("x_loaded1")]
    ctx_loaded = [sem("ctx_loaded0"), sem("ctx_loaded1")]
    toe_loaded = [sem(f"toe_loaded{k}") for k in range(4)]
    skip_loaded = sem("skip_loaded")
    small_loaded, mask_loaded = sem("small_loaded"), sem("mask_loaded")
    ring_loaded = [sem(f"ring_loaded{k}") for k in range(3)]
    consts_made = sem("consts_made")
    toe_diag, toe_off = sem("toe_diag"), sem("toe_off")
    tanh_done = sem("tanh_done")
    mu4_made, onehot_made, ind_made = sem("mu4_made"), sem("onehot_made"), sem("ind_made")
    kv_made = sem("kv_made")
    folded, gathered = sem("folded"), sem("gathered")
    stats_done, rstd_done, normed = sem("stats_done"), sem("rstd_done"), sem("normed")
    shifted, router_exp, chosen = sem("shifted"), sem("router_exp"), sem("chosen")
    soft_shifted, soft_exp, soft_made = sem("soft_shifted"), sem("soft_exp"), sem("soft_made")
    tern_abs, tern_made = sem("tern_abs"), sem("tern_made")
    s_shifted, s_exp = sem("s_shifted"), sem("s_exp")
    sq_done, hid_hi, hid_lo = sem("sq_done"), sem("hid_hi"), sem("hid_lo")
    dve_own, pool_own = sem("dve_own"), sem("pool_own")
    stored = sem("stored")

    def psum(key):
        return banks[USES[key][0]]

    def claim(eng, key):
        bank, _, before, _ = USES[key]
        if before:
            eng.wait_ge(drained[bank], before)

    def fill(ins, key):
        ins.then_inc(filled[USES[key][0]], 1)

    def wait_filled(eng, key):
        bank, n, _, _ = USES[key]
        eng.wait_ge(filled[bank], n + 1)

    def wait_drained(eng, key, reads=None):
        bank, _, before, n = USES[key]
        eng.wait_ge(drained[bank], before + (n if reads is None else reads))

    def drain(ins, key):
        ins.then_inc(drained[USES[key][0]], 1)

    def group_no(half, g):
        return half * (HEADS // 2) + g

    def view(t, offset, dims):
        whole = t[:]
        return bass.AP(whole.tensor, whole.offset + offset, [list(whole.ap[0])] + [list(d) for d in dims])

    def updates_of_x(eng, which, k):
        if which == "mix":
            eng.wait_ge(x_loaded[k], 16)
        elif which == "moe":
            for p in range(2):
                wait_drained(eng, ("turn_att", k, p))
        elif which == "cross":
            for b in batches_of(which, k):
                wait_drained(eng, ("down", b))
        else:
            wait_drained(eng, ("read", k))

    def turned(eng, which, k):
        if which in ("mix", "moe"):
            for t in range(2):
                wait_filled(eng, ("turn_q" if which == "mix" else "turn_x", k, t))
        else:
            wait_filled(eng, ("turn_0" if which == "cross" else "turn_1", k))

    def mixer_free(eng):
        eng.wait_ge(gathered, HEADS)
        for h in (HEADS - 2, HEADS - 1):
            wait_filled(eng, ("conv", 1, h))
        for p in range(2):
            wait_filled(eng, ("turn_att", 1, p))

    block = nc.Block()
    with block:
        @block.sync
        def _(sp):
            def rows_of(src, half):
                return src[half * Q:(half + 1) * Q].rearrange("b p l -> p b l")

            def ring_load(n):
                name = RING_LOADS[n]
                if n >= 3:
                    wait_filled(sp, RING_LAST[RING_LOADS[n - 3]])
                slot = ring[n % 3]
                if name[:-1] in ("gate", "up"):
                    src = (gate_p if name[0] == "g" else up_p).rearrange("g i h -> (g i) h")
                    r0 = 4 * int(name[-1])
                    n_t = min(4, TILES - r0)
                    src = src[r0 * P:(r0 + n_t) * P, :].rearrange("(r p) h -> p r h", p=P)
                    dst = slot[:, 0:n_t * L].rearrange("p (r h) -> p r h", h=L)
                elif name[:-1] == "down":
                    kt = int(name[-1])
                    src = down_p[:, kt * P:(kt + 1) * P, :].rearrange("g h i -> h g i")
                    dst = slot[:, :].rearrange("p (g i) -> p g i", i=NI)
                elif name == "fc":
                    src = w_fc.rearrange("(r p) h -> p r h", p=P)
                    dst = slot[:, 0:JT * L].rearrange("p (r h) -> p r h", h=L)
                else:
                    src = w_proj.rearrange("(r p) j -> p r j", p=P)
                    dst = slot[:, 0:2 * NJ].rearrange("p (r j) -> p r j", j=NJ)
                sp.dma_start(dst, src).then_inc(ring_loaded[n % 3], 16)

            sp.dma_start(ctx[:, 0:Q, :], rows_of(ctx_rows, 0)).then_inc(ctx_loaded[0], 16)
            sp.dma_start(x_res[:, 0:Q, :], rows_of(x, 0)).then_inc(x_loaded[0], 16)
            sp.dma_start(skip_sb[:, :], skip.partition_broadcast(P)).then_inc(skip_loaded, 16)
            for k in range(4):
                src = bass.AP(kernel_rev.tensor, k * 4 * KPAD, [[1, P], [KPAD, 4], [1, 256]])
                sp.dma_start(toe_raw[:, 4 * k:4 * k + 4, :], src).then_inc(toe_loaded[k], 16)
            sp.dma_start(router_w[:, :], gate_w).then_inc(small_loaded, 16)
            sp.dma_start(gates[:, 0:2], g_xattn.partition_broadcast(P)).then_inc(small_loaded, 16)
            sp.dma_start(gates[:, 2:4], g_ffn.partition_broadcast(P)).then_inc(small_loaded, 16)
            sp.dma_start(inv_i[:, :], inv_map.rearrange("a b -> (a b)").partition_broadcast(NE)).then_inc(small_loaded, 16)
            for kt in range(2):
                sp.dma_start(mu[:, kt, :].rearrange("p (g s) -> p g s", g=NG),
                             mask_up_w[:, kt * P:(kt + 1) * P, :].rearrange("g h s -> h g s")).then_inc(small_loaded, 16)
            for n in range(3):
                ring_load(n)
            sp.dma_start(ctx[:, Q:B, :], rows_of(ctx_rows, 1)).then_inc(ctx_loaded[1], 16)
            sp.dma_start(x_res[:, Q:B, :], rows_of(x, 1)).then_inc(x_loaded[1], 16)
            sp.dma_start(mask_words[:, :], mask.rearrange("b m -> (b m)").partition_broadcast(P)).then_inc(mask_loaded, 16)
            for n in range(3, len(RING_LOADS)):
                ring_load(n)
            for u in range(B // 2):
                wait_drained(sp, ("out", u))
                sp.dma_start(out[2 * u:2 * u + 2].rearrange("b p l -> p b l"),
                             x_res[:, 2 * u:2 * u + 2, :]).then_inc(stored, 16)
            sp.wait_ge(stored, 64)

        SMALL = 16 * 6

        @block.tensor
        def _(pe):
            def split_product(dst, lhs, rhs, start, stop):
                for i, (a, b) in enumerate(((0, 0), (1, 0), (0, 1))):
                    last = pe.matmul(dst, lhs(a), rhs(b), start=start and i == 0, stop=stop and i == 2)
                return last

            def turn(key, pieces, waits=()):
                claim(pe, key)
                for k, (piece, rows, cols) in enumerate(pieces):
                    last = pe.transpose(psum(key)[0:cols, k * rows:(k + 1) * rows], piece, ident[0:rows, 0:rows])
                fill(last, key)

            pe.wait_ge(consts_made, 2)
            for step in SCHEDULE:
                kind = step[0]
                if kind == "turn_ctx":
                    _, half, t = step
                    pe.wait_ge(ctx_loaded[half], 16)
                    turn(step, [(ctx[:, half * Q + q, t * P:(t + 1) * P], P, P) for q in range(Q)])
                elif kind in ("turn_q", "turn_x"):
                    _, half, t = step
                    pe.wait_ge(normed, rows_normed("mix" if kind == "turn_q" else "moe", half))
                    turn(step, [(xn[:, q, t * P:(t + 1) * P], P, P) for q in range(Q)])
                elif kind in ("turn_0", "turn_1"):
                    u = step[1]
                    pe.wait_ge(normed, rows_normed("cross" if kind == "turn_0" else "mlp", u))
                    turn(step, [(xn1[:, k, t * P:(t + 1) * P], P, P) for t in range(2) for k in range(2)])
                elif kind == "conv":
                    _, half, h = step
                    g = group_no(half, h // 2)
                    if half == 0:
                        pe.wait_ge(toe_diag, h // 4 + 1)
                        pe.wait_ge(toe_off, h // 4 + 1)
                    pe.wait_ge(kv_made, g + 1)
                    claim(pe, step)

                    def pairs(t):
                        return kv[:, g % 2, (2 * (h % 2) + t) * Q:(2 * (h % 2) + t + 1) * Q].rearrange(
                            "p q d j -> p q (d j)")[:, :, 3:TAPS * SPAN]
                    y = psum(step)[:, 0:2 * Q * YW].rearrange("p (t q c) -> p t q c", t=2, q=Q)
                    pe.matmul(y[:, 0], toe[:, h, 0:P], pairs(0), start=True, stop=True)
                    pe.matmul(y[:, 1], toe[:, h, P:2 * P], pairs(0), start=True, stop=False)
                    fill(pe.matmul(y[:, 1], toe[:, h, 0:P], pairs(1), start=False, stop=True), step)
                elif kind == "turn_router":
                    pe.wait_ge(small_loaded, SMALL)
                    turn(step, [(router_w[:, t * P:(t + 1) * P], NE, P) for t in range(2)])
                elif kind == "turn_w":
                    _, which, p = step
                    n = RING_LOADS.index(f"{which}{p // 2}")
                    pe.wait_ge(ring_loaded[n % 3], 16 * (n // 3 + 1))
                    tiles = range(2 * p, min(2 * p + 2, TILES))
                    turn(step, [(ring[n % 3][:, (r % 4) * L + kt * P:(r % 4) * L + (kt + 1) * P], P, P)
                                for kt in range(2) for r in tiles])
                elif kind == "turn_down":
                    p = step[1]
                    for kt in range(2):
                        n = RING_LOADS.index(f"down{kt}")
                        pe.wait_ge(ring_loaded[n % 3], 16 * (n // 3 + 1))
                    n = RING_LOADS.index("down0")
                    turn(step, [(ring[(n + kt) % 3][:, r * P:(r + 1) * P], P, P)
                                for r in range(2 * p, min(2 * p + 2, TILES)) for kt in range(2)])
                elif kind == "mask_up":
                    _, which, c = step
                    pe.wait_ge(mu4_made, 2)
                    for p in range(6):
                        wait_drained(pe, ("turn_w", which, p))
                    claim(pe, step)
                    for kt in range(2):
                        last = split_product(psum(step)[:, 0:CW], lambda part: mu4[:, part, 2 * kt + c // 2, :],
                                             lambda part: w_split[:, WORDS[which], kt, part, c * CW:(c + 1) * CW],
                                             kt == 0, kt == 1)
                    fill(last, step)
                elif kind == "tern_sum":
                    k = 0 if step[1] == "fc" else 1
                    pe.wait_ge(tern_abs, k + 1)
                    claim(pe, step)
                    fill(pe.matmul(psum(step)[:, 0:1], ones[:, :], tern[:, k, 0:1], start=True, stop=True), step)
                elif kind == "turn_fc":
                    p = step[1]
                    pe.wait_ge(tern_made, 1)
                    slot = ring[RING_LOADS.index("fc") % 3]
                    turn(step, [(slot[:, r * L + kt * P:r * L + (kt + 1) * P], P, P)
                                for kt in range(2) for r in range(2 * p, min(2 * p + 2, JT))])
                elif kind == "turn_proj":
                    p = step[1]
                    pe.wait_ge(tern_made, 2)
                    slot = ring[RING_LOADS.index("proj") % 3]
                    turn(step, [(slot[:, kt * NJ + r * P:kt * NJ + (r + 1) * P], P, P)
                                for r in range(2 * p, min(2 * p + 2, JT)) for kt in range(2)])
                elif kind == "turn_att":
                    _, half, p = step
                    pe.wait_ge(gathered, group_no(half, HEADS // 2 - 1) + 1)
                    turn(step, [(att[:, t * Q + q].rearrange("p h j -> p (h j)"), P, P) for q in (2 * p, 2 * p + 1) for t in range(2)])
                elif kind == "logits":
                    half = step[1]
                    wait_drained(pe, ("turn_router",))
                    for t in range(2):
                        wait_drained(pe, ("turn_x", half, t))
                    claim(pe, step)
                    for q in range(Q):
                        for kt in range(2):
                            last = split_product(psum(step)[:, q * NE:(q + 1) * NE],
                                                 lambda part: xt[half][:, kt, part, q * P:(q + 1) * P],
                                                 lambda part: router_t[:, kt, part, :], kt == 0, kt == 1)
                    fill(last, step)
                elif kind == "turn_top":
                    half = step[1]
                    pe.wait_ge(chosen, half + 1)
                    turn(step, [(rts[half][3][:, q * NE:(q + 1) * NE], P, NE) for q in range(Q)])
                elif kind == "flat":
                    half = step[1]
                    pe.wait_ge(onehot_made, 1)
                    wait_drained(pe, ("turn_top", half))
                    claim(pe, step)
                    for q in range(Q):
                        last = pe.matmul(psum(step)[:, q * NE:(q + 1) * NE], top_t[half][:, q * P:(q + 1) * P], onehot[:, :],
                                         start=True, stop=True)
                    fill(last, step)
                elif kind == "turn_soft":
                    _, half, gh = step
                    pe.wait_ge(soft_made, half + 1)
                    turn(step, [(soft_parts[:, 2 * q + gh].rearrange("p a c -> p (a c)"), P, P) for q in range(Q)])
                elif kind == "chunk":
                    _, b, c = step
                    half, q = b // Q, b % Q
                    if b == 0 and c == 0:
                        for which in WORDS:
                            for k in range(NCH):
                                wait_drained(pe, ("mask_up", which, k))
                    for gh in range(2):
                        wait_drained(pe, ("turn_soft", half, gh))
                    claim(pe, ("gate", b, c))
                    claim(pe, ("up", b, c))
                    rows = slice(q * P, (q + 1) * P)
                    cols = slice(c * CW, (c + 1) * CW)
                    ops = [(xt[half][:, kt, pa, rows], kt, pb) for kt in range(2) for pa, pb in ((0, 0), (0, 1), (1, 0))]
                    for i, (lhs, kt, part) in enumerate(ops):
                        for w, name in enumerate(("gate", "up")):
                            pe.matmul(psum((name, b, c))[:, 0:CW], lhs, w_split[:, w, kt, part, cols],
                                      start=i == 0, stop=False)
                    for w, name in enumerate(("gate", "up")):
                        fill(pe.matmul(psum((name, b, c))[:, 0:CW], soft_t[half][:, c // 2, rows], m_stack[:, w, cols],
                                       start=False, stop=True), (name, b, c))
                elif kind == "turn_a":
                    _, b, c = step
                    wait_drained(pe, ("up", b, c))
                    turn(step, [(act[:, r * P:(r + 1) * P], P, P) for r in DONE_TILES[c]])
                elif kind == "down":
                    b = step[1]
                    if b == 0:
                        for p in range(6):
                            wait_drained(pe, ("turn_down", p))
                    wait_drained(pe, ("turn_a", b, NCH - 1))
                    claim(pe, step)
                    for r in range(TILES):
                        last = split_product(psum(step)[:, 0:L], lambda part: a_t[:, r, part, :],
                                             lambda part: d_split[:, r, part, :], r == 0, r == TILES - 1)
                    fill(last, step)
                elif kind == "scores":
                    u = step[1]
                    wait_drained(pe, ("turn_0", u))
                    claim(pe, step)
                    for k in range(2):
                        half, q = divmod(2 * u + k, Q)
                        for t in range(2):
                            last = pe.matmul(psum(step)[:, k * P:(k + 1) * P], qt[:, t, k * P:(k + 1) * P],
                                             ctx_ext[:, half, :, t, q, 3:3 + HD], start=t == 0, stop=t == 1)
                    fill(last, step)
                elif kind == "turn_p":
                    u = step[1]
                    pe.wait_ge(s_exp, 2 * (u + 1))
                    turn(step, [(s_att[:, k, :], P, P) for k in range(2)])
                elif kind == "read":
                    u = step[1]
                    wait_drained(pe, ("turn_p", u))
                    claim(pe, step)
                    for k in range(2):
                        last = pe.matmul(psum(step)[:, k * L:(k + 1) * L], pt[:, k * P:(k + 1) * P],
                                         ctx[:, 2 * u + k, :], start=True, stop=True)
                    fill(last, step)
                elif kind == "hidden":
                    _, u, jp = step
                    wait_drained(pe, ("turn_1", u))
                    if u == 0 and jp == 0:
                        for p in range(3):
                            wait_drained(pe, ("turn_fc", p))
                    claim(pe, step)
                    for i, j in enumerate(range(2 * jp, min(2 * jp + 2, JT))):
                        for kt in range(2):
                            for part in range(2):
                                last = pe.matmul(psum(step)[:, i * 2 * P:(i + 1) * 2 * P],
                                                 fc_t[:, kt, j * P:(j + 1) * P], x1t[:, part, kt, :],
                                                 start=kt + part == 0, stop=kt + part == 2)
                    fill(last, step)
                elif kind == "out":
                    u = step[1]
                    if u == 0:
                        for k in range(3):
                            wait_drained(pe, ("turn_proj", k))
                    pe.wait_ge(hid_lo, 3 * (u + 1))
                    claim(pe, step)
                    for k in range(2):
                        for j in range(JT):
                            for part in range(2):
                                last = pe.matmul(psum(step)[:, k * L:(k + 1) * L],
                                                 hid_t[:, j, part, k * P:(k + 1) * P],
                                                 proj_t[:, j, :], start=j + part == 0, stop=j + part == JT)
                    fill(last, step)

        @block.scalar
        def _(act_e):
            def copy(dst, src):
                return act_e.activation(dst, src, ACT.Copy)

            for step in SCHEDULE:
                kind = step[0]
                if kind == "consts":
                    act_e.wait_ge(small_loaded, SMALL)
                    act_e.activation(tg[:, :], gates[:, :], ACT.Tanh).then_inc(tanh_done, 1)
                elif kind == "toe":
                    k = step[1]
                    act_e.wait_ge(toe_loaded[k], 16)
                    src = toe_raw[:, 4 * k:4 * k + 4, 0:P]
                    copy(toe[:, 4 * k:4 * k + 4, P:2 * P], src[:, :, ::-1]).then_inc(toe_off, 1)
                elif kind in ("turn_ctx", "turn_q"):
                    _, half, t = step
                    if kind == "turn_q" and half == 1 and t == 0:
                        for h in (HEADS - 2, HEADS - 1):
                            wait_drained(act_e, ("conv", 0, h))
                    wait_filled(act_e, step)
                    src = psum(step)[:, :].rearrange("p (q h i) -> p q h i", q=Q, h=HEADS)
                    dst = (ctx_ext[:, half, :, t, :, :] if kind == "turn_ctx" else
                           q_ext[:, :, t * Q:(t + 1) * Q, :]).rearrange("p h q e -> p q h e")
                    for d0, s0, n in ((3, 0, 8), (0, 5, 3), (11, 0, 4)):
                        drain(copy(dst[:, :, :, d0:d0 + n], src[:, :, :, s0:s0 + n]), step)
                elif kind == "turn_router":
                    wait_filled(act_e, step)
                    drain(copy(router_t[:, :, 0, :], psum(step)[:, 0:2 * NE].rearrange("p (t e) -> p t e", t=2)), step)
                elif kind == "turn_w":
                    _, which, p = step
                    if which == "gate" and p == 0:
                        act_e.wait_ge(toe_diag, 4)
                        act_e.wait_ge(toe_off, 4)
                    wait_filled(act_e, step)
                    n = P * len(range(2 * p, min(2 * p + 2, TILES)))
                    drain(copy(w_split[:, WORDS[which], :, 0, 2 * p * P:2 * p * P + n],
                               psum(step)[:, 0:2 * n].rearrange("p (t c) -> p t c", t=2)), step)
                elif kind == "turn_down":
                    p = step[1]
                    wait_filled(act_e, step)
                    n = len(range(2 * p, min(2 * p + 2, TILES)))
                    drain(copy(d_split[:, 2 * p:2 * p + n, 0, :],
                               psum(step)[:, 0:n * L].rearrange("p (r c) -> p r c", c=L)), step)
                elif kind == "mask_up":
                    _, which, c = step
                    act_e.wait_ge(ind_made, 2)
                    k = WORDS[which] * NCH + c
                    if k >= 2:
                        prev = [("mask_up", w, cc) for w in WORDS for cc in range(NCH)][k - 2]
                        wait_drained(act_e, prev)
                    wait_filled(act_e, step)
                    for i in range(2):
                        cols = slice(i * NI, (i + 1) * NI)
                        g = 2 * (c % 2) + i
                        drain(act_e.activation(half_m[:, k % 2, cols], psum(step)[:, cols], ACT.Copy,
                                               scale=ind[:, 1, g:g + 1]), step)
                elif kind == "turn_fc":
                    p = step[1]
                    wait_filled(act_e, step)
                    n = P * len(range(2 * p, min(2 * p + 2, JT)))
                    drain(copy(fc_t[:, :, 2 * p * P:2 * p * P + n],
                               psum(step)[:, 0:2 * n].rearrange("p (t c) -> p t c", t=2)), step)
                elif kind == "turn_proj":
                    p = step[1]
                    wait_filled(act_e, step)
                    n = len(range(2 * p, min(2 * p + 2, JT)))
                    drain(copy(proj_t[:, 2 * p:2 * p + n, :],
                               psum(step)[:, 0:n * L].rearrange("p (r c) -> p r c", c=L)), step)
                elif kind == "turn_x":
                    _, half, t = step
                    if half == 0 and t == 0:
                        for w in WORDS:
                            wait_drained(act_e, ("mask_up", w, NCH - 1))
                        act_e.wait_ge(tern_made, 2)
                    elif t == 0:
                        mixer_free(act_e)
                    wait_filled(act_e, step)
                    drain(copy(xt[half][:, t, 0, :], psum(step)[:, :]), step)
                elif kind == "turn_0":
                    u = step[1]
                    if u:
                        wait_filled(act_e, ("scores", u - 1))
                    wait_filled(act_e, step)
                    drain(copy(qt[:, :, :].rearrange("p t n -> p (t n)"), psum(step)[:, :]), step)
                elif kind == "turn_1":
                    u = step[1]
                    if u:
                        wait_filled(act_e, ("hidden", u - 1, 2))
                    wait_filled(act_e, step)
                    drain(copy(x1t[:, 0].rearrange("p t n -> p (t n)"), psum(step)[:, :]), step)
                elif kind == "top":
                    half = step[1]
                    act_e.wait_ge(shifted, half + 1)
                    act_e.activation(rts[half][0][:, :], rts[half][0][:, :], ACT.Exp).then_inc(router_exp, 1)
                elif kind == "turn_top":
                    half = step[1]
                    if half == 0:
                        wait_filled(act_e, ("turn_proj", 2))
                    wait_filled(act_e, step)
                    drain(copy(top_t[half][:, :], psum(step)[0:NE, :]), step)
                elif kind == "soft":
                    half = step[1]
                    act_e.wait_ge(soft_shifted, half + 1)
                    act_e.activation(rts[half][1][:, :], rts[half][1][:, :], ACT.Exp).then_inc(soft_exp, 1)
                elif kind == "turn_soft":
                    _, half, gh = step
                    wait_filled(act_e, step)
                    drain(copy(soft_t[half][:, gh, :], psum(step)[:, :]), step)
                elif kind == "chunk":
                    _, b, c = step
                    n = b * NCH + c
                    if n == 0:
                        wait_filled(act_e, ("flat", 0))
                    if n >= 2:
                        wait_drained(act_e, ("up", (n - 2) // NCH, (n - 2) % NCH))
                    wait_filled(act_e, ("gate", b, c))
                    drain(act_e.activation(silu[:, n % 2, :], psum(("gate", b, c))[:, 0:CW], ACT.Silu), ("gate", b, c))
                elif kind == "turn_a":
                    _, b, c = step
                    if b >= 1:
                        wait_filled(act_e, ("down", b - 1))
                    wait_filled(act_e, step)
                    r = DONE_TILES[c]
                    drain(copy(a_t[:, r.start:r.stop, 0, :],
                               psum(step)[:, 0:len(r) * P].rearrange("p (r n) -> p r n", n=P)), step)
                elif kind == "scores":
                    u = step[1]
                    act_e.wait_ge(s_shifted, u + 1)
                    for k in range(2):
                        act_e.activation(s_att[:, k, :], s_att[:, k, :], ACT.Exp, bias=nmax1[:, k:k + 1],
                                         accum_out=esum[:, k:k + 1]).then_inc(s_exp, 1)
                elif kind == "turn_p":
                    u = step[1]
                    if u:
                        wait_filled(act_e, ("read", u - 1))
                    wait_filled(act_e, step)
                    drain(copy(pt[:, :], psum(step)[:, 0:2 * P]), step)
                elif kind == "hidden":
                    _, u, jp = step
                    n = HIDDEN.index((u, jp))
                    w = 2 * P * len(range(2 * jp, min(2 * jp + 2, JT)))
                    if n == 0:
                        wait_filled(act_e, ("flat", 1))
                        act_e.wait_ge(soft_made, 2)
                    if n >= 2:
                        act_e.wait_ge(sq_done, n - 1)
                    wait_filled(act_e, step)
                    drain(act_e.activation(relu[:, n % 2, 0:w], psum(step)[:, 0:w], ACT.Relu), step)
                    if u and jp == 0:
                        wait_filled(act_e, ("out", u - 1))
                    act_e.wait_ge(sq_done, n + 1)
                    copy(hid_t[:, 2 * jp:2 * jp + w // (2 * P), 0, :],
                         hsq[:, n % 2, 0:w].rearrange("p (j c) -> p j c", c=2 * P)).then_inc(hid_hi, 1)

        @block.vector
        def _(dve):
            own = [0]

            def mine(ins):
                own[0] += 1
                ins.then_inc(dve_own, 1)
                dve.wait_ge(dve_own, own[0])

            def residue(dst, key, src, hi, reads=1):
                wait_drained(dve, key, reads)
                drain(dve.tensor_tensor(dst, src, hi.bitcast(F32), ALU.subtract), key)

            dve.wait_ge(consts_made, 4)
            for step in SCHEDULE:
                kind = step[0]
                if kind == "consts":
                    dve.wait_ge(small_loaded, SMALL)
                    dve.tensor_scalar(pidx[:, 1:2], pidx[:, 0:1], 3, 3, ALU.logical_shift_right, ALU.bitwise_and)
                    mine(dve.tensor_scalar(pidx[:, 2:3], pidx[:, 0:1], 5, 1, ALU.logical_shift_right, ALU.bitwise_and))
                    mine(dve.tensor_copy(pidx_f[:, :], pidx[:, :]))
                    for g in range(4):
                        last = dve.tensor_scalar(ind[:, 0, g:g + 1], pidx_f[:, 1:2], float(g), None, ALU.is_equal)
                    last.then_inc(ind_made, 1)
                    dve.wait_ge(ind_made, 1)
                    dve.tensor_scalar(ind[:, 1, :], ind[:, 0, :], pidx_f[:, 2:3], None, ALU.mult).then_inc(ind_made, 1)
                    mine(dve.tensor_copy(inv_f[:, 0, :], inv_i[:, :]))
                    mine(dve.tensor_scalar(inv_f[:, 1, :], inv_f[:, 0, :], 0.0, float(NE), ALU.is_lt, ALU.mult))
                    mine(dve.tensor_tensor(inv_f[:, 0, :], inv_f[:, 0, :], inv_f[:, 1, :], ALU.add))
                    dve.tensor_scalar(onehot[:, :], inv_f[:, 0, :], pidx_f[0:NE, 0:1], None, ALU.is_equal).then_inc(onehot_made, 1)
                    mu_in = mu[:, :, :].rearrange("p t (a c) -> p (t a) c", c=32).unsqueeze(2).broadcast_to([P, 4, 4, 32])
                    hi = mu4[:, 0, :, :].rearrange("p b (k c) -> p b k c", c=32)
                    lo = mu4[:, 1, :, :].rearrange("p b (k c) -> p b k c", c=32)
                    dve.tensor_copy(hi, mu_in).then_inc(mu4_made, 1)
                    dve.wait_ge(mu4_made, 1)
                    dve.tensor_tensor(lo, mu_in, hi.bitcast(F32), ALU.subtract).then_inc(mu4_made, 1)
                elif kind == "toe":
                    k = step[1]
                    if k == 0:
                        dve.wait_ge(skip_loaded, 16)
                    dve.wait_ge(toe_loaded[k], 16)
                    for h in range(4 * k, 4 * k + 4):
                        src = toe_raw[:, h, P:2 * P]
                        last = dve.scalar_tensor_tensor(out=toe[:, h, 0:P], in0=ident[:, :], scalar=skip_sb[:, h:h + 1],
                                                        in1=src[:, ::-1], op0=ALU.mult, op1=ALU.add)
                    last.then_inc(toe_diag, 1)
                elif kind == "stat":
                    _, which, k = step
                    rows = batches_of(which, k)
                    updates_of_x(dve, which, k)
                    for i, b in enumerate(rows):
                        last = dve.bn_stats(stats[:, i, :], x_res[:, b, :])
                    mine(last)
                    for i in range(len(rows)):
                        last = dve.bn_aggr(mv[:, i, :], stats[:, i, :])
                    last.then_inc(stats_done, 1)
                elif kind == "norm":
                    _, which, k = step
                    n = NORMS.index((which, k))
                    dst = xn if which in ("mix", "moe") else xn1
                    before = [m for m in NORMS[:n] if (m[0] in ("mix", "moe")) == (dst is xn)]
                    if before:
                        turned(dve, *before[-1])
                    if (which, k) == ("moe", 1):
                        wait_filled(dve, ("turn_soft", 0, 1))
                    dve.wait_ge(rstd_done, n + 1)
                    for i, b in enumerate(batches_of(which, k)):
                        dve.tensor_scalar(dst[:, i, :], x_res[:, b, :], mv[:, i, 0:1], rstd[:, i:i + 1],
                                          ALU.subtract, ALU.mult).then_inc(normed, 1)
                elif kind == "conv":
                    _, half, h = step
                    if h == 0:
                        for t in range(2):
                            wait_drained(dve, ("turn_q", half, t))
                    hn = half * HEADS + h
                    if hn >= 2:
                        dve.wait_ge(folded, hn - 1)
                    wait_filled(dve, step)
                    y = psum(step)
                    qb = h * 2 * Q * EXT
                    o = prod[:, h % 2]
                    drain(dve.tensor_tensor(o[:, :, 0:TAPS, :], view(y, 0, [[YW, 2 * Q], [SPAN, TAPS], [1, HD]]),
                                            view(q_ext, qb + 3, [[EXT, 2 * Q], [1, TAPS], [1, HD]]), ALU.mult), step)
                    drain(dve.tensor_tensor(o[:, :, TAPS:HD, :], view(y, SPAN - 1, [[YW, 2 * Q], [SPAN - 1, 3], [1, HD]]),
                                            view(q_ext, qb + 2, [[EXT, 2 * Q], [-1, 3], [1, HD]]), ALU.mult), step)
                elif kind == "gather":
                    _, half, g = step
                    n = group_no(half, g)
                    dve.wait_ge(folded, 2 * (n + 1))
                    if half == 1 and g == 0:
                        for p in range(2):
                            wait_filled(dve, ("turn_att", 0, p))
                    dve.tensor_reduce(att[:, :, 2 * g:2 * g + 2].rearrange("p n h j -> p h n j"),
                                      fold[:, n % 2].rearrange("p (h n) s j -> p h n j s", h=2), AXX,
                                      ALU.add).then_inc(gathered, 1)
                elif kind == "turn_att":
                    _, half, p = step
                    b0 = half * Q + 2 * p
                    if half == 0 and p == 0:
                        dve.wait_ge(tanh_done, 1)
                    dve.wait_ge(x_loaded[half], 16)
                    wait_filled(dve, step)
                    rows = x_res[:, b0:b0 + 2, :].rearrange("p b l -> p (b l)")
                    drain(dve.scalar_tensor_tensor(out=rows, in0=psum(step)[:, :], scalar=tg[:, 0:1], in1=rows,
                                                   op0=ALU.mult, op1=ALU.add), step)
                elif kind == "turn_router":
                    residue(router_t[:, :, 1, :], step, psum(step)[:, 0:2 * NE].rearrange("p (t e) -> p t e", t=2),
                            router_t[:, :, 0, :])
                elif kind == "turn_w":
                    _, which, p = step
                    n = P * len(range(2 * p, min(2 * p + 2, TILES)))
                    cols = slice(2 * p * P, 2 * p * P + n)
                    w = WORDS[which]
                    residue(w_split[:, w, :, 1, cols], step, psum(step)[:, 0:2 * n].rearrange("p (t c) -> p t c", t=2),
                            w_split[:, w, :, 0, cols])
                elif kind == "turn_down":
                    p = step[1]
                    n = len(range(2 * p, min(2 * p + 2, TILES)))
                    residue(d_split[:, 2 * p:2 * p + n, 1, :], step,
                            psum(step)[:, 0:n * L].rearrange("p (r c) -> p r c", c=L), d_split[:, 2 * p:2 * p + n, 0, :])
                elif kind == "mask_up":
                    _, which, c = step
                    k = WORDS[which] * NCH + c
                    wait_drained(dve, step, 2)
                    for i in range(2):
                        cols = slice(i * NI, (i + 1) * NI)
                        g = 2 * (c % 2) + i
                        drain(dve.scalar_tensor_tensor(
                            out=m_stack[:, WORDS[which], c * CW + i * NI:c * CW + (i + 1) * NI], in0=psum(step)[:, cols],
                            scalar=ind[:, 0, g:g + 1], in1=half_m[:, k % 2, cols].bitcast(F32), op0=ALU.mult,
                            op1=ALU.subtract), step)
                elif kind == "tern_sum":
                    name = step[1]
                    k = 0 if name == "fc" else 1
                    n = RING_LOADS.index(name)
                    w = ring[n % 3][:, 0:2 * NJ]
                    dve.wait_ge(ring_loaded[n % 3], 16 * (n // 3 + 1))
                    dve.tensor_reduce(tern[:, k, 0:1], w, AXX, ALU.add, apply_absolute_value=True).then_inc(tern_abs, 1)
                    wait_filled(dve, step)
                    drain(dve.tensor_scalar(tern[:, k, 1:2], psum(step)[:, 0:1], 1.0 / (NJ * L), 1e-5, ALU.mult, ALU.max),
                          step)
                    wait_drained(dve, step)
                    dve.tensor_scalar(tern[:, k, 2:3], tern[:, k, 1:2], 0.7, None, ALU.mult)
                    mine(dve.tensor_scalar(tern[:, k, 3:4], tern[:, k, 1:2], -0.7, None, ALU.mult))
                    mine(dve.tensor_scalar(tern_tmp[:, :], w, tern[:, k, 3:4], None, ALU.is_lt))
                    dve.scalar_tensor_tensor(out=w, in0=w, scalar=tern[:, k, 2:3], in1=tern_tmp[:, :], op0=ALU.is_gt,
                                             op1=ALU.subtract).then_inc(tern_made, 1)
                    if k == 1:
                        dve.wait_ge(tanh_done, 1)
                        mine(dve.tensor_tensor(out_scale[:, 0:1], tern[:, 0, 1:2], tern[:, 0, 1:2], ALU.mult))
                        mine(dve.tensor_tensor(out_scale[:, 1:2], out_scale[:, 0:1], tern[:, 1, 1:2], ALU.mult))
                        mine(dve.tensor_tensor(out_scale[:, 2:3], out_scale[:, 1:2], tg[:, 3:4], ALU.mult))
                elif kind == "turn_x":
                    _, half, t = step
                    residue(xt[half][:, t, 1, :], step, psum(step)[:, :], xt[half][:, t, 0, :])
                elif kind == "turn_1":
                    residue(x1t[:, 1].rearrange("p t n -> p (t n)"), step, psum(step)[:, :],
                            x1t[:, 0].rearrange("p t n -> p (t n)"))
                elif kind == "logits":
                    half = step[1]
                    if half == 0:
                        wait_filled(dve, ("turn_proj", 2))
                    else:
                        mixer_free(dve)
                    rt = rts[half]
                    wait_filled(dve, step)
                    z = psum(step)[:, 0:Q * NE].rearrange("p (q e) -> p q e", q=Q)
                    drain(dve.tensor_reduce(nmax[:, :], z, AXX, ALU.max, negate=True), step)
                    wait_drained(dve, step, 1)
                    r0 = rt[0][:, :].rearrange("p (q e) -> p q e", q=Q)
                    drain(dve.tensor_tensor(r0, z, nmax[:, :].unsqueeze(2).broadcast_to([P, Q, NE]), ALU.add), step)
                    wait_drained(dve, step)
                    dve.nop().then_inc(shifted, 1)
                elif kind == "top":
                    half = step[1]
                    rt = rts[half]
                    v = [r[:, :].rearrange("p (q e) -> p q e", q=Q) for r in rt]
                    dve.wait_ge(router_exp, half + 1)
                    mine(dve.tensor_reduce(rsum[:, 0, :], v[0], AXX, ALU.add))
                    mine(dve.reciprocal(rsum[:, 1, :], rsum[:, 0, :]))
                    mine(dve.tensor_tensor(v[1], v[0], rsum[:, 1, :].unsqueeze(2).broadcast_to([P, Q, NE]), ALU.mult))
                    for q in range(Q):
                        last = dve.max(top8[:, q, :], v[1][:, q, :])
                    mine(last)
                    for q in range(Q):
                        last = dve.match_replace(v[2][:, q, :], top8[:, q, :], v[1][:, q, :], 0.0)
                    mine(last)
                    dve.tensor_tensor(rt[3][:, :], rt[1][:, :], rt[2][:, :], ALU.subtract).then_inc(chosen, 1)
                elif kind == "flat":
                    half = step[1]
                    rt = rts[half]
                    wait_filled(dve, step)
                    f = psum(step)[:, 0:Q * NE]
                    f3 = f.rearrange("p (n s) -> p n s", s=GS)
                    dst = scal[:, half * Q:(half + 1) * Q, :].rearrange("p q g -> p (q g)")
                    drain(dve.tensor_reduce(dst, f3, AXX, ALU.add), step)
                    drain(dve.tensor_scalar(rt[0][:, :], f, 0.0, -1e9, ALU.is_equal, ALU.mult), step)
                    wait_drained(dve, step, 2)
                    drain(dve.tensor_tensor(rt[2][:, :], f, rt[0][:, :], ALU.add), step)
                    wait_drained(dve, step)
                    v2 = rt[2][:, :].rearrange("p (n s) -> p n s", s=GS)
                    v1 = rt[1][:, :].rearrange("p (n s) -> p n s", s=GS)
                    mine(dve.tensor_reduce(gmax[:, 0, :], v2, AXX, ALU.max))
                    dve.tensor_tensor(v1, v2, gmax[:, 0, :].unsqueeze(2).broadcast_to([P, Q * NG, GS]),
                                      ALU.subtract).then_inc(soft_shifted, 1)
                elif kind == "soft":
                    half = step[1]
                    rt = rts[half]
                    v1 = rt[1][:, :].rearrange("p (n s) -> p n s", s=GS)
                    v0 = rt[0][:, :].rearrange("p (n s) -> p n s", s=GS)
                    dve.wait_ge(soft_exp, half + 1)
                    mine(dve.tensor_reduce(gmax[:, 1, :], v1, AXX, ALU.add))
                    mine(dve.reciprocal(gmax[:, 2, :], gmax[:, 1, :]))
                    mine(dve.tensor_tensor(v0, v1, gmax[:, 2, :].unsqueeze(2).broadcast_to([P, Q * NG, GS]), ALU.mult))
                    src = rt[0][:, :].rearrange("p (n c) -> p n c", c=32).unsqueeze(2).broadcast_to([P, 2 * Q, 2, 32])
                    for t in range(2):
                        wait_filled(dve, ("turn_x", half, t))
                    mine(dve.tensor_copy(soft_parts[:, :, 0:2, :].bitcast(F32R), src))
                    dve.tensor_tensor(soft_parts[:, :, 2:4, :].bitcast(F32R), src, soft_parts[:, :, 0:2, :],
                                      ALU.subtract).then_inc(soft_made, 1)
                elif kind == "chunk":
                    _, b, c = step
                    n = b * NCH + c
                    if n == 0:
                        wait_filled(dve, ("turn_top", 0))
                    if b:
                        wait_filled(dve, ("turn_a", b - 1, min(c + 1, NCH - 1)))
                    wait_drained(dve, ("gate", b, c))
                    wait_filled(dve, ("up", b, c))
                    for i in range(2):
                        cols = slice(i * NI, (i + 1) * NI)
                        g = 2 * c + i
                        drain(dve.scalar_tensor_tensor(out=act[:, g * NI:(g + 1) * NI], in0=silu[:, n % 2, cols],
                                                       scalar=scal[:, b, g:g + 1], in1=psum(("up", b, c))[:, cols],
                                                       op0=ALU.mult, op1=ALU.mult), ("up", b, c))
                elif kind == "turn_a":
                    _, b, c = step
                    r = DONE_TILES[c]
                    residue(a_t[:, r.start:r.stop, 1, :], step,
                            psum(step)[:, 0:len(r) * P].rearrange("p (r n) -> p r n", n=P), a_t[:, r.start:r.stop, 0, :])
                elif kind == "down":
                    b = step[1]
                    wait_filled(dve, step)
                    drain(dve.scalar_tensor_tensor(out=x_res[:, b, :], in0=psum(step)[:, 0:L], scalar=tg[:, 2:3],
                                                   in1=x_res[:, b, :], op0=ALU.mult, op1=ALU.add), step)
                elif kind == "scores":
                    u = step[1]
                    if u == 0:
                        dve.wait_ge(mask_loaded, 16)
                        mixer_free(dve)
                        mine(dve.tensor_reduce(valid[:, 0, :], mask_sb.rearrange("p (b m) -> p b m", b=B), AXX, ALU.max))
                        dve.tensor_scalar(valid[:, 1, :], valid[:, 0, :], tg[:, 1:2], None, ALU.mult)
                        mine(dve.tensor_scalar(neg[:, :], mask_sb, -1.0, 1e30, ALU.add, ALU.mult))
                    else:
                        wait_filled(dve, ("turn_p", u - 1))
                    wait_filled(dve, step)
                    s2 = s_att[:, :, :].rearrange("p k m -> p (k m)")
                    drain(dve.scalar_tensor_tensor(out=s2, in0=psum(step)[:, 0:2 * P], scalar=1.0 / float(np.sqrt(L)),
                                                   in1=neg[:, 2 * u * P:(2 * u + 2) * P], op0=ALU.mult, op1=ALU.add),
                          step)
                    wait_drained(dve, step)
                    dve.tensor_reduce(nmax1[:, :], s_att[:, :, :], AXX, ALU.max, negate=True).then_inc(s_shifted, 1)
                elif kind == "read":
                    u = step[1]
                    dve.wait_ge(s_exp, 2 * (u + 1))
                    mine(dve.reciprocal(rv[:, 0, :], esum[:, :]))
                    mine(dve.tensor_tensor(rv[:, 1, :], rv[:, 0, :], valid[:, 1, 2 * u:2 * u + 2], ALU.mult))
                    wait_filled(dve, step)
                    for k in range(2):
                        b = 2 * u + k
                        drain(dve.scalar_tensor_tensor(out=x_res[:, b, :], in0=psum(step)[:, k * L:(k + 1) * L],
                                                       scalar=rv[:, 1, k:k + 1], in1=x_res[:, b, :], op0=ALU.mult,
                                                       op1=ALU.add), step)
                elif kind == "hidden":
                    _, u, jp = step
                    n = HIDDEN.index((u, jp))

                    def hidden_lo(m):
                        mj = HIDDEN[m][1]
                        tiles = range(2 * mj, min(2 * mj + 2, JT))
                        sq = hsq[:, m % 2, 0:2 * P * len(tiles)].rearrange("p (j c) -> p j c", c=2 * P)
                        dve.wait_ge(hid_hi, m + 1)
                        dve.tensor_tensor(hid_t[:, tiles.start:tiles.stop, 1, :], sq,
                                          hid_t[:, tiles.start:tiles.stop, 0, :].bitcast(F32),
                                          ALU.subtract).then_inc(hid_lo, 1)

                    w = 2 * P * len(range(2 * jp, min(2 * jp + 2, JT)))
                    wait_drained(dve, step)
                    if n >= 2:
                        dve.wait_ge(hid_lo, n - 1)
                        dve.wait_ge(hid_hi, n - 1)
                    dve.tensor_tensor(hsq[:, n % 2, 0:w], relu[:, n % 2, 0:w], relu[:, n % 2, 0:w],
                                      ALU.mult).then_inc(sq_done, 1)
                    if jp:
                        hidden_lo(n - 1)
                    if jp == 2:
                        hidden_lo(n)
                elif kind == "out":
                    u = step[1]
                    rows = x_res[:, 2 * u:2 * u + 2, :].rearrange("p b l -> p (b l)")
                    wait_filled(dve, step)
                    drain(dve.scalar_tensor_tensor(out=rows, in0=psum(step)[:, :], scalar=out_scale[:, 2:3], in1=rows,
                                                   op0=ALU.mult, op1=ALU.add), step)

        @block.gpsimd
        def _(pool):
            pool.memset(ones[:, :], 1.0).then_inc(consts_made, 1)
            pool.iota(pidx[:, 0:1], pattern=[[0, 1]], base=0, channel_multiplier=1)
            pool.memset(mhalf[:, :], -0.5)
            pool.wait_ge(consts_made, 1)
            pool.affine_select(out=ident[:, :], in_=ones[:, :], compare_op=ALU.is_equal, fill=0.0, base=0,
                               pattern=[[1, P]], channel_multiplier=-1).then_inc(consts_made, 1)
            pool.wait_ge(consts_made, 2)
            pool.nop().then_inc(consts_made, 2)
            for step in SCHEDULE:
                kind = step[0]
                if kind == "stat":
                    n = NORMS.index(step[1:])
                    rows = len(batches_of(*step[1:]))
                    pool.wait_ge(stats_done, n + 1)
                    pool.tensor_scalar(ve[:, 0:rows], mv[:, 0:rows, 1], EPS, None, ALU.add).then_inc(pool_own, 1)
                    pool.wait_ge(pool_own, n + 1)
                    if n:
                        pool.wait_ge(normed, rows_normed(*NORMS[n - 1]))
                    pool.tensor_tensor(rstd[:, 0:rows], ve[:, 0:rows], mhalf[:, 0:rows], ALU.pow).then_inc(rstd_done, 1)
                elif kind == "kv":
                    _, half, g = step
                    n = group_no(half, g)
                    if g == 0:
                        for t in range(2):
                            wait_drained(pool, ("turn_ctx", half, t))
                    if n >= 2:
                        hf, gg = divmod(n - 2, HEADS // 2)
                        for h in (2 * gg, 2 * gg + 1):
                            wait_filled(pool, ("conv", hf, h))
                    base = (half * HEADS + 2 * g) * 2 * Q * EXT
                    pool.tensor_tensor(kv[:, n % 2], view(ctx_ext, base, [[EXT, 4 * Q], [0, TAPS], [1, SPAN]]),
                                       view(ctx_ext, base, [[EXT, 4 * Q], [1, TAPS], [1, SPAN]]),
                                       ALU.mult).then_inc(kv_made, 1)
                elif kind == "fold":
                    _, half, h = step
                    n = group_no(half, h // 2)
                    wait_drained(pool, ("conv", half, h))
                    if h % 2 == 0 and n >= 2:
                        pool.wait_ge(gathered, n - 1)
                    p4 = prod[:, h % 2].rearrange("p n s j -> p n (s j)")
                    f = fold[:, n % 2, 2 * Q * (h % 2):2 * Q * (h % 2 + 1)].rearrange("p n s j -> p n (s j)")
                    pool.tensor_tensor(f, p4[:, :, 0:32], p4[:, :, 32:64], ALU.add).then_inc(folded, 1)


def kernel(**inputs):
    import concourse.bacc as bacc
    from concourse.bass_utils import run_bass_kernel_spmd as run

    a = {k: np.ascontiguousarray(v) for k, v in inputs.items()}
    rev = np.zeros((HEADS, KPAD), np.float32)
    rev[:, 0:L] = a["L0_xattn_ssm_kernel"][:, ::-1]
    arrays = {
        "x": a["x"], "ctx_rows": a["ctx_2048"], "mask": a["mask_BxS2_bk0"].view(np.int32), "g_xattn": a["g_xattn"],
        "g_ffn": a["g_ffn"], "kernel_rev": rev, "skip": a["L0_xattn_D"], "gate_w": a["L0_ffn_gate_w"],
        "mask_up_w": a["L0_ffn_mask_up_w"], "gate_p": a["L0_ffn_gate_proj_w"], "up_p": a["L0_ffn_up_proj_w"],
        "down_p": a["L0_ffn_down_proj_w"], "inv_map": a["L0_ffn_inv_map"], "w_fc": a["L1_ffn_w_fc"],
        "w_proj": a["L1_ffn_w_proj"],
    }
    nc = bacc.Bacc("TRN2", target_bir_lowering=False, num_devices=1)
    args = {n: nc.dram_tensor(f"in_{n}", v.shape, mybir.dt.from_np(v.dtype), kind="ExternalInput").ap()
            for n, v in arrays.items()}
    out = nc.dram_tensor("out_x", (B, P, L), F32, kind="ExternalOutput").ap()
    build(nc, out=out, **args)
    r = run(nc, [{f"in_{n}": v for n, v in arrays.items()}], core_ids=[0])
    return r.results[0]["out_x"]
```

```python
import numpy as np
import concourse.bass as bass
from concourse import mybir

F32, F32R, I32, U8 = mybir.dt.float32, mybir.dt.float32r, mybir.dt.int32, mybir.dt.uint8
ALU, ACT, AXX = mybir.AluOpType, mybir.ActivationFunctionType, mybir.AxisListType.X

P = 128
B, L = 8, 256
HEADS, HD = 16, 8
Q = 4
NE, NG, GS = 64, 8, 8
NI = 176
GI = NG * NI
TILES = GI // P
CW = 2 * NI
NCH = GI // CW
NJ = 640
JT = NJ // P
TAPS = 5
SPAN = 11
YW = TAPS * SPAN - 3
EXT = 15
KPAD = 384
EPS = 1e-5
DONE_TILES = [range(0, 2), range(2, 5), range(5, 8), range(8, 11)]
WORDS = {"gate": 0, "up": 1}
TERNARY = ["fc", "proj"]
UNITS = [range(0, 2), range(2, 4), range(4, 6), range(6, 7), range(7, 8)]

RING_LOADS = ["gate0", "gate1", "gate2", "up0", "up1", "up2", "down0", "down1"]
RING_LAST = {"gate0": ("turn_w", "gate", 1), "gate1": ("turn_w", "gate", 3), "gate2": ("turn_w", "gate", 5),
             "up0": ("turn_w", "up", 1), "up1": ("turn_w", "up", 3), "up2": ("turn_w", "up", 5),
             "down0": ("turn_down", 5), "down1": ("turn_down", 5)}


WEIGHT_STEPS_AFTER = [0, 0, 0, 0, 1, 1, 2, 2, 1, 2, 2, 0, 1, 3, 1, 2, 1, 2, 2, 2, 2]
HEADS_AFTER = [1, 3, 0, 1, 2, 1, 2, 2, 0]
HEADS_AT = [1, 2, 2, 3]
ATT_AT = [5, 6]
ROUTER_AT = [7, 9, 11, 13, 13, 15, 16, 17, 19]
MASK_AT = [9]
TERNARY_AT = [11, 14, 15, 16, 19, 20, 23, 23, 24, 25, 26, 27, 29, 30]
LAYER1_AT = [[20, 22, 24, 25, 27, 28, 31, 33, 34, 35, 36, 38],
             [35, 37, 38, 41, 43, 44, 46, 48, 49, 50, 51, 53],
             [49, 51, 53, 55, 56, 57, 59, 61, 63, 64, 65, 67],
             [61, 63, 65, 66, 67, 70, 71, 72, 75, 76, 77, 79],
             [66, 68, 70, 70, 73, 74, 76, 78, 79, 80, 82, 84]]


def make_schedule():
    w_steps = [("turn_w", "gate", p) for p in range(6)] + [("turn_w", "up", p) for p in range(6)] + [("turn_router",)]
    w_steps += [("mask_up", w, c) for w in ("gate", "up") for c in range(NCH)]
    w_steps += [("turn_down", p) for p in range(6)]
    assert sum(WEIGHT_STEPS_AFTER) == len(w_steps)

    def conv_head(half, h):
        out = [("conv", half, h), ("fold", half, h)]
        g = h // 2
        if h % 2:
            if g + 2 < HEADS // 2:
                out.append(("kv", half, g + 2))
            if g >= 1:
                out.append(("gather", half, g - 1))
        return out

    def router(half):
        return [[("stat", "moe", half)], [("norm", "moe", half)], [("turn_x", half, 0), ("turn_x", half, 1)],
                [("logits", half)], [("top", half)], [("turn_top", half)], [("flat", half)], [("soft", half)],
                [("turn_soft", half, 0), ("turn_soft", half, 1)]]

    def layer1(u):
        return [[("stat", "cross", u)], [("norm", "cross", u)], [("turn_0", u)], [("scores", u)], [("turn_p", u)],
                [("read", u), ("stat", "mlp", u)], [("norm", "mlp", u)], [("turn_1", u)],
                [("hidden", u, 0)], [("hidden", u, 1)], [("hidden", u, 2)], [("out", u)]]

    s = [("warm", 9), ("turn_ctx", 0, 0), ("turn_ctx", 0, 1), ("stat", "mix", 0), ("kv", 0, 0), ("norm", "mix", 0),
         ("warm", 22), ("turn_q", 0, 0), ("turn_q", 0, 1), ("kv", 0, 1), ("warm", 10)]
    pieces = []
    for h in range(HEADS):
        step = [("toe", h)] if h < 4 else []
        step += conv_head(0, h)
        if h == 4:
            step += [("consts",)]
        if h == 9:
            step += [("turn_ctx", 1, 0), ("turn_ctx", 1, 1)]
        if h == 14:
            step += [("stat", "mix", 1)]
        pieces.append(step)
    pieces += [[("norm", "mix", 1), ("gather", 0, HEADS // 2 - 1)], [("turn_q", 1, 0), ("turn_q", 1, 1)],
               [("turn_att", 0, 0), ("turn_att", 0, 1)], [("kv", 1, 0), ("stat", "moe", 0)], [("kv", 1, 1)]]
    for piece, n in zip(pieces, WEIGHT_STEPS_AFTER):
        s += piece + w_steps[:n]
        w_steps = w_steps[n:]

    h = 0
    for piece, n in zip(router(0)[1:] + [[]], HEADS_AFTER):
        s += piece
        for h in range(h, h + n):
            s += conv_head(1, h)
        h += n > 0
    assert h + len(HEADS_AT) * 1 == HEADS, h

    places = {}

    def place(where, pieces):
        for k, steps in zip(where, pieces, strict=True):
            places[k] = places.get(k, []) + steps

    place(HEADS_AT, [conv_head(1, k) for k in range(HEADS - len(HEADS_AT), HEADS)])
    place(ATT_AT, [[("gather", 1, HEADS // 2 - 1)], [("turn_att", 1, 0), ("turn_att", 1, 1)]])
    place(ROUTER_AT, router(1))
    place(TERNARY_AT, [[("tern_abs", "fc")], [("tern_abs", "proj")], [("tern_sum", "fc")], [("tern_sum", "proj")]] +
          [[("tern_sign", name, part)] for name in TERNARY for part in range(2)] +
          [[("turn_fc", p)] for p in range(3)] + [[("turn_proj", p)] for p in range(3)])
    place(MASK_AT, [[("mask",)]])
    for u, where in enumerate(LAYER1_AT):
        place(where, layer1(u))
    late = []
    for k in range(B * NCH):
        b, c = k // NCH, k % NCH
        s.append(("chunk", b, c))
        s += places.pop(2 * k, [])
        s += late
        s += places.pop(2 * k + 1, [])
        late = [("turn_a", b, c)] + ([("down", b)] if c == NCH - 1 else [])
    s += late
    for k in sorted(places):
        s += places[k]
    return s


SCHEDULE = make_schedule()
G0, U0, G1, U1, Y0, Y1, TR, DN = range(8)


def plan_psum():
    early = [G0, U0, G1, U1, TR]
    late = [TR, DN]
    mixed = [Y0, Y1]
    n_early = n_late = n_mixed = 0
    uses, n_use, n_read = {}, [0] * 8, [0] * 8
    first_chunk = SCHEDULE.index(("chunk", 0, 0))
    conv_end = SCHEDULE.index(("gather", 1, HEADS // 2 - 1))
    tail = SCHEDULE.index(("down", B - 1))
    conv = 0

    def use(key, bank, reads):
        uses[key] = (bank, n_use[bank], n_read[bank], reads)
        n_use[bank] += 1
        n_read[bank] += reads

    reads = {"turn_ctx": 3, "turn_q": 3, "turn_router": 2, "turn_w": 2, "mask_up": 4, "turn_down": 2, "tern_sum": 1,
             "turn_fc": 1, "turn_proj": 1, "turn_att": 1, "turn_x": 2, "logits": 2, "turn_top": 1, "flat": 3,
             "turn_soft": 1, "turn_0": 1, "turn_1": 2, "scores": 1, "turn_p": 1, "read": 1, "hidden": 1, "out": 1}
    for i, step in enumerate(SCHEDULE):
        kind = step[0]
        if kind == "read":
            reads[kind] = len(UNITS[step[1]])
        if kind == "conv":
            use(step, [Y0, Y1][conv % 2], 2)
            conv += 1
        elif kind == "chunk":
            k = (step[1] * NCH + step[2]) % 2
            use(("gate",) + step[1:], [G0, G1][k], 1)
            use(("up",) + step[1:], [U0, U1][k], 2)
        elif kind == "turn_a":
            use(step, TR, 2)
        elif kind == "down":
            use(step, DN, 1)
        elif kind in reads:
            n = reads[kind]
            if i < first_chunk or i > tail:
                use(step, early[n_early % len(early)], n)
                n_early += 1
            elif i < conv_end:
                use(step, late[n_late % 2], n)
                n_late += 1
            else:
                use(step, mixed[n_mixed % 2], n)
                n_mixed += 1
    return uses


USES = plan_psum()
NORMS = [s[1:] for s in SCHEDULE if s[0] == "stat"]
assert NORMS == [s[1:] for s in SCHEDULE if s[0] == "norm"]


def batches_of(which, k):
    return range(k * Q, (k + 1) * Q) if which in ("mix", "moe") else UNITS[k]


def rows_normed(which, k):
    return sum(len(batches_of(*m)) for m in NORMS[:NORMS.index((which, k)) + 1])


HIDDEN = [(u, j) for _, u, j in (s for s in SCHEDULE if s[0] == "hidden")]


def build(nc, x, ctx_rows, mask, g_xattn, g_ffn, kernel_rev, skip, gate_w, mask_up_w, gate_p, up_p, down_p, inv_map,
          w_fc, w_proj, out):
    at = [((nc.sbuf_base + 31) // 32) * 32]

    def region(size):
        start = at[0]
        at[0] += -(-size // 32) * 32
        assert at[0] <= nc.sbuf_usable_end, at[0] - nc.sbuf_usable_end
        return start

    def sb(name, shape, dt=F32, offset=None):
        size = int(np.prod(shape[1:])) * (1 if dt == U8 else 4)
        return nc.alloc_sbuf_tensor_at(name, shape, dt, offset=region(size) if offset is None else offset)

    x_res = sb("x_res", [P, B, L])
    ctx = sb("ctx", [P, B, L])
    ctx_ext = sb("ctx_ext", [P, 2, HEADS, 2, Q, EXT])
    w_split = sb("w_split", [P, 2, 2, 2, GI], F32R)
    toe_raw = nc.alloc_sbuf_tensor_at("toe_raw", [P, HEADS, 256], F32, offset=at[0] - 4 * 8 * GI)
    d_split = sb("d_split", [P, TILES, 2, L], F32R)
    m_stack = sb("m_stack", [P, 2, GI], F32R)
    fc_t = sb("fc_t", [P, 2, NJ], F32R)
    proj_t = sb("proj_t", [P, JT, L], F32R)
    xt_at = region(4 * 2 * 2 * 512)
    xt = [sb("xt0", [P, 2, 2, 512], F32R, xt_at)]
    half_m = sb("half_m", [P, 2, CW], F32R, xt_at)
    soft_at = region(4 * 2 * 512)
    soft_t = [sb("soft_t0", [P, 2, 512], F32R, soft_at)]
    mu4 = sb("mu4", [P, 2, 4, 4 * 32], F32R, soft_at)
    ring_at = region(4 * TILES * 2 * P)
    a_t = sb("a_t", [P, TILES, 2, P], F32R, ring_at)
    a_at = region(4 * GI)
    act = sb("act", [P, GI], F32, a_at)
    silu_at = region(4 * 2 * CW)
    silu = sb("silu", [P, 2, CW], F32, silu_at)
    ring = [sb(f"ring{k}", [P, GI], F32, ring_at + 4 * GI * k) for k in range(3)]
    assert ring_at + 12 * GI <= silu_at + 4 * 2 * CW
    rts = [[sb(f"rt0_{k}", [P, Q * NE], F32, a_at + 4 * Q * NE * k) for k in range(4)]]
    top_t = [sb("top_t0", [NE, 512], F32, silu_at)]
    xn_at = region(4 * Q * L)
    xn = sb("xn", [P, Q, L], F32, xn_at)
    soft_parts = sb("soft_parts", [P, Q * 2, 4, 32], F32, xn_at)
    xn1 = sb("xn1", [P, 2, L])
    mixer_at = at[0]
    toe = sb("toe", [P, HEADS, 256])
    q_ext = sb("q_ext", [P, HEADS, 2 * Q, EXT])
    kv = sb("kv", [P, 2, 4 * Q, TAPS, SPAN])
    prod = sb("prod", [P, 2, 2 * Q, HD, HD])
    fold = sb("fold", [P, 2, 4 * Q, 4, HD])
    att = sb("att", [P, 2 * Q, HEADS, HD])
    mixer_end = at[0]
    at[0] = mixer_at
    xt.append(sb("xt1", [P, 2, 2, 512], F32R))
    soft_t.append(sb("soft_t1", [P, 2, 512], F32R))
    hid_at = region(4 * JT * 4 * P)
    hid_t = sb("hid_t", [P, JT, 2, 2 * P], F32R, hid_at)
    tern_w = sb("tern_w", [P, 2, 2 * NJ], F32, hid_at)
    x1t = sb("x1t", [P, 2, 2, 2 * P], F32R)
    qt = sb("qt", [P, 2, 2 * P])
    neg = sb("neg", [P, B * P])
    s_att = sb("s_att", [P, 2, P])
    pt = sb("pt", [P, 2 * P])
    relu_at = region(4 * (4 * Q * NE + 512))
    relu = sb("relu", [P, 2, 512], F32, relu_at)
    hsq = sb("hsq", [P, 512], F32, relu_at + 4 * 2 * 512)
    rts.append([sb(f"rt1_{k}", [P, Q * NE], F32, relu_at + 4 * Q * NE * k) for k in range(4)])
    top_t.append(sb("top_t1", [NE, 512], F32, relu_at + 16 * Q * NE))
    assert at[0] <= mixer_end, at[0] - mixer_end
    at[0] = mixer_end
    mask_words = sb("mask_words", [P, B * P // 4], I32)
    mask_sb = mask_words[:, :].bitcast(U8)
    tern_tmp = sb("tern_tmp", [P, NJ])
    ident = sb("ident", [P, P])
    ones = sb("ones", [P, P])
    router_w = sb("router_w", [NE, L])
    router_t = sb("router_t", [P, 2, 2, NE], F32R)
    mu = sb("mu", [P, 2, NE])
    onehot = sb("onehot", [NE, NE])
    inv_i = sb("inv_i", [NE, NE], I32)
    inv_f = sb("inv_f", [NE, 2, NE])
    skip_sb = sb("skip_sb", [P, HEADS])
    gates = sb("gates", [P, 4])
    tg = sb("tg", [P, 4])
    pidx = sb("pidx", [P, 3], I32)
    pidx_f = sb("pidx_f", [P, 3])
    ind = sb("ind", [P, 2, 4])
    stats = sb("stats", [P, Q, 6])
    mv = sb("mv", [P, Q, 2])
    ve = sb("ve", [P, Q])
    rstd = sb("rstd", [P, Q])
    mhalf = sb("mhalf", [P, Q])
    nmax = sb("nmax", [P, Q])
    nmax1 = sb("nmax1", [P, 2])
    rsum = sb("rsum", [P, 2, Q])
    top8 = sb("top8", [P, Q, 8])
    scal = sb("scal", [P, B, NG])
    gmax = sb("gmax", [P, 3, Q * NG])
    tern = sb("tern", [P, 2, 6])
    out_scale = sb("out_scale", [P, 3])
    valid = sb("valid", [P, 2, B])
    esum = sb("esum", [P, 2])
    rv = sb("rv", [P, 2, 2])

    banks = [nc.alloc_psum_tensor(f"bank{k}", [P, 512], F32) for k in range(8)]
    filled = [nc.alloc_semaphore(f"filled{k}") for k in range(8)]
    drained = [nc.alloc_semaphore(f"drained{k}") for k in range(8)]
    sem = nc.alloc_semaphore
    x_loaded = [sem("x_loaded0"), sem("x_loaded1")]
    ctx_loaded = [sem("ctx_loaded0"), sem("ctx_loaded1")]
    toe_loaded = [sem(f"toe_loaded{k}") for k in range(4)]
    skip_loaded = sem("skip_loaded")
    small_loaded, mask_loaded = sem("small_loaded"), sem("mask_loaded")
    tern_loaded = [sem("tern_loaded0"), sem("tern_loaded1")]
    ring_loaded = [sem(f"ring_loaded{k}") for k in range(3)]
    consts_made = sem("consts_made")
    toe_diag, toe_off = sem("toe_diag"), sem("toe_off")
    tanh_done = sem("tanh_done")
    mu4_made, onehot_made, ind_made = sem("mu4_made"), sem("onehot_made"), sem("ind_made")
    kv_made = sem("kv_made")
    folded, gathered = sem("folded"), sem("gathered")
    stats_done, rstd_done, normed = sem("stats_done"), sem("rstd_done"), sem("normed")
    shifted, router_exp, chosen = sem("shifted"), sem("router_exp"), sem("chosen")
    soft_shifted, soft_exp, soft_made = sem("soft_shifted"), sem("soft_exp"), sem("soft_made")
    tern_abs, tern_thr, tern_low, tern_made = sem("tern_abs"), sem("tern_thr"), sem("tern_low"), sem("tern_made")
    s_shifted, s_exp = sem("s_shifted"), sem("s_exp")
    hid_hi, hid_lo = sem("hid_hi"), sem("hid_lo")
    dve_own, pool_own = sem("dve_own"), sem("pool_own")
    stored = sem("stored")

    def psum(key):
        return banks[USES[key][0]]

    def claim(eng, key):
        bank, _, before, _ = USES[key]
        if before:
            eng.wait_ge(drained[bank], before)

    def fill(ins, key):
        ins.then_inc(filled[USES[key][0]], 1)

    def wait_filled(eng, key):
        bank, n, _, _ = USES[key]
        eng.wait_ge(filled[bank], n + 1)

    def wait_drained(eng, key, reads=None):
        bank, _, before, n = USES[key]
        eng.wait_ge(drained[bank], before + (n if reads is None else reads))

    def drain(ins, key):
        ins.then_inc(drained[USES[key][0]], 1)

    def group_no(half, g):
        return half * (HEADS // 2) + g

    def view(t, offset, dims):
        whole = t[:]
        return bass.AP(whole.tensor, whole.offset + offset, [list(whole.ap[0])] + [list(d) for d in dims])

    def updates_of_x(eng, which, k):
        if which == "mix":
            eng.wait_ge(x_loaded[k], 16)
        elif which == "moe":
            for p in range(2):
                wait_drained(eng, ("turn_att", k, p))
        elif which == "cross":
            for b in batches_of(which, k):
                wait_drained(eng, ("down", b))
        else:
            wait_drained(eng, ("read", k))

    def turned(eng, which, k):
        if which in ("mix", "moe"):
            for t in range(2):
                wait_filled(eng, ("turn_q" if which == "mix" else "turn_x", k, t))
        else:
            wait_filled(eng, ("turn_0" if which == "cross" else "turn_1", k))

    def mixer_free(eng):
        eng.wait_ge(gathered, HEADS)
        for h in (HEADS - 2, HEADS - 1):
            wait_filled(eng, ("conv", 1, h))
        for p in range(2):
            wait_filled(eng, ("turn_att", 1, p))

    block = nc.Block()
    with block:
        @block.sync
        def _(sp):
            def rows_of(src, half):
                return src[half * Q:(half + 1) * Q].rearrange("b p l -> p b l")

            def ring_load(n):
                name = RING_LOADS[n]
                if n >= 3:
                    wait_filled(sp, RING_LAST[RING_LOADS[n - 3]])
                slot = ring[n % 3]
                if name[:-1] in ("gate", "up"):
                    src = (gate_p if name[0] == "g" else up_p).rearrange("g i h -> (g i) h")
                    r0 = 4 * int(name[-1])
                    n_t = min(4, TILES - r0)
                    src = src[r0 * P:(r0 + n_t) * P, :].rearrange("(r p) h -> p r h", p=P)
                    dst = slot[:, 0:n_t * L].rearrange("p (r h) -> p r h", h=L)
                else:
                    kt = int(name[-1])
                    src = down_p[:, kt * P:(kt + 1) * P, :].rearrange("g h i -> h g i")
                    dst = slot[:, :].rearrange("p (g i) -> p g i", i=NI)
                sp.dma_start(dst, src).then_inc(ring_loaded[n % 3], 16)

            sp.dma_start(ctx[:, 0:Q, :], rows_of(ctx_rows, 0)).then_inc(ctx_loaded[0], 16)
            sp.dma_start(x_res[:, 0:Q, :], rows_of(x, 0)).then_inc(x_loaded[0], 16)
            sp.dma_start(skip_sb[:, :], skip.partition_broadcast(P)).then_inc(skip_loaded, 16)
            for k in range(4):
                src = bass.AP(kernel_rev.tensor, k * 4 * KPAD, [[1, P], [KPAD, 4], [1, 256]])
                sp.dma_start(toe_raw[:, 4 * k:4 * k + 4, :], src).then_inc(toe_loaded[k], 16)
            sp.dma_start(router_w[:, :], gate_w).then_inc(small_loaded, 16)
            sp.dma_start(gates[:, 0:2], g_xattn.partition_broadcast(P)).then_inc(small_loaded, 16)
            sp.dma_start(gates[:, 2:4], g_ffn.partition_broadcast(P)).then_inc(small_loaded, 16)
            sp.dma_start(inv_i[:, :], inv_map.rearrange("a b -> (a b)").partition_broadcast(NE)).then_inc(small_loaded, 16)
            for kt in range(2):
                sp.dma_start(mu[:, kt, :].rearrange("p (g s) -> p g s", g=NG),
                             mask_up_w[:, kt * P:(kt + 1) * P, :].rearrange("g h s -> h g s")).then_inc(small_loaded, 16)
            for n in range(3):
                ring_load(n)
            sp.dma_start(ctx[:, Q:B, :], rows_of(ctx_rows, 1)).then_inc(ctx_loaded[1], 16)
            sp.dma_start(x_res[:, Q:B, :], rows_of(x, 1)).then_inc(x_loaded[1], 16)
            sp.dma_start(mask_words[:, :], mask.rearrange("b m -> (b m)").partition_broadcast(P)).then_inc(mask_loaded, 16)
            for n in range(3, len(RING_LOADS)):
                ring_load(n)
            mixer_free(sp)
            sp.dma_start(tern_w[:, 0].rearrange("p (r h) -> p r h", h=L),
                         w_fc.rearrange("(r p) h -> p r h", p=P)).then_inc(tern_loaded[0], 16)
            sp.dma_start(tern_w[:, 1].rearrange("p (r j) -> p r j", j=NJ),
                         w_proj.rearrange("(r p) j -> p r j", p=P)).then_inc(tern_loaded[1], 16)
            for u, bs in enumerate(UNITS):
                wait_drained(sp, ("out", u))
                sp.dma_start(out[bs.start:bs.stop].rearrange("b p l -> p b l"),
                             x_res[:, bs.start:bs.stop, :]).then_inc(stored, 16)
            sp.wait_ge(stored, 16 * len(UNITS))

        SMALL = 16 * 6

        @block.tensor
        def _(pe):
            def split_product(dst, lhs, rhs, start, stop):
                for i, (a, b) in enumerate(((0, 0), (1, 0), (0, 1))):
                    last = pe.matmul(dst, lhs(a), rhs(b), start=start and i == 0, stop=stop and i == 2)
                return last

            def turn(key, pieces, waits=()):
                claim(pe, key)
                for k, (piece, rows, cols) in enumerate(pieces):
                    last = pe.transpose(psum(key)[0:cols, k * rows:(k + 1) * rows], piece, ident[0:rows, 0:rows])
                fill(last, key)

            pe.wait_ge(consts_made, 2)
            for step in SCHEDULE:
                kind = step[0]
                if kind == "warm":
                    for _ in range(step[1]):
                        pe.matmul(banks[DN][:, 0:P], ones[:, :], ident[:, :], start=True, stop=True)
                elif kind == "turn_ctx":
                    _, half, t = step
                    pe.wait_ge(ctx_loaded[half], 16)
                    turn(step, [(ctx[:, half * Q + q, t * P:(t + 1) * P], P, P) for q in range(Q)])
                elif kind in ("turn_q", "turn_x"):
                    _, half, t = step
                    pe.wait_ge(normed, rows_normed("mix" if kind == "turn_q" else "moe", half))
                    turn(step, [(xn[:, q, t * P:(t + 1) * P], P, P) for q in range(Q)])
                elif kind in ("turn_0", "turn_1"):
                    u = step[1]
                    pe.wait_ge(normed, rows_normed("cross" if kind == "turn_0" else "mlp", u))
                    turn(step, [(xn1[:, k, t * P:(t + 1) * P], P, P) for t in range(2) for k in range(len(UNITS[u]))])
                elif kind == "conv":
                    _, half, h = step
                    g = group_no(half, h // 2)
                    if half == 0:
                        pe.wait_ge(toe_diag, h // 4 + 1)
                        pe.wait_ge(toe_off, h // 4 + 1)
                    pe.wait_ge(kv_made, g + 1)
                    claim(pe, step)

                    def pairs(t):
                        return kv[:, g % 2, (2 * (h % 2) + t) * Q:(2 * (h % 2) + t + 1) * Q].rearrange(
                            "p q d j -> p q (d j)")[:, :, 3:TAPS * SPAN]
                    y = psum(step)[:, 0:2 * Q * YW].rearrange("p (t q c) -> p t q c", t=2, q=Q)
                    pe.matmul(y[:, 0], toe[:, h, 0:P], pairs(0), start=True, stop=True)
                    pe.matmul(y[:, 1], toe[:, h, P:2 * P], pairs(0), start=True, stop=False)
                    fill(pe.matmul(y[:, 1], toe[:, h, 0:P], pairs(1), start=False, stop=True), step)
                elif kind == "turn_router":
                    pe.wait_ge(small_loaded, SMALL)
                    turn(step, [(router_w[:, t * P:(t + 1) * P], NE, P) for t in range(2)])
                elif kind == "turn_w":
                    _, which, p = step
                    n = RING_LOADS.index(f"{which}{p // 2}")
                    pe.wait_ge(ring_loaded[n % 3], 16 * (n // 3 + 1))
                    tiles = range(2 * p, min(2 * p + 2, TILES))
                    turn(step, [(ring[n % 3][:, (r % 4) * L + kt * P:(r % 4) * L + (kt + 1) * P], P, P)
                                for kt in range(2) for r in tiles])
                elif kind == "turn_down":
                    p = step[1]
                    for kt in range(2):
                        n = RING_LOADS.index(f"down{kt}")
                        pe.wait_ge(ring_loaded[n % 3], 16 * (n // 3 + 1))
                    n = RING_LOADS.index("down0")
                    turn(step, [(ring[(n + kt) % 3][:, r * P:(r + 1) * P], P, P)
                                for r in range(2 * p, min(2 * p + 2, TILES)) for kt in range(2)])
                elif kind == "mask_up":
                    _, which, c = step
                    pe.wait_ge(mu4_made, 2)
                    for p in range(6):
                        wait_drained(pe, ("turn_w", which, p))
                    claim(pe, step)
                    for kt in range(2):
                        last = split_product(psum(step)[:, 0:CW], lambda part: mu4[:, part, 2 * kt + c // 2, :],
                                             lambda part: w_split[:, WORDS[which], kt, part, c * CW:(c + 1) * CW],
                                             kt == 0, kt == 1)
                    fill(last, step)
                elif kind == "tern_sum":
                    k = TERNARY.index(step[1])
                    pe.wait_ge(tern_abs, k + 1)
                    claim(pe, step)
                    fill(pe.matmul(psum(step)[:, 0:1], ones[:, :], tern[:, k, 0:1], start=True, stop=True), step)
                elif kind == "turn_fc":
                    p = step[1]
                    pe.wait_ge(tern_made, 2)
                    slot = tern_w[:, 0]
                    turn(step, [(slot[:, r * L + kt * P:r * L + (kt + 1) * P], P, P)
                                for kt in range(2) for r in range(2 * p, min(2 * p + 2, JT))])
                elif kind == "turn_proj":
                    p = step[1]
                    pe.wait_ge(tern_made, 4)
                    slot = tern_w[:, 1]
                    turn(step, [(slot[:, kt * NJ + r * P:kt * NJ + (r + 1) * P], P, P)
                                for r in range(2 * p, min(2 * p + 2, JT)) for kt in range(2)])
                elif kind == "turn_att":
                    _, half, p = step
                    pe.wait_ge(gathered, group_no(half, HEADS // 2 - 1) + 1)
                    turn(step, [(att[:, t * Q + q].rearrange("p h j -> p (h j)"), P, P) for q in (2 * p, 2 * p + 1) for t in range(2)])
                elif kind == "logits":
                    half = step[1]
                    wait_drained(pe, ("turn_router",))
                    for t in range(2):
                        wait_drained(pe, ("turn_x", half, t))
                    claim(pe, step)
                    for q in range(Q):
                        for kt in range(2):
                            last = split_product(psum(step)[:, q * NE:(q + 1) * NE],
                                                 lambda part: xt[half][:, kt, part, q * P:(q + 1) * P],
                                                 lambda part: router_t[:, kt, part, :], kt == 0, kt == 1)
                    fill(last, step)
                elif kind == "turn_top":
                    half = step[1]
                    pe.wait_ge(chosen, half + 1)
                    turn(step, [(rts[half][3][:, q * NE:(q + 1) * NE], P, NE) for q in range(Q)])
                elif kind == "flat":
                    half = step[1]
                    pe.wait_ge(onehot_made, 1)
                    wait_drained(pe, ("turn_top", half))
                    claim(pe, step)
                    for q in range(Q):
                        last = pe.matmul(psum(step)[:, q * NE:(q + 1) * NE], top_t[half][:, q * P:(q + 1) * P], onehot[:, :],
                                         start=True, stop=True)
                    fill(last, step)
                elif kind == "turn_soft":
                    _, half, gh = step
                    pe.wait_ge(soft_made, half + 1)
                    turn(step, [(soft_parts[:, 2 * q + gh].rearrange("p a c -> p (a c)"), P, P) for q in range(Q)])
                elif kind == "chunk":
                    _, b, c = step
                    half, q = b // Q, b % Q
                    if b == 0 and c == 0:
                        for which in WORDS:
                            for k in range(NCH):
                                wait_drained(pe, ("mask_up", which, k))
                    for gh in range(2):
                        wait_drained(pe, ("turn_soft", half, gh))
                    claim(pe, ("gate", b, c))
                    claim(pe, ("up", b, c))
                    rows = slice(q * P, (q + 1) * P)
                    cols = slice(c * CW, (c + 1) * CW)
                    ops = [(xt[half][:, kt, pa, rows], kt, pb) for kt in range(2) for pa, pb in ((0, 0), (0, 1), (1, 0))]
                    for i, (lhs, kt, part) in enumerate(ops):
                        for w, name in enumerate(("gate", "up")):
                            pe.matmul(psum((name, b, c))[:, 0:CW], lhs, w_split[:, w, kt, part, cols],
                                      start=i == 0, stop=False)
                    for w, name in enumerate(("gate", "up")):
                        fill(pe.matmul(psum((name, b, c))[:, 0:CW], soft_t[half][:, c // 2, rows], m_stack[:, w, cols],
                                       start=False, stop=True), (name, b, c))
                elif kind == "turn_a":
                    _, b, c = step
                    wait_drained(pe, ("up", b, c))
                    turn(step, [(act[:, r * P:(r + 1) * P], P, P) for r in DONE_TILES[c]])
                elif kind == "down":
                    b = step[1]
                    if b == 0:
                        for p in range(6):
                            wait_drained(pe, ("turn_down", p))
                    claim(pe, step)
                    for r in range(TILES):
                        for c in range(NCH):
                            if r == DONE_TILES[c].start:
                                wait_drained(pe, ("turn_a", b, c))
                        last = split_product(psum(step)[:, 0:L], lambda part: a_t[:, r, part, :],
                                             lambda part: d_split[:, r, part, :], r == 0, r == TILES - 1)
                    fill(last, step)
                elif kind == "scores":
                    u = step[1]
                    wait_drained(pe, ("turn_0", u))
                    claim(pe, step)
                    for k, b in enumerate(UNITS[u]):
                        half, q = divmod(b, Q)
                        for t in range(2):
                            last = pe.matmul(psum(step)[:, k * P:(k + 1) * P], qt[:, t, k * P:(k + 1) * P],
                                             ctx_ext[:, half, :, t, q, 3:3 + HD], start=t == 0, stop=t == 1)
                    fill(last, step)
                elif kind == "turn_p":
                    u = step[1]
                    pe.wait_ge(s_exp, UNITS[u].stop)
                    turn(step, [(s_att[:, k, :], P, P) for k in range(len(UNITS[u]))])
                elif kind == "read":
                    u = step[1]
                    wait_drained(pe, ("turn_p", u))
                    claim(pe, step)
                    for k, b in enumerate(UNITS[u]):
                        last = pe.matmul(psum(step)[:, k * L:(k + 1) * L], pt[:, k * P:(k + 1) * P],
                                         ctx[:, b, :], start=True, stop=True)
                    fill(last, step)
                elif kind == "hidden":
                    _, u, jp = step
                    wait_drained(pe, ("turn_1", u))
                    if u == 0 and jp == 0:
                        for p in range(3):
                            wait_drained(pe, ("turn_fc", p))
                    claim(pe, step)
                    n = P * len(UNITS[u])
                    for i, j in enumerate(range(2 * jp, min(2 * jp + 2, JT))):
                        for kt in range(2):
                            for part in range(2):
                                last = pe.matmul(psum(step)[:, i * n:(i + 1) * n],
                                                 fc_t[:, kt, j * P:(j + 1) * P], x1t[:, part, kt, 0:n],
                                                 start=kt + part == 0, stop=kt + part == 2)
                    fill(last, step)
                elif kind == "out":
                    u = step[1]
                    if u == 0:
                        for k in range(3):
                            wait_drained(pe, ("turn_proj", k))
                    pe.wait_ge(hid_lo, 3 * (u + 1))
                    claim(pe, step)
                    for k in range(len(UNITS[u])):
                        for j in range(JT):
                            for part in range(2):
                                last = pe.matmul(psum(step)[:, k * L:(k + 1) * L],
                                                 hid_t[:, j, part, k * P:(k + 1) * P],
                                                 proj_t[:, j, :], start=j + part == 0, stop=j + part == JT)
                    fill(last, step)

        @block.scalar
        def _(act_e):
            def copy(dst, src):
                return act_e.activation(dst, src, ACT.Copy)

            for step in SCHEDULE:
                kind = step[0]
                if kind == "consts":
                    act_e.wait_ge(small_loaded, SMALL)
                    act_e.activation(tg[:, :], gates[:, :], ACT.Tanh).then_inc(tanh_done, 1)
                elif kind == "toe":
                    k = step[1]
                    act_e.wait_ge(toe_loaded[k], 16)
                    src = toe_raw[:, 4 * k:4 * k + 4, 0:P]
                    copy(toe[:, 4 * k:4 * k + 4, P:2 * P], src[:, :, ::-1]).then_inc(toe_off, 1)
                elif kind in ("turn_ctx", "turn_q"):
                    _, half, t = step
                    if kind == "turn_q" and half == 1 and t == 0:
                        for h in (HEADS - 2, HEADS - 1):
                            wait_drained(act_e, ("conv", 0, h))
                    wait_filled(act_e, step)
                    src = psum(step)[:, :].rearrange("p (q h i) -> p q h i", q=Q, h=HEADS)
                    dst = (ctx_ext[:, half, :, t, :, :] if kind == "turn_ctx" else
                           q_ext[:, :, t * Q:(t + 1) * Q, :]).rearrange("p h q e -> p q h e")
                    for d0, s0, n in ((3, 0, 8), (0, 5, 3), (11, 0, 4)):
                        drain(copy(dst[:, :, :, d0:d0 + n], src[:, :, :, s0:s0 + n]), step)
                elif kind == "turn_router":
                    wait_filled(act_e, step)
                    drain(copy(router_t[:, :, 0, :], psum(step)[:, 0:2 * NE].rearrange("p (t e) -> p t e", t=2)), step)
                elif kind == "turn_w":
                    _, which, p = step
                    if which == "gate" and p == 0:
                        act_e.wait_ge(toe_diag, 4)
                        act_e.wait_ge(toe_off, 4)
                    wait_filled(act_e, step)
                    n = P * len(range(2 * p, min(2 * p + 2, TILES)))
                    drain(copy(w_split[:, WORDS[which], :, 0, 2 * p * P:2 * p * P + n],
                               psum(step)[:, 0:2 * n].rearrange("p (t c) -> p t c", t=2)), step)
                elif kind == "turn_down":
                    p = step[1]
                    wait_filled(act_e, step)
                    n = len(range(2 * p, min(2 * p + 2, TILES)))
                    drain(copy(d_split[:, 2 * p:2 * p + n, 0, :],
                               psum(step)[:, 0:n * L].rearrange("p (r c) -> p r c", c=L)), step)
                elif kind == "mask_up":
                    _, which, c = step
                    act_e.wait_ge(ind_made, 2)
                    k = WORDS[which] * NCH + c
                    if k >= 2:
                        prev = [("mask_up", w, cc) for w in WORDS for cc in range(NCH)][k - 2]
                        wait_drained(act_e, prev)
                    wait_filled(act_e, step)
                    for i in range(2):
                        cols = slice(i * NI, (i + 1) * NI)
                        g = 2 * (c % 2) + i
                        drain(act_e.activation(half_m[:, k % 2, cols], psum(step)[:, cols], ACT.Copy,
                                               scale=ind[:, 1, g:g + 1]), step)
                elif kind == "turn_fc":
                    p = step[1]
                    wait_filled(act_e, step)
                    n = P * len(range(2 * p, min(2 * p + 2, JT)))
                    drain(copy(fc_t[:, :, 2 * p * P:2 * p * P + n],
                               psum(step)[:, 0:2 * n].rearrange("p (t c) -> p t c", t=2)), step)
                elif kind == "turn_proj":
                    p = step[1]
                    wait_filled(act_e, step)
                    n = len(range(2 * p, min(2 * p + 2, JT)))
                    drain(copy(proj_t[:, 2 * p:2 * p + n, :],
                               psum(step)[:, 0:n * L].rearrange("p (r c) -> p r c", c=L)), step)
                elif kind == "turn_x":
                    _, half, t = step
                    if half == 0 and t == 0:
                        for w in WORDS:
                            wait_drained(act_e, ("mask_up", w, NCH - 1))
                    elif t == 0:
                        mixer_free(act_e)
                    wait_filled(act_e, step)
                    drain(copy(xt[half][:, t, 0, :], psum(step)[:, :]), step)
                elif kind == "turn_0":
                    u = step[1]
                    if u:
                        wait_filled(act_e, ("scores", u - 1))
                    wait_filled(act_e, step)
                    n = P * len(UNITS[u])
                    drain(copy(qt[:, :, 0:n], psum(step)[:, 0:2 * n].rearrange("p (t n) -> p t n", t=2)), step)
                elif kind == "turn_1":
                    u = step[1]
                    if u:
                        wait_filled(act_e, ("hidden", u - 1, 2))
                    wait_filled(act_e, step)
                    n = P * len(UNITS[u])
                    drain(copy(x1t[:, 0, :, 0:n], psum(step)[:, 0:2 * n].rearrange("p (t n) -> p t n", t=2)), step)
                elif kind == "top":
                    half = step[1]
                    act_e.wait_ge(shifted, half + 1)
                    act_e.activation(rts[half][0][:, :], rts[half][0][:, :], ACT.Exp).then_inc(router_exp, 1)
                elif kind == "turn_top":
                    half = step[1]
                    if half == 0:
                        wait_filled(act_e, ("turn_down", 5))
                    wait_filled(act_e, step)
                    drain(copy(top_t[half][:, :], psum(step)[0:NE, :]), step)
                elif kind == "soft":
                    half = step[1]
                    act_e.wait_ge(soft_shifted, half + 1)
                    act_e.activation(rts[half][1][:, :], rts[half][1][:, :], ACT.Exp).then_inc(soft_exp, 1)
                elif kind == "turn_soft":
                    _, half, gh = step
                    wait_filled(act_e, step)
                    drain(copy(soft_t[half][:, gh, :], psum(step)[:, :]), step)
                elif kind == "chunk":
                    _, b, c = step
                    n = b * NCH + c
                    if n == 0:
                        wait_filled(act_e, ("flat", 0))
                    if n >= 2:
                        wait_drained(act_e, ("up", (n - 2) // NCH, (n - 2) % NCH))
                    wait_filled(act_e, ("gate", b, c))
                    drain(act_e.activation(silu[:, n % 2, :], psum(("gate", b, c))[:, 0:CW], ACT.Silu), ("gate", b, c))
                elif kind == "turn_a":
                    _, b, c = step
                    if b >= 1:
                        wait_filled(act_e, ("down", b - 1))
                    wait_filled(act_e, step)
                    r = DONE_TILES[c]
                    drain(copy(a_t[:, r.start:r.stop, 0, :],
                               psum(step)[:, 0:len(r) * P].rearrange("p (r n) -> p r n", n=P)), step)
                elif kind == "scores":
                    u = step[1]
                    act_e.wait_ge(s_shifted, u + 1)
                    for k in range(len(UNITS[u])):
                        act_e.activation(s_att[:, k, :], s_att[:, k, :], ACT.Exp, bias=nmax1[:, k:k + 1],
                                         accum_out=esum[:, k:k + 1]).then_inc(s_exp, 1)
                elif kind == "turn_p":
                    u = step[1]
                    if u:
                        wait_filled(act_e, ("read", u - 1))
                    wait_filled(act_e, step)
                    n = P * len(UNITS[u])
                    drain(copy(pt[:, 0:n], psum(step)[:, 0:n]), step)
                elif kind == "hidden":
                    _, u, jp = step
                    n = HIDDEN.index((u, jp))
                    rows = P * len(UNITS[u])
                    j0, nj = 2 * jp, min(2, JT - 2 * jp)
                    if n == 0:
                        wait_filled(act_e, ("flat", 1))
                        act_e.wait_ge(soft_made, 2)
                    if n >= 2:
                        act_e.wait_ge(hid_lo, n - 1)
                    wait_filled(act_e, step)
                    drain(act_e.activation(relu[:, n % 2, 0:nj * rows], psum(step)[:, 0:nj * rows], ACT.Relu), step)
                    if jp == 0:
                        wait_filled(act_e, ("out", u - 1) if u else ("turn_proj", 2))
                    wait_drained(act_e, step)
                    act_e.activation(hid_t[:, j0:j0 + nj, 0, 0:rows], relu[:, n % 2, 0:nj * rows].rearrange(
                        "p (j c) -> p j c", c=rows), ACT.Square).then_inc(hid_hi, 1)

        @block.vector
        def _(dve):
            own = [0]

            def mine(ins):
                own[0] += 1
                ins.then_inc(dve_own, 1)
                dve.wait_ge(dve_own, own[0])

            def residue(dst, key, src, hi, reads=1):
                wait_drained(dve, key, reads)
                drain(dve.tensor_tensor(dst, src, hi.bitcast(F32), ALU.subtract), key)

            dve.wait_ge(consts_made, 4)
            for step in SCHEDULE:
                kind = step[0]
                if kind == "consts":
                    dve.wait_ge(small_loaded, SMALL)
                    dve.tensor_scalar(pidx[:, 1:2], pidx[:, 0:1], 3, 3, ALU.logical_shift_right, ALU.bitwise_and)
                    mine(dve.tensor_scalar(pidx[:, 2:3], pidx[:, 0:1], 5, 1, ALU.logical_shift_right, ALU.bitwise_and))
                    mine(dve.tensor_copy(pidx_f[:, :], pidx[:, :]))
                    for g in range(4):
                        last = dve.tensor_scalar(ind[:, 0, g:g + 1], pidx_f[:, 1:2], float(g), None, ALU.is_equal)
                    last.then_inc(ind_made, 1)
                    dve.wait_ge(ind_made, 1)
                    dve.tensor_scalar(ind[:, 1, :], ind[:, 0, :], pidx_f[:, 2:3], None, ALU.mult).then_inc(ind_made, 1)
                    mine(dve.tensor_copy(inv_f[:, 0, :], inv_i[:, :]))
                    mine(dve.tensor_scalar(inv_f[:, 1, :], inv_f[:, 0, :], 0.0, float(NE), ALU.is_lt, ALU.mult))
                    mine(dve.tensor_tensor(inv_f[:, 0, :], inv_f[:, 0, :], inv_f[:, 1, :], ALU.add))
                    dve.tensor_scalar(onehot[:, :], inv_f[:, 0, :], pidx_f[0:NE, 0:1], None, ALU.is_equal).then_inc(onehot_made, 1)
                    mu_in = mu[:, :, :].rearrange("p t (a c) -> p (t a) c", c=32).unsqueeze(2).broadcast_to([P, 4, 4, 32])
                    hi = mu4[:, 0, :, :].rearrange("p b (k c) -> p b k c", c=32)
                    lo = mu4[:, 1, :, :].rearrange("p b (k c) -> p b k c", c=32)
                    dve.tensor_copy(hi, mu_in).then_inc(mu4_made, 1)
                    dve.wait_ge(mu4_made, 1)
                    dve.tensor_tensor(lo, mu_in, hi.bitcast(F32), ALU.subtract).then_inc(mu4_made, 1)
                elif kind == "toe":
                    k = step[1]
                    if k == 0:
                        dve.wait_ge(skip_loaded, 16)
                    dve.wait_ge(toe_loaded[k], 16)
                    for h in range(4 * k, 4 * k + 4):
                        src = toe_raw[:, h, P:2 * P]
                        last = dve.scalar_tensor_tensor(out=toe[:, h, 0:P], in0=ident[:, :], scalar=skip_sb[:, h:h + 1],
                                                        in1=src[:, ::-1], op0=ALU.mult, op1=ALU.add)
                    last.then_inc(toe_diag, 1)
                elif kind == "stat":
                    _, which, k = step
                    rows = batches_of(which, k)
                    updates_of_x(dve, which, k)
                    for i, b in enumerate(rows):
                        last = dve.bn_stats(stats[:, i, :], x_res[:, b, :])
                    mine(last)
                    for i in range(len(rows)):
                        last = dve.bn_aggr(mv[:, i, :], stats[:, i, :])
                    last.then_inc(stats_done, 1)
                elif kind == "norm":
                    _, which, k = step
                    n = NORMS.index((which, k))
                    dst = xn if which in ("mix", "moe") else xn1
                    before = [m for m in NORMS[:n] if (m[0] in ("mix", "moe")) == (dst is xn)]
                    if before:
                        turned(dve, *before[-1])
                    if (which, k) == ("moe", 1):
                        wait_filled(dve, ("turn_soft", 0, 1))
                    dve.wait_ge(rstd_done, n + 1)
                    for i, b in enumerate(batches_of(which, k)):
                        dve.tensor_scalar(dst[:, i, :], x_res[:, b, :], mv[:, i, 0:1], rstd[:, i:i + 1],
                                          ALU.subtract, ALU.mult).then_inc(normed, 1)
                elif kind == "conv":
                    _, half, h = step
                    if h == 0:
                        for t in range(2):
                            wait_drained(dve, ("turn_q", half, t))
                    hn = half * HEADS + h
                    if hn >= 2:
                        dve.wait_ge(folded, hn - 1)
                    wait_filled(dve, step)
                    y = psum(step)
                    qb = h * 2 * Q * EXT
                    o = prod[:, h % 2]
                    drain(dve.tensor_tensor(o[:, :, 0:TAPS, :], view(y, 0, [[YW, 2 * Q], [SPAN, TAPS], [1, HD]]),
                                            view(q_ext, qb + 3, [[EXT, 2 * Q], [1, TAPS], [1, HD]]), ALU.mult), step)
                    drain(dve.tensor_tensor(o[:, :, TAPS:HD, :], view(y, SPAN - 1, [[YW, 2 * Q], [SPAN - 1, 3], [1, HD]]),
                                            view(q_ext, qb + 2, [[EXT, 2 * Q], [-1, 3], [1, HD]]), ALU.mult), step)
                elif kind == "gather":
                    _, half, g = step
                    n = group_no(half, g)
                    dve.wait_ge(folded, 2 * (n + 1))
                    if half == 1 and g == 0:
                        for p in range(2):
                            wait_filled(dve, ("turn_att", 0, p))
                    dve.tensor_reduce(att[:, :, 2 * g:2 * g + 2].rearrange("p n h j -> p h n j"),
                                      fold[:, n % 2].rearrange("p (h n) s j -> p h n j s", h=2), AXX,
                                      ALU.add).then_inc(gathered, 1)
                elif kind == "turn_att":
                    _, half, p = step
                    b0 = half * Q + 2 * p
                    if half == 0 and p == 0:
                        dve.wait_ge(tanh_done, 1)
                    dve.wait_ge(x_loaded[half], 16)
                    wait_filled(dve, step)
                    rows = x_res[:, b0:b0 + 2, :].rearrange("p b l -> p (b l)")
                    drain(dve.scalar_tensor_tensor(out=rows, in0=psum(step)[:, :], scalar=tg[:, 0:1], in1=rows,
                                                   op0=ALU.mult, op1=ALU.add), step)
                elif kind == "turn_router":
                    residue(router_t[:, :, 1, :], step, psum(step)[:, 0:2 * NE].rearrange("p (t e) -> p t e", t=2),
                            router_t[:, :, 0, :])
                elif kind == "turn_w":
                    _, which, p = step
                    n = P * len(range(2 * p, min(2 * p + 2, TILES)))
                    cols = slice(2 * p * P, 2 * p * P + n)
                    w = WORDS[which]
                    residue(w_split[:, w, :, 1, cols], step, psum(step)[:, 0:2 * n].rearrange("p (t c) -> p t c", t=2),
                            w_split[:, w, :, 0, cols])
                elif kind == "turn_down":
                    p = step[1]
                    n = len(range(2 * p, min(2 * p + 2, TILES)))
                    residue(d_split[:, 2 * p:2 * p + n, 1, :], step,
                            psum(step)[:, 0:n * L].rearrange("p (r c) -> p r c", c=L), d_split[:, 2 * p:2 * p + n, 0, :])
                elif kind == "mask_up":
                    _, which, c = step
                    k = WORDS[which] * NCH + c
                    wait_drained(dve, step, 2)
                    for i in range(2):
                        cols = slice(i * NI, (i + 1) * NI)
                        g = 2 * (c % 2) + i
                        drain(dve.scalar_tensor_tensor(
                            out=m_stack[:, WORDS[which], c * CW + i * NI:c * CW + (i + 1) * NI], in0=psum(step)[:, cols],
                            scalar=ind[:, 0, g:g + 1], in1=half_m[:, k % 2, cols].bitcast(F32), op0=ALU.mult,
                            op1=ALU.subtract), step)
                elif kind == "tern_abs":
                    k = TERNARY.index(step[1])
                    dve.wait_ge(tern_loaded[k], 16)
                    dve.tensor_reduce(tern[:, k, 0:1], tern_w[:, k, :], AXX, ALU.add,
                                      apply_absolute_value=True).then_inc(tern_abs, 1)
                elif kind == "tern_sum":
                    k = TERNARY.index(step[1])
                    wait_filled(dve, step)
                    drain(dve.tensor_scalar(tern[:, k, 1:2], psum(step)[:, 0:1], 1.0 / (NJ * L), 1e-5, ALU.mult, ALU.max),
                          step)
                    wait_drained(dve, step)
                    dve.tensor_scalar(tern[:, k, 2:3], tern[:, k, 1:2], 0.7, None, ALU.mult)
                    mine(dve.tensor_scalar(tern[:, k, 3:4], tern[:, k, 1:2], -0.7, None, ALU.mult))
                    dve.nop().then_inc(tern_thr, 1)
                    if k == 1:
                        dve.wait_ge(tanh_done, 1)
                        mine(dve.tensor_tensor(out_scale[:, 0:1], tern[:, 0, 1:2], tern[:, 0, 1:2], ALU.mult))
                        mine(dve.tensor_tensor(out_scale[:, 1:2], out_scale[:, 0:1], tern[:, 1, 1:2], ALU.mult))
                        mine(dve.tensor_tensor(out_scale[:, 2:3], out_scale[:, 1:2], tg[:, 3:4], ALU.mult))
                elif kind == "tern_sign":
                    _, name, part = step
                    k = TERNARY.index(name)
                    w = tern_w[:, k, part * NJ:(part + 1) * NJ]
                    dve.wait_ge(tern_low, 2 * k + part + 1)
                    dve.scalar_tensor_tensor(out=w, in0=w, scalar=tern[:, k, 2:3], in1=tern_tmp[:, :], op0=ALU.is_gt,
                                             op1=ALU.subtract).then_inc(tern_made, 1)
                elif kind == "mask":
                    dve.wait_ge(mask_loaded, 16)
                    mixer_free(dve)
                    mine(dve.tensor_reduce(valid[:, 0, :], mask_sb.rearrange("p (b m) -> p b m", b=B), AXX, ALU.max))
                    dve.tensor_scalar(valid[:, 1, :], valid[:, 0, :], tg[:, 1:2], None, ALU.mult)
                    mine(dve.tensor_scalar(neg[:, :], mask_sb, -1.0, 1e30, ALU.add, ALU.mult))
                elif kind == "turn_x":
                    _, half, t = step
                    residue(xt[half][:, t, 1, :], step, psum(step)[:, :], xt[half][:, t, 0, :])
                elif kind == "turn_1":
                    n = P * len(UNITS[step[1]])
                    residue(x1t[:, 1, :, 0:n], step, psum(step)[:, 0:2 * n].rearrange("p (t n) -> p t n", t=2),
                            x1t[:, 0, :, 0:n])
                elif kind == "logits":
                    half = step[1]
                    if half == 0:
                        wait_filled(dve, ("turn_down", 5))
                    else:
                        mixer_free(dve)
                    rt = rts[half]
                    wait_filled(dve, step)
                    z = psum(step)[:, 0:Q * NE].rearrange("p (q e) -> p q e", q=Q)
                    drain(dve.tensor_reduce(nmax[:, :], z, AXX, ALU.max, negate=True), step)
                    wait_drained(dve, step, 1)
                    r0 = rt[0][:, :].rearrange("p (q e) -> p q e", q=Q)
                    drain(dve.tensor_tensor(r0, z, nmax[:, :].unsqueeze(2).broadcast_to([P, Q, NE]), ALU.add), step)
                    wait_drained(dve, step)
                    dve.nop().then_inc(shifted, 1)
                elif kind == "top":
                    half = step[1]
                    rt = rts[half]
                    v = [r[:, :].rearrange("p (q e) -> p q e", q=Q) for r in rt]
                    dve.wait_ge(router_exp, half + 1)
                    mine(dve.tensor_reduce(rsum[:, 0, :], v[0], AXX, ALU.add))
                    mine(dve.reciprocal(rsum[:, 1, :], rsum[:, 0, :]))
                    mine(dve.tensor_tensor(v[1], v[0], rsum[:, 1, :].unsqueeze(2).broadcast_to([P, Q, NE]), ALU.mult))
                    for q in range(Q):
                        last = dve.max(top8[:, q, :], v[1][:, q, :])
                    mine(last)
                    for q in range(Q):
                        last = dve.match_replace(v[2][:, q, :], top8[:, q, :], v[1][:, q, :], 0.0)
                    mine(last)
                    dve.tensor_tensor(rt[3][:, :], rt[1][:, :], rt[2][:, :], ALU.subtract).then_inc(chosen, 1)
                elif kind == "flat":
                    half = step[1]
                    rt = rts[half]
                    wait_filled(dve, step)
                    f = psum(step)[:, 0:Q * NE]
                    f3 = f.rearrange("p (n s) -> p n s", s=GS)
                    dst = scal[:, half * Q:(half + 1) * Q, :].rearrange("p q g -> p (q g)")
                    drain(dve.tensor_reduce(dst, f3, AXX, ALU.add), step)
                    drain(dve.tensor_scalar(rt[0][:, :], f, 0.0, -1e9, ALU.is_equal, ALU.mult), step)
                    wait_drained(dve, step, 2)
                    drain(dve.tensor_tensor(rt[2][:, :], f, rt[0][:, :], ALU.add), step)
                    wait_drained(dve, step)
                    v2 = rt[2][:, :].rearrange("p (n s) -> p n s", s=GS)
                    v1 = rt[1][:, :].rearrange("p (n s) -> p n s", s=GS)
                    mine(dve.tensor_reduce(gmax[:, 0, :], v2, AXX, ALU.max))
                    dve.tensor_tensor(v1, v2, gmax[:, 0, :].unsqueeze(2).broadcast_to([P, Q * NG, GS]),
                                      ALU.subtract).then_inc(soft_shifted, 1)
                elif kind == "soft":
                    half = step[1]
                    rt = rts[half]
                    v1 = rt[1][:, :].rearrange("p (n s) -> p n s", s=GS)
                    v0 = rt[0][:, :].rearrange("p (n s) -> p n s", s=GS)
                    dve.wait_ge(soft_exp, half + 1)
                    mine(dve.tensor_reduce(gmax[:, 1, :], v1, AXX, ALU.add))
                    mine(dve.reciprocal(gmax[:, 2, :], gmax[:, 1, :]))
                    mine(dve.tensor_tensor(v0, v1, gmax[:, 2, :].unsqueeze(2).broadcast_to([P, Q * NG, GS]), ALU.mult))
                    src = rt[0][:, :].rearrange("p (n c) -> p n c", c=32).unsqueeze(2).broadcast_to([P, 2 * Q, 2, 32])
                    for t in range(2):
                        wait_filled(dve, ("turn_x", half, t))
                    mine(dve.tensor_copy(soft_parts[:, :, 0:2, :].bitcast(F32R), src))
                    dve.tensor_tensor(soft_parts[:, :, 2:4, :].bitcast(F32R), src, soft_parts[:, :, 0:2, :],
                                      ALU.subtract).then_inc(soft_made, 1)
                elif kind == "chunk":
                    _, b, c = step
                    n = b * NCH + c
                    if n == 0:
                        wait_filled(dve, ("turn_top", 0))
                    if b:
                        wait_filled(dve, ("turn_a", b - 1, min(c + 1, NCH - 1)))
                    wait_drained(dve, ("gate", b, c))
                    wait_filled(dve, ("up", b, c))
                    for i in range(2):
                        cols = slice(i * NI, (i + 1) * NI)
                        g = 2 * c + i
                        drain(dve.scalar_tensor_tensor(out=act[:, g * NI:(g + 1) * NI], in0=silu[:, n % 2, cols],
                                                       scalar=scal[:, b, g:g + 1], in1=psum(("up", b, c))[:, cols],
                                                       op0=ALU.mult, op1=ALU.mult), ("up", b, c))
                elif kind == "turn_a":
                    _, b, c = step
                    r = DONE_TILES[c]
                    residue(a_t[:, r.start:r.stop, 1, :], step,
                            psum(step)[:, 0:len(r) * P].rearrange("p (r n) -> p r n", n=P), a_t[:, r.start:r.stop, 0, :])
                elif kind == "down":
                    b = step[1]
                    wait_filled(dve, step)
                    drain(dve.scalar_tensor_tensor(out=x_res[:, b, :], in0=psum(step)[:, 0:L], scalar=tg[:, 2:3],
                                                   in1=x_res[:, b, :], op0=ALU.mult, op1=ALU.add), step)
                elif kind == "scores":
                    u = step[1]
                    if u:
                        wait_filled(dve, ("turn_p", u - 1))
                    wait_filled(dve, step)
                    bs = UNITS[u]
                    n = len(bs)
                    s2 = s_att[:, 0:n, :].rearrange("p k m -> p (k m)")
                    drain(dve.scalar_tensor_tensor(out=s2, in0=psum(step)[:, 0:n * P], scalar=1.0 / float(np.sqrt(L)),
                                                   in1=neg[:, bs.start * P:bs.stop * P], op0=ALU.mult, op1=ALU.add),
                          step)
                    wait_drained(dve, step)
                    dve.tensor_reduce(nmax1[:, 0:n], s_att[:, 0:n, :], AXX, ALU.max, negate=True).then_inc(s_shifted, 1)
                elif kind == "read":
                    u = step[1]
                    bs = UNITS[u]
                    n = len(bs)
                    dve.wait_ge(s_exp, bs.stop)
                    mine(dve.reciprocal(rv[:, 0, 0:n], esum[:, 0:n]))
                    mine(dve.tensor_tensor(rv[:, 1, 0:n], rv[:, 0, 0:n], valid[:, 1, bs.start:bs.stop], ALU.mult))
                    wait_filled(dve, step)
                    for k, b in enumerate(bs):
                        drain(dve.scalar_tensor_tensor(out=x_res[:, b, :], in0=psum(step)[:, k * L:(k + 1) * L],
                                                       scalar=rv[:, 1, k:k + 1], in1=x_res[:, b, :], op0=ALU.mult,
                                                       op1=ALU.add), step)
                elif kind == "hidden":
                    _, u, jp = step
                    n = HIDDEN.index((u, jp))

                    rows = P * len(UNITS[u])
                    j0, nj = 2 * jp, min(2, JT - 2 * jp)
                    w = nj * rows
                    if n == 0:
                        wait_filled(dve, ("flat", 1))
                        dve.wait_ge(soft_made, 2)
                    if n:
                        dve.wait_ge(hid_lo, n)
                    wait_drained(dve, step)
                    mine(dve.tensor_tensor(hsq[:, 0:w], relu[:, n % 2, 0:w], relu[:, n % 2, 0:w], ALU.mult))
                    dve.wait_ge(hid_hi, n + 1)
                    dve.tensor_tensor(hid_t[:, j0:j0 + nj, 1, 0:rows], hsq[:, 0:w].rearrange("p (j c) -> p j c", c=rows),
                                      hid_t[:, j0:j0 + nj, 0, 0:rows].bitcast(F32), ALU.subtract).then_inc(hid_lo, 1)
                elif kind == "out":
                    u = step[1]
                    rows = x_res[:, UNITS[u].start:UNITS[u].stop, :].rearrange("p b l -> p (b l)")
                    wait_filled(dve, step)
                    drain(dve.scalar_tensor_tensor(out=rows, in0=psum(step)[:, 0:L * len(UNITS[u])], scalar=out_scale[:, 2:3], in1=rows,
                                                   op0=ALU.mult, op1=ALU.add), step)

        @block.gpsimd
        def _(pool):
            pool.memset(ones[:, :], 1.0).then_inc(consts_made, 1)
            pool.iota(pidx[:, 0:1], pattern=[[0, 1]], base=0, channel_multiplier=1)
            pool.memset(mhalf[:, :], -0.5)
            pool.wait_ge(consts_made, 1)
            pool.affine_select(out=ident[:, :], in_=ones[:, :], compare_op=ALU.is_equal, fill=0.0, base=0,
                               pattern=[[1, P]], channel_multiplier=-1).then_inc(consts_made, 1)
            pool.wait_ge(consts_made, 2)
            pool.nop().then_inc(consts_made, 2)
            for step in SCHEDULE:
                kind = step[0]
                if kind == "stat":
                    n = NORMS.index(step[1:])
                    rows = len(batches_of(*step[1:]))
                    pool.wait_ge(stats_done, n + 1)
                    pool.tensor_scalar(ve[:, 0:rows], mv[:, 0:rows, 1], EPS, None, ALU.add).then_inc(pool_own, 1)
                    pool.wait_ge(pool_own, n + 1)
                    if n:
                        pool.wait_ge(normed, rows_normed(*NORMS[n - 1]))
                    pool.tensor_tensor(rstd[:, 0:rows], ve[:, 0:rows], mhalf[:, 0:rows], ALU.pow).then_inc(rstd_done, 1)
                elif kind == "tern_sign":
                    _, name, part = step
                    k = TERNARY.index(name)
                    pool.wait_ge(tern_thr, k + 1)
                    if k or part:
                        pool.wait_ge(tern_made, 2 * k + part)
                    pool.tensor_scalar(tern_tmp[:, :], tern_w[:, k, part * NJ:(part + 1) * NJ], tern[:, k, 3:4], None,
                                       ALU.is_lt).then_inc(tern_low, 1)
                elif kind == "kv":
                    _, half, g = step
                    n = group_no(half, g)
                    if g == 0:
                        for t in range(2):
                            wait_drained(pool, ("turn_ctx", half, t))
                    if n >= 2:
                        hf, gg = divmod(n - 2, HEADS // 2)
                        for h in (2 * gg, 2 * gg + 1):
                            wait_filled(pool, ("conv", hf, h))
                    base = (half * HEADS + 2 * g) * 2 * Q * EXT
                    pool.tensor_tensor(kv[:, n % 2], view(ctx_ext, base, [[EXT, 4 * Q], [0, TAPS], [1, SPAN]]),
                                       view(ctx_ext, base, [[EXT, 4 * Q], [1, TAPS], [1, SPAN]]),
                                       ALU.mult).then_inc(kv_made, 1)
                elif kind == "fold":
                    _, half, h = step
                    n = group_no(half, h // 2)
                    wait_drained(pool, ("conv", half, h))
                    if h % 2 == 0 and n >= 2:
                        pool.wait_ge(gathered, n - 1)
                    p4 = prod[:, h % 2].rearrange("p n s j -> p n (s j)")
                    f = fold[:, n % 2, 2 * Q * (h % 2):2 * Q * (h % 2 + 1)].rearrange("p n s j -> p n (s j)")
                    pool.tensor_tensor(f, p4[:, :, 0:32], p4[:, :, 32:64], ALU.add).then_inc(folded, 1)


def kernel(**inputs):
    import concourse.bacc as bacc
    from concourse.bass_utils import run_bass_kernel_spmd as run

    a = {k: np.ascontiguousarray(v) for k, v in inputs.items()}
    rev = np.zeros((HEADS, KPAD), np.float32)
    rev[:, 0:L] = a["L0_xattn_ssm_kernel"][:, ::-1]
    arrays = {
        "x": a["x"], "ctx_rows": a["ctx_2048"], "mask": a["mask_BxS2_bk0"].view(np.int32), "g_xattn": a["g_xattn"],
        "g_ffn": a["g_ffn"], "kernel_rev": rev, "skip": a["L0_xattn_D"], "gate_w": a["L0_ffn_gate_w"],
        "mask_up_w": a["L0_ffn_mask_up_w"], "gate_p": a["L0_ffn_gate_proj_w"], "up_p": a["L0_ffn_up_proj_w"],
        "down_p": a["L0_ffn_down_proj_w"], "inv_map": a["L0_ffn_inv_map"], "w_fc": a["L1_ffn_w_fc"],
        "w_proj": a["L1_ffn_w_proj"],
    }
    nc = bacc.Bacc("TRN2", target_bir_lowering=False, num_devices=1)
    args = {n: nc.dram_tensor(f"in_{n}", v.shape, mybir.dt.from_np(v.dtype), kind="ExternalInput").ap()
            for n, v in arrays.items()}
    out = nc.dram_tensor("out_x", (B, P, L), F32, kind="ExternalOutput").ap()
    build(nc, out=out, **args)
    r = run(nc, [{f"in_{n}": v for n, v in arrays.items()}], core_ids=[0])
    return r.results[0]["out_x"]
```
